# Optimizing a Trainium2 kernel written in Bass

```python
import numpy as np
import jax
import jax.numpy as jnp

def _softmax(x, axis=-1):
    return jax.nn.softmax(x, axis=axis)

def _gelu(x):
    return jax.nn.gelu(x, approximate=True)

def _silu(x):
    return jax.nn.silu(x)

def _sigmoid(x):
    return jax.nn.sigmoid(x)

def _layernorm(x, axis=-1, eps=1e-05):
    m = jnp.mean(x, axis=axis, keepdims=True)
    v = jnp.var(x, axis=axis, keepdims=True)
    return (x - m) / jnp.sqrt(v + eps)

def _scatter_add(tgt, idx, src, axis=0):
    return tgt.at[idx].add(src)

def _segment_sum(src, seg, n):
    return jax.ops.segment_sum(src, seg, n)
kernel_name = 'mk_sandwich_d1_jaxref_r8_3402b3'

def setup_inputs(seed: int=0):
    np.random.seed(seed)
    _w = jnp.asarray

    def _L0_attn_setup():
        import jax, jax.numpy as jnp
        import numpy as np
        D_MODEL = 128
        HEADDIM = 128
        D_STATE = 64
        NGROUPS = 1
        NHEADS = D_MODEL // HEADDIM

        def segsum(x):
            T = x.shape[-1]
            xe = jnp.broadcast_to(x[..., None], x.shape + (T,))
            mask_lower = jnp.tril(jnp.ones((T, T), dtype=bool), k=-1)
            xe = jnp.where(mask_lower, xe, 0.0)
            x_segsum = jnp.cumsum(xe, axis=-2)
            mask_incl = jnp.tril(jnp.ones((T, T), dtype=bool), k=0)
            return jnp.where(mask_incl, x_segsum, -jnp.inf)

        def ssd_minimal_discrete(X, A, B, C, chunk):
            b, T = (X.shape[0], X.shape[1])
            c = T // chunk
            resh = lambda t: t.reshape(b, c, chunk, *t.shape[2:])
            X, B, C = (resh(X), resh(B), resh(C))
            A = resh(A).transpose(0, 3, 1, 2)
            A_cumsum = jnp.cumsum(A, axis=-1)
            Lmat = jnp.exp(segsum(A))
            Y_diag = jnp.einsum('bclhn,bcshn,bhcls,bcshp->bclhp', C, B, Lmat, X)
            decay_states = jnp.exp(A_cumsum[..., -1:] - A_cumsum)
            states = jnp.einsum('bclhn,bhcl,bclhp->bchpn', B, decay_states, X)
            init = jnp.zeros_like(states[:, :1])
            states = jnp.concatenate([init, states], axis=1)
            A_last = jnp.pad(A_cumsum[..., -1], ((0, 0), (0, 0), (1, 0)))
            decay_chunk = jnp.exp(segsum(A_last))
            new_states = jnp.einsum('bhzc,bchpn->bzhpn', decay_chunk, states)
            states = new_states[:, :-1]
            state_decay_out = jnp.exp(A_cumsum)
            Y_off = jnp.einsum('bclhn,bchpn,bhcl->bclhp', C, states, state_decay_out)
            return (Y_diag + Y_off).reshape(b, T, NHEADS, HEADDIM)

        def ssd_forward(x, W_xproj, dt_bias, A_log, D):
            b, T, _ = x.shape
            dtBC = x @ W_xproj.T
            dt = dtBC[..., :NHEADS]
            Bm = dtBC[..., NHEADS:NHEADS + NGROUPS * D_STATE]
            Cm = dtBC[..., NHEADS + NGROUPS * D_STATE:]
            dt = jax.nn.softplus(dt + dt_bias)
            A = -jnp.exp(A_log)
            Xh = x.reshape(b, T, NHEADS, HEADDIM) * dt[..., None]
            Bh = jnp.broadcast_to(Bm.reshape(b, T, NGROUPS, D_STATE), (b, T, NHEADS, D_STATE))
            Ch = jnp.broadcast_to(Cm.reshape(b, T, NGROUPS, D_STATE), (b, T, NHEADS, D_STATE))
            y = ssd_minimal_discrete(Xh, A * dt, Bh, Ch, T)
            y = y.reshape(b, T, D_MODEL)
            D_full = jnp.repeat(D, HEADDIM)
            return y + x * D_full
        key = jax.random.key(seed)
        k1, k2, k3 = jax.random.split(key, 3)
        x = jax.random.normal(k1, (2, 256, D_MODEL), dtype=jnp.float32)
        W_xproj = jax.random.normal(k2, (NHEADS + 2 * NGROUPS * D_STATE, D_MODEL), dtype=jnp.float32) * (1.0 / np.sqrt(D_MODEL))
        dt_bias = jnp.zeros((NHEADS,), dtype=jnp.float32)
        A_log = jnp.log(jax.random.uniform(k3, (NHEADS,), minval=1.0, maxval=16.0, dtype=jnp.float32))
        D = jnp.ones((NHEADS,), dtype=jnp.float32)
        return {'x': x, 'W_xproj': W_xproj, 'dt_bias': dt_bias, 'A_log': A_log, 'D': D}
    _L0_attn_in = _L0_attn_setup()

    def _L0_ffn_setup():
        import jax, jax.numpy as jnp
        import numpy as np
        DIM = 128
        DEPTH = 2
        HEADS = 8
        DIM_HEAD = 64
        WINDOW = 64
        INNER = HEADS * DIM_HEAD
        HID = int(DIM * 4 * 2 / 3)
        B, N = (2, 1024)
        QK_SCALE = 8.0

        def shift_token(t):
            t1, t2 = jnp.split(t, 2, axis=-1)
            t2 = jnp.pad(t2, ((0, 0), (1, 0), (0, 0)))[:, :-1]
            return jnp.concatenate([t1, t2], axis=-1)

        def l2norm(t):
            return t / jnp.clip(jnp.linalg.norm(t, axis=-1, keepdims=True), 1e-12)

        def rotate_half(x):
            x1, x2 = jnp.split(x, 2, axis=-1)
            return jnp.concatenate([-x2, x1], axis=-1)

        def rotary_xpos(q, k):
            n = q.shape[-2]
            half_idx = jnp.arange(0, DIM_HEAD, 2, dtype=jnp.float32)
            inv_freq = 1.0 / 10000.0 ** (half_idx / DIM_HEAD)
            t = jnp.arange(n, dtype=jnp.float32)
            freqs = t[:, None] * inv_freq[None, :]
            freqs = jnp.concatenate([freqs, freqs], axis=-1)
            base = (half_idx + 0.4 * DIM_HEAD) / (1.4 * DIM_HEAD)
            power = (t - n // 2) / float(WINDOW // 2)
            scale = base[None, :] ** power[:, None]
            scale = jnp.concatenate([scale, scale], axis=-1)
            cos, sin = (jnp.cos(freqs), jnp.sin(freqs))
            q = q * cos * scale + rotate_half(q) * sin * scale
            k = k * cos / scale + rotate_half(k) * sin / scale
            return (q, k)

        def local_attention(q, k, v):
            b, h, n, d = q.shape
            w = n // WINDOW
            bq = q.reshape(b, h, w, WINDOW, d) * QK_SCALE
            bk = k.reshape(b, h, w, WINDOW, d)
            bv = v.reshape(b, h, w, WINDOW, d)

            def look_around(t):
                p = jnp.pad(t, ((0, 0), (0, 0), (1, 0), (0, 0), (0, 0)))
                return jnp.concatenate([p[:, :, :w], p[:, :, 1:]], axis=3)
            bk, bv = (look_around(bk), look_around(bv))
            bt = jnp.arange(n).reshape(w, WINDOW)
            btp = jnp.pad(bt, ((1, 0), (0, 0)), constant_values=-1)
            btk = jnp.concatenate([btp[:w], btp[1:]], axis=1)
            sim = jnp.einsum('bhwid,bhwjd->bhwij', bq, bk)
            i = bt[:, :, None]
            j = btk[:, None, :]
            mask = (i < j) | (i > j + WINDOW) | (j == -1)
            sim = jnp.where(mask, -jnp.finfo(sim.dtype).max, sim)
            attn = jax.nn.softmax(sim, axis=-1)
            out = jnp.einsum('bhwij,bhwjd->bhwid', attn, bv)
            return out.reshape(b, h, n, d)

        def _layer(x, wqkv, qs, ksc, wo, lg, lb, w1, b1, w2, b2):
            b, n, _ = x.shape
            h = shift_token(x)
            qkv = h @ wqkv
            q, k, v = jnp.split(qkv, 3, axis=-1)
            to_heads = lambda t: t.reshape(b, n, HEADS, DIM_HEAD).transpose(0, 2, 1, 3)
            q, k, v = (to_heads(q), to_heads(k), to_heads(v))
            q = l2norm(q) * qs
            k = l2norm(k) * ksc
            q, k = rotary_xpos(q, k)
            o = local_attention(q, k, v)
            o = o.transpose(0, 2, 1, 3).reshape(b, n, INNER)
            x = x + o @ wo
            h = shift_token(x)
            mu = h.mean(-1, keepdims=True)
            var = h.var(-1, keepdims=True)
            h = (h - mu) / jnp.sqrt(var + 1e-05) * lg + lb
            h = h @ w1 + b1
            a, g = jnp.split(h, 2, axis=-1)
            h = a * jax.nn.gelu(g, approximate=False)
            x = x + h @ w2 + b2
            return x
        key = jax.random.key(seed)
        ks = jax.random.split(key, 6)
        return {'x': jax.random.normal(ks[0], (B, N, DIM), jnp.float32), 'wqkv': jax.random.normal(ks[1], (DEPTH, DIM, 3 * INNER), jnp.float32) * 0.02, 'q_scale': jnp.ones((DEPTH, DIM_HEAD), jnp.float32), 'k_scale': jnp.ones((DEPTH, DIM_HEAD), jnp.float32), 'wo': jax.random.normal(ks[2], (DEPTH, INNER, DIM), jnp.float32) * 0.02, 'ln_g': jnp.ones((DEPTH, DIM), jnp.float32), 'ln_b': jnp.zeros((DEPTH, DIM), jnp.float32), 'w1': jax.random.normal(ks[3], (DEPTH, DIM, 2 * HID), jnp.float32) * 0.02, 'b1': jnp.zeros((DEPTH, 2 * HID), jnp.float32), 'w2': jax.random.normal(ks[4], (DEPTH, HID, DIM), jnp.float32) * 0.02, 'b2': jnp.zeros((DEPTH, DIM), jnp.float32)}
    _L0_ffn_in = _L0_ffn_setup()
    _d = {'L0_attn_x': _L0_attn_in['x'], 'L0_attn_W_xproj': _L0_attn_in['W_xproj'], 'L0_attn_dt_bias': _L0_attn_in['dt_bias'], 'L0_attn_A_log': _L0_attn_in['A_log'], 'L0_attn_D': _L0_attn_in['D'], 'L0_ffn_wqkv': _L0_ffn_in['wqkv'], 'L0_ffn_q_scale': _L0_ffn_in['q_scale'], 'L0_ffn_k_scale': _L0_ffn_in['k_scale'], 'L0_ffn_wo': _L0_ffn_in['wo'], 'L0_ffn_ln_g': _L0_ffn_in['ln_g'], 'L0_ffn_ln_b': _L0_ffn_in['ln_b'], 'L0_ffn_w1': _L0_ffn_in['w1'], 'L0_ffn_b1': _L0_ffn_in['b1'], 'L0_ffn_w2': _L0_ffn_in['w2'], 'L0_ffn_b2': _L0_ffn_in['b2']}
    _x0 = _d['L0_attn_x']
    _d['L0_attn_x'] = jax.random.normal(jax.random.fold_in(jax.random.key(seed), 1), (16, 512, 128), dtype=_x0.dtype)
    del _x0
    return _d

def reference(L0_attn_x, L0_attn_W_xproj, L0_attn_dt_bias, L0_attn_A_log, L0_attn_D, L0_ffn_wqkv, L0_ffn_q_scale, L0_ffn_k_scale, L0_ffn_wo, L0_ffn_ln_g, L0_ffn_ln_b, L0_ffn_w1, L0_ffn_b1, L0_ffn_w2, L0_ffn_b2):

    def _L0_attn_ref(x, W_xproj, dt_bias, A_log, D):
        import jax, jax.numpy as jnp
        import numpy as np
        D_MODEL = 128
        HEADDIM = 128
        D_STATE = 64
        NGROUPS = 1
        NHEADS = D_MODEL // HEADDIM

        def segsum(x):
            T = x.shape[-1]
            xe = jnp.broadcast_to(x[..., None], x.shape + (T,))
            mask_lower = jnp.tril(jnp.ones((T, T), dtype=bool), k=-1)
            xe = jnp.where(mask_lower, xe, 0.0)
            x_segsum = jnp.cumsum(xe, axis=-2)
            mask_incl = jnp.tril(jnp.ones((T, T), dtype=bool), k=0)
            return jnp.where(mask_incl, x_segsum, -jnp.inf)

        def ssd_minimal_discrete(X, A, B, C, chunk):
            b, T = (X.shape[0], X.shape[1])
            c = T // chunk
            resh = lambda t: t.reshape(b, c, chunk, *t.shape[2:])
            X, B, C = (resh(X), resh(B), resh(C))
            A = resh(A).transpose(0, 3, 1, 2)
            A_cumsum = jnp.cumsum(A, axis=-1)
            Lmat = jnp.exp(segsum(A))
            Y_diag = jnp.einsum('bclhn,bcshn,bhcls,bcshp->bclhp', C, B, Lmat, X)
            decay_states = jnp.exp(A_cumsum[..., -1:] - A_cumsum)
            states = jnp.einsum('bclhn,bhcl,bclhp->bchpn', B, decay_states, X)
            init = jnp.zeros_like(states[:, :1])
            states = jnp.concatenate([init, states], axis=1)
            A_last = jnp.pad(A_cumsum[..., -1], ((0, 0), (0, 0), (1, 0)))
            decay_chunk = jnp.exp(segsum(A_last))
            new_states = jnp.einsum('bhzc,bchpn->bzhpn', decay_chunk, states)
            states = new_states[:, :-1]
            state_decay_out = jnp.exp(A_cumsum)
            Y_off = jnp.einsum('bclhn,bchpn,bhcl->bclhp', C, states, state_decay_out)
            return (Y_diag + Y_off).reshape(b, T, NHEADS, HEADDIM)

        def ssd_forward(x, W_xproj, dt_bias, A_log, D):
            b, T, _ = x.shape
            dtBC = x @ W_xproj.T
            dt = dtBC[..., :NHEADS]
            Bm = dtBC[..., NHEADS:NHEADS + NGROUPS * D_STATE]
            Cm = dtBC[..., NHEADS + NGROUPS * D_STATE:]
            dt = jax.nn.softplus(dt + dt_bias)
            A = -jnp.exp(A_log)
            Xh = x.reshape(b, T, NHEADS, HEADDIM) * dt[..., None]
            Bh = jnp.broadcast_to(Bm.reshape(b, T, NGROUPS, D_STATE), (b, T, NHEADS, D_STATE))
            Ch = jnp.broadcast_to(Cm.reshape(b, T, NGROUPS, D_STATE), (b, T, NHEADS, D_STATE))
            y = ssd_minimal_discrete(Xh, A * dt, Bh, Ch, T)
            y = y.reshape(b, T, D_MODEL)
            D_full = jnp.repeat(D, HEADDIM)
            return y + x * D_full
        return ssd_forward(x, W_xproj, dt_bias, A_log, D)

    def _L0_ffn_ref(x, wqkv, q_scale, k_scale, wo, ln_g, ln_b, w1, b1, w2, b2):
        import jax, jax.numpy as jnp
        import numpy as np
        DIM = 128
        DEPTH = 2
        HEADS = 8
        DIM_HEAD = 64
        WINDOW = 64
        INNER = HEADS * DIM_HEAD
        HID = int(DIM * 4 * 2 / 3)
        B, N = (2, 1024)
        QK_SCALE = 8.0

        def shift_token(t):
            t1, t2 = jnp.split(t, 2, axis=-1)
            t2 = jnp.pad(t2, ((0, 0), (1, 0), (0, 0)))[:, :-1]
            return jnp.concatenate([t1, t2], axis=-1)

        def l2norm(t):
            return t / jnp.clip(jnp.linalg.norm(t, axis=-1, keepdims=True), 1e-12)

        def rotate_half(x):
            x1, x2 = jnp.split(x, 2, axis=-1)
            return jnp.concatenate([-x2, x1], axis=-1)

        def rotary_xpos(q, k):
            n = q.shape[-2]
            half_idx = jnp.arange(0, DIM_HEAD, 2, dtype=jnp.float32)
            inv_freq = 1.0 / 10000.0 ** (half_idx / DIM_HEAD)
            t = jnp.arange(n, dtype=jnp.float32)
            freqs = t[:, None] * inv_freq[None, :]
            freqs = jnp.concatenate([freqs, freqs], axis=-1)
            base = (half_idx + 0.4 * DIM_HEAD) / (1.4 * DIM_HEAD)
            power = (t - n // 2) / float(WINDOW // 2)
            scale = base[None, :] ** power[:, None]
            scale = jnp.concatenate([scale, scale], axis=-1)
            cos, sin = (jnp.cos(freqs), jnp.sin(freqs))
            q = q * cos * scale + rotate_half(q) * sin * scale
            k = k * cos / scale + rotate_half(k) * sin / scale
            return (q, k)

        def local_attention(q, k, v):
            b, h, n, d = q.shape
            w = n // WINDOW
            bq = q.reshape(b, h, w, WINDOW, d) * QK_SCALE
            bk = k.reshape(b, h, w, WINDOW, d)
            bv = v.reshape(b, h, w, WINDOW, d)

            def look_around(t):
                p = jnp.pad(t, ((0, 0), (0, 0), (1, 0), (0, 0), (0, 0)))
                return jnp.concatenate([p[:, :, :w], p[:, :, 1:]], axis=3)
            bk, bv = (look_around(bk), look_around(bv))
            bt = jnp.arange(n).reshape(w, WINDOW)
            btp = jnp.pad(bt, ((1, 0), (0, 0)), constant_values=-1)
            btk = jnp.concatenate([btp[:w], btp[1:]], axis=1)
            sim = jnp.einsum('bhwid,bhwjd->bhwij', bq, bk)
            i = bt[:, :, None]
            j = btk[:, None, :]
            mask = (i < j) | (i > j + WINDOW) | (j == -1)
            sim = jnp.where(mask, -jnp.finfo(sim.dtype).max, sim)
            attn = jax.nn.softmax(sim, axis=-1)
            out = jnp.einsum('bhwij,bhwjd->bhwid', attn, bv)
            return out.reshape(b, h, n, d)

        def _layer(x, wqkv, qs, ksc, wo, lg, lb, w1, b1, w2, b2):
            b, n, _ = x.shape
            h = shift_token(x)
            qkv = h @ wqkv
            q, k, v = jnp.split(qkv, 3, axis=-1)
            to_heads = lambda t: t.reshape(b, n, HEADS, DIM_HEAD).transpose(0, 2, 1, 3)
            q, k, v = (to_heads(q), to_heads(k), to_heads(v))
            q = l2norm(q) * qs
            k = l2norm(k) * ksc
            q, k = rotary_xpos(q, k)
            o = local_attention(q, k, v)
            o = o.transpose(0, 2, 1, 3).reshape(b, n, INNER)
            x = x + o @ wo
            h = shift_token(x)
            mu = h.mean(-1, keepdims=True)
            var = h.var(-1, keepdims=True)
            h = (h - mu) / jnp.sqrt(var + 1e-05) * lg + lb
            h = h @ w1 + b1
            a, g = jnp.split(h, 2, axis=-1)
            h = a * jax.nn.gelu(g, approximate=False)
            x = x + h @ w2 + b2
            return x
        for l in range(DEPTH):
            x = _layer(x, wqkv[l], q_scale[l], k_scale[l], wo[l], ln_g[l], ln_b[l], w1[l], b1[l], w2[l], b2[l])
        return x
    x = L0_attn_x
    x = x + _layernorm(_L0_attn_ref(_layernorm(x, axis=-1), L0_attn_W_xproj, L0_attn_dt_bias, L0_attn_A_log, L0_attn_D), axis=-1)
    x = x + _layernorm(_L0_ffn_ref(_layernorm(x, axis=-1), L0_ffn_wqkv, L0_ffn_q_scale, L0_ffn_k_scale, L0_ffn_wo, L0_ffn_ln_g, L0_ffn_ln_b, L0_ffn_w1, L0_ffn_b1, L0_ffn_w2, L0_ffn_b2), axis=-1)
    return x

_drawn_inputs = setup_inputs


def setup_inputs(seed=0):
    import zlib

    import numpy as np

    out = dict(_drawn_inputs(seed))
    spreads = {'L0_ffn_q_scale': (1.0, 0.6),
     'L0_ffn_k_scale': (1.0, 0.6),
     'L0_ffn_ln_g': (1.0, 0.6),
     'L0_ffn_ln_b': (0.0, 0.8),
     'L0_ffn_b1': (0.0, 0.8),
     'L0_ffn_b2': (0.0, 0.8)}
    factors = {'L0_ffn_wqkv': 4.305, 'L0_ffn_wo': 4.297, 'L0_ffn_w1': 7.129, 'L0_ffn_w2': 7.014}
    for name, (base, spread) in spreads.items():
        noise = np.random.default_rng([zlib.crc32(name.encode()), seed]).standard_normal(out[name].shape)
        drawn = base * np.exp(spread * noise) if base else spread * noise
        out[name] = jnp.asarray(drawn.astype(out[name].dtype))
    for name, factor in factors.items():
        out[name] = (out[name] * factor).astype(out[name].dtype)
    return out
```

```python
from contextlib import ExitStack

import numpy as np
import concourse.bass as bass
from concourse import mybir

F32 = mybir.dt.float32
I32 = mybir.dt.int32
BF16 = mybir.dt.bfloat16
ALU = mybir.AluOpType
ACT = mybir.ActivationFunctionType
AX = mybir.AxisListType

P = 128
D = 128
STATE = 64
HEADS, DH, WIN = 8, 64, 64
INNER = HEADS * DH
QK_SCALE = 8.0
NEG = -1.0e30
LN_EPS = 1e-5
CHUNKS = 3
STRIDE = 64
CHAIN = 1024


def shape_constants(tokens):
    k = np.arange(P)
    ident = (k[:, None] == k[None, :]).astype(np.float32)
    upto = (k[:, None] <= k[None, :]).astype(np.float32)
    later = (k[:, None] > k[None, :]).astype(np.float32)
    causal = np.where(k[:, None] <= k[None, :], 0.0, NEG).astype(np.float32)
    i = (k % WIN)[:, None]
    j = np.arange(WIN)[None, :]
    own = np.where(j <= i, 0.0, NEG)
    prev = np.where(j >= i, 0.0, NEG)
    even = k[:, None] < WIN
    rest = np.concatenate([np.where(even, own, prev), np.where(even, prev, own)], axis=1).astype(np.float32)
    first = rest.copy()
    first[:WIN, WIN:] = NEG
    half = np.arange(0, DH, 2, dtype=np.float32)
    inv_freq = (1.0 / np.float32(10000.0) ** (half / np.float32(DH))).astype(np.float32)
    t = np.arange(tokens, dtype=np.float32)
    freqs = (t[:, None] * inv_freq[None, :]).astype(np.float32)
    base = ((half + np.float32(0.4 * DH)) / np.float32(1.4 * DH)).astype(np.float32)
    power = ((t - tokens // 2) / np.float32(WIN // 2)).astype(np.float32)
    scale = (base[None, :] ** power[:, None]).astype(np.float32)
    cos, sin = np.cos(freqs), np.sin(freqs)
    cosines = np.stack([np.tile(cos * scale, 2), np.tile(cos / scale, 2)], axis=1)
    sines = np.stack([np.concatenate([-sin * scale, sin * scale], 1), np.concatenate([-sin / scale, sin / scale], 1)],
                     axis=1)

    def rows(a):
        return a.reshape(tokens // P, P, 2 * DH).transpose(1, 0, 2).reshape(P, -1)

    return np.ascontiguousarray(
        np.concatenate([ident, upto, later, causal, first, rest, rows(cosines), rows(sines)], axis=1).astype(np.float32))


def attention_steps(z, layer):
    units = [(m, g) for m in range(4) for g in range(2)]
    slots = []
    for k in range(len(units) + 2):
        now, late, last = [], [], []
        if k < len(units):
            for name in ("scores", "smax", "exp"):
                now.append((name, z, layer, units[k]))
        if 0 < k <= len(units):
            m, g = units[k - 1]
            now += [(name, z, layer, (m, g)) for name in ("turn_p", "p_evac")]
            late += [(name, z, layer, (m, g)) for name in ("pv", "o_norm")]
            if g == 1:
                last += [(name, z, layer, (m, g)) for name in ("turn_o", "o_evac")]
        if k > 1 and units[k - 2][1] == 1:
            m, g = units[k - 2]
            now += [(name, z, layer, (m, g)) for name in ("wo", "wo_add")]
        slots += now + late + last
    return slots


def ln_steps(z, layer, kind):
    return [(n, z, layer, kind) for n in ("ln_stats", "ln_rstd", "ln_apply")]


def mlp_steps(z, layer):
    s = [(n, z, layer, "mlp") for n in ("turn_x", "shift_lo", "shift_hi", "resid_bias", "turn_h")]
    s += ln_steps(z, layer, "h")
    s += [(n, z, layer, 0) for n in ("turn_hn", "ln_affine")]
    s += [("up", z, layer, 0), ("up", z, layer, 1), ("gelu", z, layer, 0), ("gate", z, layer, 0), ("up", z, layer, 2)]
    s += [(n, z, layer, j) for j in (1, 2) for n in ("gelu", "gate")]
    s += [("down", z, layer, 0), ("resid", z, layer, 0)]
    return s


def qkv_steps(z, layer):
    s = [(n, z, layer, "qkv") for n in ("turn_x", "shift_lo", "shift_hi")]
    for m in range(5):
        if m < 4:
            s += [(n, z, layer, m) for n in ("qkv", "qk_copy", "v_evac", "rope_c", "qk_square", "v_shift", "rope_s", "qk_sum",
                                             "rinv", "rope_add", "k_scale")]
            s += [("v_next", z, layer, m)] if m < 3 else []
        if m > 0:
            s += [(n, z, layer, m - 1) for n in ("turn_q", "q_evac", "turn_k", "k_evac")]
    return s


def output_steps(z):
    return ln_steps(z, 1, "o") + [("store", z, 1, 0)]


def ssd_steps(z):
    s = ln_steps(z, 0, "x")
    s += [(n, z, 0, 0) for n in (
        "turn_xn", "xn_evac", "ssd_proj", "bt_evac", "ct_evac", "tok_evac", "dt_abs", "dt_log", "decay", "ssd_g",
        "ssd_seg", "seg_exp", "mt", "ssd_y", "y_skip", "ssd_off", "y_off")]
    return s + ln_steps(z, 0, "y") + ln_steps(z, 0, "1")


PHASE = {(0, 0): 0, (1, 0): 1, (0, 1): 2, (1, 1): 3}
REST_PHASE = {(1, 1): 0, (0, 0): 1, (1, 0): 2, (0, 1): 3}

FIRST = ssd_steps(0) + qkv_steps(0, 0)
ATTENTION = [attention_steps(0, 0), attention_steps(1, 0), attention_steps(0, 1), attention_steps(1, 1)]
REST = [mlp_steps(1, 1) + output_steps(1) + ssd_steps(1) + qkv_steps(1, 0),
        mlp_steps(0, 0) + qkv_steps(0, 1),
        mlp_steps(1, 0) + qkv_steps(1, 1),
        mlp_steps(0, 1) + output_steps(0) + ssd_steps(0) + qkv_steps(0, 0)]
PASS = sum(ATTENTION, []) + sum(REST, [])
ORDER = [
    288, 290, 289, 292, 293, 0, 1, 2, 3, 294, 295, 296, 297, 6, 4, 7, 298, 300, 299, 5, 301, 303, 302, 8, 13,
    304, 305, 306, 307, 291, 10, 14, 9, 308, 309, 15, 19, 16, 11, 12, 17, 18, 22, 24, 310, 311, 313, 314, 28,
    20, 315, 25, 23, 21, 31, 29, 316, 317, 30, 26, 27, 318, 37, 32, 321, 322, 319, 323, 33, 320, 324, 325, 326,
    34, 38, 46, 327, 35, 36, 328, 329, 42, 40, 330, 43, 331, 332, 333, 47, 39, 41, 49, 334, 50, 55, 44, 45, 335,
    336, 51, 52, 48, 53, 54, 56, 337, 60, 338, 339, 58, 57, 340, 61, 341, 342, 59, 343, 62, 64, 346, 345, 344,
    63, 65, 353, 354, 66, 348, 349, 351, 355, 357, 356, 350, 366, 360, 370, 358, 361, 363, 367, 352, 368, 371,
    372, 369, 386, 362, 373, 382, 347, 376, 374, 383, 364, 387, 72, 67, 384, 377, 379, 73, 392, 390, 359, 68,
    69, 75, 70, 385, 388, 378, 76, 74, 78, 397, 79, 375, 71, 389, 82, 393, 398, 395, 380, 399, 394, 77, 396, 80,
    85, 81, 400, 86, 91, 401, 87, 402, 403, 404, 365, 83, 88, 89, 90, 92, 405, 407, 406, 409, 96, 84, 93, 410,
    411, 100, 94, 109, 95, 97, 412, 413, 101, 98, 414, 103, 415, 102, 99, 110, 381, 417, 418, 416, 104, 111,
    105, 420, 419, 421, 422, 106, 107, 118, 408, 423, 108, 424, 112, 425, 426, 114, 428, 427, 119, 113, 429,
    430, 115, 116, 121, 433, 127, 432, 431, 117, 122, 441, 442, 443, 435, 436, 128, 438, 123, 453, 445, 437,
    457, 120, 447, 454, 458, 459, 439, 448, 461, 455, 124, 125, 126, 473, 444, 456, 129, 449, 130, 132, 131,
    450, 464, 475, 463, 136, 440, 391, 460, 469, 451, 470, 133, 465, 144, 434, 471, 472, 474, 137, 145, 134,
    135, 466, 477, 147, 146, 138, 148, 139, 484, 140, 141, 154, 150, 149, 142, 467, 479, 476, 480, 446, 485,
    486, 487, 482, 481, 483, 488, 151, 143, 157, 155, 152, 158, 153, 462, 489, 490, 159, 491, 492, 160, 494,
    493, 156, 161, 496, 163, 162, 478, 497, 168, 166, 164, 172, 498, 169, 499, 495, 452, 500, 173, 167, 165,
    501, 170, 171, 502, 503, 504, 507, 505, 506, 508, 509, 174, 181, 510, 511, 175, 182, 512, 513, 515, 176,
    177, 178, 514, 516, 517, 179, 518, 522, 190, 520, 191, 180, 519, 183, 523, 528, 530, 529, 184, 186, 525,
    532, 540, 521, 185, 524, 199, 193, 194, 187, 188, 535, 526, 531, 534, 189, 544, 541, 542, 195, 536, 537,
    546, 196, 545, 550, 547, 548, 538, 560, 551, 197, 192, 543, 553, 198, 552, 556, 561, 557, 468, 564, 204,
    216, 200, 202, 203, 201, 205, 558, 559, 206, 533, 567, 554, 527, 208, 209, 566, 562, 571, 572, 207, 210,
    563, 219, 569, 573, 574, 211, 212, 213, 568, 570, 575, 214, 215, 576, 577, 578, 579, 217, 580, 581, 218,
    583, 584, 585, 220, 586, 312, 222, 223, 226, 221, 227, 224, 229, 225, 587, 588, 589, 590, 582, 230, 591,
    594, 592, 593, 595, 596, 597, 231, 232, 598, 599, 600, 601, 228, 233, 235, 234, 240, 539, 236, 244, 241,
    238, 237, 239, 253, 602, 604, 605, 245, 242, 243, 247, 248, 249, 246, 606, 607, 250, 549, 608, 251, 609,
    252, 256, 612, 613, 611, 610, 258, 616, 614, 565, 254, 615, 617, 618, 619, 257, 259, 262, 263, 255, 620,
    264, 621, 265, 260, 622, 266, 271, 261, 555, 267, 623, 624, 625, 272, 268, 269, 270, 274, 626, 627, 628,
    275, 273, 276, 277, 278, 280, 281, 629, 630, 631, 632, 279, 633, 634, 636, 282, 637, 635, 645, 283, 639,
    646, 647, 640, 649, 642, 648, 641, 661, 643, 651, 652, 657, 284, 654, 662, 658, 644, 664, 659, 663, 638,
    653, 665, 650, 677, 285, 286, 660, 678, 667, 668, 670, 679, 669, 655, 656, 673, 603, 680, 666, 671, 674,
    675, 681, 672, 676, 683, 684, 686, 688, 689, 685, 687, 690, 691, 692, 682, 693, 694, 287, 695,
]
LAST = mlp_steps(1, 1) + output_steps(1)


def build(nc, x, w_xproj, dt_bias, a_log, d_skip, wqkv, q_scale, k_scale, wo, ln_g, ln_b, w1, b1, w2, b2, const, out):
    SEQS, T, _ = x.shape
    BLK = T // P
    DEPTH = wqkv.shape[0]
    HID = w2.shape[1]
    SIZES = [min(P, HID - P * j) for j in range(CHUNKS)]
    PASSES = SEQS // 2
    assert T == 512 and D == P and SEQS % 2 == 0

    ctx = ExitStack()
    with ctx:
        def sb(name, shape, dt=F32):
            return ctx.enter_context(nc.sbuf_tensor(name, shape, dt))

        def ps(name, shape):
            return ctx.enter_context(nc.psum_tensor(name, shape, F32))

        cst = sb("cst", [P, const.shape[1]])
        ident, upto, later = cst[:, 0:P], cst[:, P:2 * P], cst[:, 2 * P:3 * P]
        rope_cos = cst[:, 6 * P:6 * P + BLK * P].rearrange("p (m a f) -> p m a f", m=BLK, a=2)
        rope_sin = cst[:, 6 * P + BLK * P:6 * P + 2 * BLK * P].rearrange("p (m a f) -> p m a f", m=BLK, a=2)
        ident_h = sb("ident_h", [P, P], BF16)
        masks_h = sb("masks_h", [P, 3, P], BF16)
        wx_rows = sb("wx_rows", [P, D])
        wx_bc = sb("wx_bc", [D, P])
        wx_tok = sb("wx_tok", [D, 1 + STATE])
        wqkv_s = sb("wqkv_s", [D, DEPTH, 3 * INNER])
        wo_s = sb("wo_s", [P, DEPTH, INNER // P, D])
        w1_s = sb("w1_s", [D, DEPTH, 2 * HID])
        w2_s = sb("w2_s", [P, DEPTH, CHUNKS, D])
        b1_s = sb("b1_s", [P, DEPTH, 2, CHUNKS])
        b2_s = sb("b2_s", [P, DEPTH, D])
        lng_s = sb("lng_s", [P, DEPTH])
        lnb_s = sb("lnb_s", [P, DEPTH])
        scales = sb("scales", [P, DEPTH, 2, DH])
        ssd_par = sb("ssd_par", [P, 4])
        tab_c = sb("tab_c", [P, DEPTH, BLK, 2, DH])
        tab_s = sb("tab_s", [P, DEPTH, BLK, 2, DH])
        ones = sb("ones", [P, P])
        minus_half = sb("minus_half", [P, BLK])

        xin = [sb(f"xin{z}", [P, BLK, D]) for z in range(2)]
        x1 = [sb(f"x1{z}", [P, BLK, D]) for z in range(2)]
        xres = [sb(f"xres{z}", [P, BLK, D]) for z in range(2)]
        outb = [sb(f"outb{z}", [P, BLK, D]) for z in range(2)]
        qT = [sb(f"qT{z}", [P, HEADS // 2, T]) for z in range(2)]
        kT = [sb(f"kT{z}", [P, HEADS // 2, WIN + T]) for z in range(2)]
        v_odd = [sb(f"v_odd{z}", [P, BLK, HEADS, DH + 1]) for z in range(2)]
        v_even = [sb(f"v_even{z}", [P, BLK, HEADS, DH + 1]) for z in range(2)]
        rnorm = [sb(f"rnorm{z}", [P, BLK, 2 * HEADS]) for z in range(2)]

        hT = sb("hT", [P, T])
        hn = sb("hn", [P, BLK, D])
        hnT = sb("hnT", [P, T])
        xb = sb("xb", [P, BLK, D])
        gates = sb("gates", [P, 2, T])
        uT = sb("uT", [P, CHUNKS, T])
        stats = sb("stats", [P, BLK, 6])
        mv = sb("mv", [P, BLK, 2])
        veps = sb("veps", [P, BLK])
        rstd = sb("rstd", [P, BLK])
        qk = sb("qk", [P, 2, 2 * INNER])
        sq = sb("sq", [P, 2 * INNER])
        ss = sb("ss", [P, 2 * HEADS])
        ssc = sb("ssc", [P, 2 * HEADS])
        guess = sb("guess", [P, 2 * HEADS])
        square = sb("square", [P, 2 * HEADS])
        rc = sb("rc", [P, 2 * INNER])
        rs = sb("rs", [P, 2 * INNER])
        rot = sb("rot", [P, 2, 2 * INNER])

        xn = sb("xn", [P, BLK, D])
        xnT = sb("xnT", [P, T])
        BT = sb("BT", [STATE, T])
        CT = sb("CT", [STATE, T])
        tok = sb("tok", [P, BLK, 1 + STATE])
        zb = sb("zb", [P, BLK])
        nz = sb("nz", [P, BLK])
        ez = sb("ez", [P, BLK])
        lz = sb("lz", [P, BLK])
        dts = sb("dts", [P, BLK])
        adt = sb("adt", [P, BLK])
        wdt = sb("wdt", [P, BLK])
        R = rc[:, 0:T].rearrange("p (m l) -> p m l", m=BLK)
        MT = rc[:, T:2 * T].rearrange("p (m l) -> p m l", m=BLK)
        E = rs[:, 0:T].rearrange("p (m l) -> p m l", m=BLK)
        et = sb("et", [P, 2 * BLK])
        Bd = sb("Bd", [P, BLK, STATE])
        St = sb("St", [STATE, BLK - 1, D])
        y = sb("y", [P, BLK, D])
        yn = hn

        nmx = sb("nmx", [P, 2, 4])
        nb = sb("nb", [P, 2, 4])
        probs = sb("probs", [P, 2, 4, P])
        probsT = sb("probsT", [P, 2, 4, P])
        rl = sb("rl", [P, 4])
        otok = sb("otok", [P, 2, INNER])
        oT = sb("oT", [P, INNER // P, P])

        pS = [ps(f"pS{i}", [P, 4, P]) for i in range(2)]
        pT = ps("pT", [P, 4, P])
        pO = ps("pO", [P, 512])
        pQK = ps("pQK", [P, 2, 512])
        pV = ps("pV", [P, 512])
        pM = ps("pM", [P, 512])

        def semaphore(name):
            return ctx.enter_context(nc.semaphore(name))

        s_bt_evac = semaphore("s_bt_evac")
        s_ct_evac = semaphore("s_ct_evac")
        s_decay = semaphore("s_decay")
        s_down = semaphore("s_down")
        s_dt_abs = semaphore("s_dt_abs")
        s_dt_log = semaphore("s_dt_log")
        s_exp = semaphore("s_exp")
        s_gate = semaphore("s_gate")
        s_gelu = semaphore("s_gelu")
        s_k_evac = semaphore("s_k_evac")
        s_k_scale = semaphore("s_k_scale")
        s_ln_affine = semaphore("s_ln_affine")
        s_ln_apply = semaphore("s_ln_apply")
        s_ln_rstd = semaphore("s_ln_rstd")
        s_ln_stats = semaphore("s_ln_stats")
        s_mt = semaphore("s_mt")
        s_o_evac = semaphore("s_o_evac")
        s_o_norm = semaphore("s_o_norm")
        s_p_evac = semaphore("s_p_evac")
        s_pv = semaphore("s_pv")
        s_q_evac = semaphore("s_q_evac")
        s_qk_copy = semaphore("s_qk_copy")
        s_qk_square = semaphore("s_qk_square")
        s_qk_sum = semaphore("s_qk_sum")
        s_qkv = semaphore("s_qkv")
        s_resid = semaphore("s_resid")
        s_resid_bias = semaphore("s_resid_bias")
        s_rinv = semaphore("s_rinv")
        s_rope_add = semaphore("s_rope_add")
        s_rope_c = semaphore("s_rope_c")
        s_rope_s = semaphore("s_rope_s")
        s_scores = semaphore("s_scores")
        s_seg_exp = semaphore("s_seg_exp")
        s_shift_hi = semaphore("s_shift_hi")
        s_shift_lo = semaphore("s_shift_lo")
        s_smax = semaphore("s_smax")
        s_ssd_g = semaphore("s_ssd_g")
        s_ssd_off = semaphore("s_ssd_off")
        s_ssd_proj = semaphore("s_ssd_proj")
        s_ssd_seg = semaphore("s_ssd_seg")
        s_ssd_y = semaphore("s_ssd_y")
        s_tok_evac = semaphore("s_tok_evac")
        s_turn_h = semaphore("s_turn_h")
        s_turn_hn = semaphore("s_turn_hn")
        s_turn_k = semaphore("s_turn_k")
        s_turn_o = semaphore("s_turn_o")
        s_turn_p = semaphore("s_turn_p")
        s_turn_q = semaphore("s_turn_q")
        s_turn_x = semaphore("s_turn_x")
        s_turn_xn = semaphore("s_turn_xn")
        s_up = semaphore("s_up")
        s_v_evac = semaphore("s_v_evac")
        s_v_next = semaphore("s_v_next")
        s_v_shift = semaphore("s_v_shift")
        s_wo = semaphore("s_wo")
        s_wo_add = semaphore("s_wo_add")
        s_xn_evac = semaphore("s_xn_evac")
        s_y_off = semaphore("s_y_off")
        s_y_skip = semaphore("s_y_skip")
        s_section = semaphore("s_section")
        s_hold = semaphore("s_hold")
        s_weights = semaphore("s_weights")
        s_rows = semaphore("s_rows")
        s_setup = semaphore("s_setup")
        s_wx = semaphore("s_wx")
        s_scaled = semaphore("s_scaled")
        s_loaded = [semaphore(f"s_loaded{z}") for z in range(2)]
        s_stored = [semaphore(f"s_stored{z}") for z in range(2)]
        s_act_chain = semaphore("s_act_chain")
        s_dve_chain = semaphore("s_dve_chain")
        s_pool_chain = semaphore("s_pool_chain")

        class Count:

            def __init__(self, section, listed, order=None):
                self.section, self.listed, self.links = section, listed, 0
                self.order = range(len(listed)) if order is None else order

            def steps(self):
                for self.at in self.order:
                    name, z, layer, arg = self.listed[self.at]
                    yield name, z, layer, arg, sum(s[0] == name for s in self.listed[:self.at + 1])
                self.at = len(self.listed)

            def nth(self, name, k):
                return self.section * STRIDE + max(k, 0)

            def so_far(self, name):
                return self.nth(name, sum(s[0] == name for s in self.listed[:self.at]))

            def rest(self, name):
                return STRIDE - sum(s[0] == name for s in self.listed)

            def next_link(self):
                self.links += 1
                return self.section * CHAIN + self.links

        block = ctx.enter_context(nc.Block())

        @block.sync
        def _(sp):
            def load(z, seq):
                sp.dma_start(xin[z][:, :, :], x[seq].rearrange("(m p) d -> p m d", p=P)).then_inc(s_loaded[z], 16)

            load(0, 0)
            for z in range(2):
                sp.sem_inc(s_stored[z], 16)
            sp.dma_start(cst[:, :], const[:, :]).then_inc(s_weights, 16)
            sp.dma_start(wx_rows[:, :], w_xproj[1:1 + P, :]).then_inc(s_weights, 16)
            sp.dma_start(wx_tok[:, 0:1], w_xproj[0:1, :].rearrange("a d -> d a")).then_inc(s_weights, 16)
            for n, src in enumerate((dt_bias, a_log, d_skip)):
                sp.dma_start(ssd_par[:, n:n + 1], src.partition_broadcast(P)).then_inc(s_weights, 16)
            for l in range(DEPTH):
                sp.dma_start(wqkv_s[:, l, :], wqkv[l]).then_inc(s_weights, 16)
                sp.dma_start(scales[:, l, 0, :], q_scale[l].partition_broadcast(P)).then_inc(s_weights, 16)
                sp.dma_start(scales[:, l, 1, :], k_scale[l].partition_broadcast(P)).then_inc(s_weights, 16)
                sp.dma_start(wo_s[:, l, :, :], wo[l].rearrange("(c p) n -> p c n", p=P)).then_inc(s_weights, 16)
                sp.dma_start(w1_s[:, l, :], w1[l]).then_inc(s_weights, 16)
                sp.dma_start(b2_s[:, l, :], b2[l].partition_broadcast(P)).then_inc(s_weights, 16)
                sp.dma_start(lng_s[:, l:l + 1], ln_g[l:l + 1, :].rearrange("a d -> d a")).then_inc(s_weights, 16)
                sp.dma_start(lnb_s[:, l:l + 1], ln_b[l:l + 1, :].rearrange("a d -> d a")).then_inc(s_weights, 16)
                for j, n in enumerate(SIZES):
                    sp.dma_start(w2_s[0:n, l, j, :], w2[l, P * j:P * j + n, :]).then_inc(s_weights, 16)
                    for half in range(2):
                        lo = half * HID + P * j
                        sp.dma_start(b1_s[0:n, l, half, j:j + 1],
                                     b1[l:l + 1, lo:lo + n].rearrange("a d -> d a")).then_inc(s_weights, 16)

            def section(count):
                for name, z, layer, arg, n in count.steps():
                    if name == "v_shift":
                        m = arg
                        sp.wait_ge(s_v_shift, 16 * count.nth("v_shift", n - 1))
                        sp.sem_inc(s_hold, 1)
                        sp.wait_ge(s_v_evac, count.nth("v_evac", n))
                        sp.dma_start(v_even[z][0:WIN, m, :, :], v_odd[z][0:WIN, m, :, :]).then_inc(s_v_shift, 16)
                    elif name == "v_next":
                        m = arg
                        sp.wait_ge(s_v_next, 16 * count.nth("v_next", n - 1))
                        sp.sem_inc(s_hold, 1)
                        sp.wait_ge(s_v_evac, count.so_far("v_evac"))
                        sp.dma_start(v_even[z][WIN:P, m + 1, :, :], v_odd[z][WIN:P, m, :, :]).then_inc(s_v_next, 16)
                    elif name == "store":
                        sp.wait_ge(s_ln_apply, count.so_far("ln_apply"))
                        sp.sem_inc(s_hold, 1)
                        if isinstance(count.section, int):
                            seq = SEQS - 1
                        elif z == 0:
                            seq = 2 * (count.section - 1)
                        else:
                            seq = (2 * (count.section - 1) + (SEQS - 1)) % SEQS
                        sp.dma_start(out[seq].rearrange("(m p) d -> p m d", p=P),
                                            outb[z][:, :, :]).then_inc(s_stored[z], 16)
                sp.wait_ge(s_v_shift, 16 * count.so_far("v_shift"))
                sp.sem_inc(s_hold, 1)
                sp.wait_ge(s_v_next, 16 * count.so_far("v_next"))
                sp.sem_inc(s_hold, 1)
                sp.sem_inc(s_v_shift, 16 * count.rest("v_shift"))
                sp.sem_inc(s_v_next, 16 * count.rest("v_next"))
                sp.drain()
                sp.drain().then_inc(s_section, 1)
                sp.wait_ge(s_section, (count.section + 1) * 5)
                sp.sem_inc(s_hold, 1)

            section(Count(0, FIRST))
            with sp.Fori(0, PASSES) as i:
                load(1, 2 * i + 1)
                load(0, (2 * i + 2) % SEQS)
                section(Count(i + 1, PASS, ORDER))
            section(Count(PASSES + 1, LAST))
            sp.wait_ge(s_stored[0], 16 * (PASSES + 1))
            sp.wait_ge(s_stored[1], 16 * (PASSES + 2))
            sp.wait_ge(s_loaded[0], 16 * (PASSES + 1))

        N_WEIGHTS = 16 * (6 + DEPTH * (8 + 3 * CHUNKS))

        @block.tensor
        def _(pe):
            mm, turn = nc.tensor.matmul, nc.tensor.transpose

            def section(count):
                for name, z, layer, arg, n in count.steps():
                    if name == "turn_x":
                        pe.wait_ge(s_shift_lo, count.so_far("shift_lo"))
                        pe.wait_ge(s_shift_hi, count.so_far("shift_hi"))
                        pe.wait_ge(s_k_evac, count.so_far("k_evac"))
                        pe.wait_ge(s_gelu, count.so_far("gelu"))
                        pe.wait_ge(s_y_off, count.so_far("y_off"))
                        pe.wait_ge(s_wo_add, count.nth("wo_add", 4 * REST_PHASE[z, layer]) if arg == "mlp" else count.nth("wo_add", 0))
                        pe.wait_ge(s_resid, count.so_far("resid"))
                        pe.wait_ge(s_ln_apply, count.so_far("ln_apply"))
                        for m in range(BLK):
                            last = turn(pM[:, m * P:(m + 1) * P], xres[z][:, m, :], ident)
                        last.then_inc(s_turn_x, 1)
                    elif name == "turn_h":
                        pe.wait_ge(s_shift_lo, count.so_far("shift_lo"))
                        pe.wait_ge(s_shift_hi, count.so_far("shift_hi"))
                        pe.wait_ge(s_v_evac, count.so_far("v_evac"))
                        pe.wait_ge(s_resid, count.so_far("resid"))
                        for m in range(BLK):
                            last = turn(pV[:, m * P:(m + 1) * P], hT[:, m * P:(m + 1) * P], ident)
                        last.then_inc(s_turn_h, 1)
                    elif name == "turn_hn":
                        pe.wait_ge(s_ln_apply, count.so_far("ln_apply"))
                        pe.wait_ge(s_shift_lo, count.so_far("shift_lo"))
                        pe.wait_ge(s_shift_hi, count.so_far("shift_hi"))
                        for m in range(BLK):
                            last = turn(pM[:, m * P:(m + 1) * P], hn[:, m, :], ident)
                        last.then_inc(s_turn_hn, 1)
                    elif name == "up":
                        j = arg
                        if j == 0:
                            pe.wait_ge(s_ln_affine, count.so_far("ln_affine"))
                            pe.wait_ge(s_qk_copy, count.so_far("qk_copy"))
                        if j == 1:
                            pe.wait_ge(s_ln_apply, count.so_far("ln_apply"))
                            pe.wait_ge(s_ln_affine, count.so_far("ln_affine"))
                        if j == 2:
                            pe.wait_ge(s_gelu, count.nth("gelu", n - 2))
                            pe.wait_ge(s_gate, count.nth("gate", n - 2))
                        a, g = (pV[:, :], pM[:, :]) if j == 1 else (pQK[:, 0, :], pQK[:, 1, :])
                        lo, size = P * j, SIZES[j]
                        mm(a[0:size], w1_s[:, layer, lo:lo + size], hnT[:, :], start=True, stop=True)
                        mm(g[0:size], w1_s[:, layer, HID + lo:HID + lo + size], hnT[:, :], start=True, stop=True).then_inc(s_up, 1)
                    elif name == "down":
                        pe.wait_ge(s_gate, count.so_far("gate"))
                        for m in range(BLK):
                            for j, size in enumerate(SIZES):
                                last = mm(pV[:, m * P:(m + 1) * P], uT[0:size, j, m * P:(m + 1) * P],
                                          w2_s[0:size, layer, j, :], start=j == 0, stop=j == CHUNKS - 1)
                        last.then_inc(s_down, 1)
                    elif name == "qkv":
                        m = arg
                        pe.wait_ge(s_shift_lo, count.so_far("shift_lo"))
                        pe.wait_ge(s_shift_hi, count.so_far("shift_hi"))
                        pe.wait_ge(s_qk_copy, count.so_far("qk_copy"))
                        pe.wait_ge(s_v_evac, count.so_far("v_evac"))
                        if m == 0:
                            pe.wait_ge(s_gate, count.so_far("gate"))
                            pe.wait_ge(s_gelu, count.so_far("gelu"))
                            pe.wait_ge(s_resid, count.so_far("resid"))
                            pe.wait_ge(s_mt, count.so_far("mt"))
                            pe.wait_ge(s_y_skip, count.so_far("y_skip"))
                            pe.wait_ge(s_y_off, count.so_far("y_off"))
                        for c in range(3):
                            last = mm(pV[:, :] if c == 2 else pQK[:, c, :], hT[:, m * P:(m + 1) * P],
                                      wqkv_s[:, layer, c * INNER:(c + 1) * INNER], start=True, stop=True)
                        last.then_inc(s_qkv, 1)
                    elif name == "turn_q":
                        m = arg
                        pe.wait_ge(s_shift_lo, count.so_far("shift_lo"))
                        pe.wait_ge(s_shift_hi, count.so_far("shift_hi"))
                        pe.wait_ge(s_k_evac, count.so_far("k_evac"))
                        pe.wait_ge(s_rope_add, count.nth("rope_add", n))
                        for c in range(4):
                            last = turn(pM[:, c * P:(c + 1) * P], rot[:, n % 2, c * P:(c + 1) * P], ident)
                        last.then_inc(s_turn_q, 1)
                    elif name == "turn_k":
                        m = arg
                        pe.wait_ge(s_q_evac, count.nth("q_evac", n))
                        pe.wait_ge(s_k_scale, count.nth("k_scale", n))
                        for c in range(4):
                            last = turn(pM[:, c * P:(c + 1) * P], rot[:, n % 2, INNER + c * P:INNER + (c + 1) * P], ident)
                        last.then_inc(s_turn_k, 1)
                    elif name == "turn_xn":
                        pe.wait_ge(s_ln_apply, count.so_far("ln_apply"))
                        pe.wait_ge(s_gelu, count.so_far("gelu"))
                        pe.wait_ge(s_k_evac, count.so_far("k_evac"))
                        for m in range(BLK):
                            last = turn(pM[:, m * P:(m + 1) * P], xn[:, m, :], ident)
                        last.then_inc(s_turn_xn, 1)
                    elif name == "ssd_proj":
                        pe.wait_ge(s_xn_evac, count.so_far("xn_evac"))
                        pe.wait_ge(s_gate, count.so_far("gate"))
                        pe.wait_ge(s_gelu, count.so_far("gelu"))
                        pe.wait_ge(s_qk_copy, count.so_far("qk_copy"))
                        mm(pQK[:, 0, :], wx_bc[:, :], xnT[:, :], start=True, stop=True)
                        for m in range(BLK):
                            last = mm(pQK[:, 1, m * (1 + STATE):(m + 1) * (1 + STATE)], xnT[:, m * P:(m + 1) * P],
                                      wx_tok[:, :], start=True, stop=True)
                        last.then_inc(s_ssd_proj, 1)
                    elif name == "ssd_g":
                        pe.wait_ge(s_bt_evac, count.so_far("bt_evac"))
                        pe.wait_ge(s_ct_evac, count.so_far("ct_evac"))
                        for m in range(BLK):
                            last = mm(pQK[:, 0, m * P:(m + 1) * P], BT[:, m * P:(m + 1) * P], CT[:, m * P:(m + 1) * P],
                                      start=True, stop=True)
                        last.then_inc(s_ssd_g, 1)
                    elif name == "ssd_seg":
                        pe.wait_ge(s_decay, count.so_far("decay"))
                        pe.wait_ge(s_resid, count.so_far("resid"))
                        pe.wait_ge(s_v_evac, count.so_far("v_evac"))
                        pe.wait_ge(s_xn_evac, count.so_far("xn_evac"))
                        mm(pV[:, :], ident_h[:, :], masks_h[:, 0:1, :].to_broadcast([P, BLK, P]), start=True, stop=False)
                        mm(pV[:, :], later, R[:, :, :], start=False, stop=True)
                        mm(pM[:, 0:BLK], upto, adt[:, :], start=True, stop=True)
                        mm(pM[:, BLK:2 * BLK], ones[:, :], adt[:, :], start=True, stop=True).then_inc(s_ssd_seg, 1)
                    elif name == "ssd_y":
                        pe.wait_ge(s_mt, count.so_far("mt"))
                        pe.wait_ge(s_seg_exp, count.so_far("seg_exp"))
                        pe.wait_ge(s_tok_evac, count.so_far("tok_evac"))
                        for m in range(BLK):
                            mm(pM[:, m * P:(m + 1) * P], MT[:, m, :], xn[:, m, :], start=True, stop=True)
                        for m in range(BLK - 1):
                            last = mm(pQK[0:STATE, 1, m * P:(m + 1) * P], Bd[:, m, :], xn[:, m, :], start=True, stop=True)
                        last.then_inc(s_ssd_y, 1)
                    elif name == "ssd_off":
                        pe.wait_ge(s_y_skip, count.so_far("y_skip"))
                        pe.wait_ge(s_seg_exp, count.so_far("seg_exp"))
                        for m in range(1, BLK):
                            last = mm(pV[:, m * P:(m + 1) * P], CT[:, m * P:(m + 1) * P], St[:, m - 1, :],
                                      start=True, stop=True)
                        last.then_inc(s_ssd_off, 1)
                    elif name == "scores":
                        mg = arg
                        m, g = mg
                        before = 4 * (PHASE[z, layer] - 1)
                        pe.wait_ge(s_q_evac, count.nth("q_evac", before + m + 1))
                        pe.wait_ge(s_k_evac, count.nth("k_evac", before + m + 1))
                        pe.wait_ge(s_exp, count.nth("exp", n - 2))
                        bank = pS[n % 2]
                        mask = masks_h[:, 1:2, :] if m == 0 else masks_h[:, 2:3, :]
                        mm(bank[:, :, :], ident_h[:, :], mask.to_broadcast([P, 4, P]), start=True, stop=False,
                           skip_group_check=True)
                        for h in range(4):
                            c, r = h, DH * g
                            lo = m * P
                            q = qT[z][r:r + DH, c, lo:lo + P]
                            keys = kT[z][r:r + DH, c, lo:lo + WIN + P]
                            own_prev = keys[:, 0:2 * WIN].rearrange("p (a b) -> p a b", a=2)[:, ::-1, :]
                            mm(bank[0:WIN, h, :], q[:, 0:WIN], own_prev, start=False, stop=h == 3, skip_group_check=True)
                            last = mm(bank[WIN:P, h, :], q[:, WIN:P], keys[:, WIN:WIN + P], start=False, stop=h == 3,
                                      skip_group_check=True)
                        last.then_inc(s_scores, 1)
                    elif name == "turn_p":
                        mg = arg
                        pe.wait_ge(s_exp, count.nth("exp", n))
                        pe.wait_ge(s_p_evac, count.so_far("p_evac"))
                        pe.wait_ge(s_o_evac, count.so_far("o_evac"))
                        for h in range(4):
                            last = turn(pT[:, h, :], probs[:, n % 2, h, :], ident)
                        last.then_inc(s_turn_p, 1)
                    elif name == "pv":
                        mg = arg
                        m, g = mg
                        before = PHASE[z, layer] - 1
                        pe.wait_ge(s_v_shift, 16 * count.nth("v_shift", 4 * before + m + 1))
                        pe.wait_ge(s_v_next, 16 * count.nth("v_next", 3 * before + m))
                        pe.wait_ge(s_p_evac, count.nth("p_evac", n))
                        pe.wait_ge(s_o_norm, count.so_far("o_norm"))
                        pe.wait_ge(s_wo_add, count.so_far("wo_add"))
                        for h in range(4):
                            for row, values in ((0, v_even[z]), (WIN, v_odd[z])):
                                last = mm(pO[row:row + WIN, h * (DH + 1):(h + 1) * (DH + 1)],
                                          probsT[:, n % 2, h, row:row + WIN], values[:, m, 2 * h + g, :],
                                          start=True, stop=True)
                        last.then_inc(s_pv, 1)
                    elif name == "turn_o":
                        mg = arg
                        pe.wait_ge(s_o_norm, count.so_far("o_norm"))
                        pe.wait_ge(s_p_evac, count.so_far("p_evac"))
                        pe.wait_ge(s_o_evac, count.so_far("o_evac"))
                        for c in range(4):
                            last = turn(pT[:, c, :], otok[:, mg[0] % 2, c * P:(c + 1) * P], ident)
                        last.then_inc(s_turn_o, 1)
                    elif name == "wo":
                        mg = arg
                        pe.wait_ge(s_o_evac, count.so_far("o_evac"))
                        pe.wait_ge(s_o_norm, count.so_far("o_norm"))
                        for c in range(4):
                            last = mm(pO[:, 0:D], oT[:, c, :], wo_s[:, layer, c, :], start=c == 0, stop=c == 3)
                        last.then_inc(s_wo, 1)
                pe.drain()
                pe.sem_inc(s_turn_x, count.rest("turn_x"))
                pe.sem_inc(s_turn_h, count.rest("turn_h"))
                pe.sem_inc(s_turn_hn, count.rest("turn_hn"))
                pe.sem_inc(s_up, count.rest("up"))
                pe.sem_inc(s_down, count.rest("down"))
                pe.sem_inc(s_qkv, count.rest("qkv"))
                pe.sem_inc(s_turn_q, count.rest("turn_q"))
                pe.sem_inc(s_turn_k, count.rest("turn_k"))
                pe.sem_inc(s_turn_xn, count.rest("turn_xn"))
                pe.sem_inc(s_ssd_proj, count.rest("ssd_proj"))
                pe.sem_inc(s_ssd_g, count.rest("ssd_g"))
                pe.sem_inc(s_ssd_seg, count.rest("ssd_seg"))
                pe.sem_inc(s_ssd_y, count.rest("ssd_y"))
                pe.sem_inc(s_ssd_off, count.rest("ssd_off"))
                pe.sem_inc(s_scores, count.rest("scores"))
                pe.sem_inc(s_turn_p, count.rest("turn_p"))
                pe.sem_inc(s_pv, count.rest("pv"))
                pe.sem_inc(s_turn_o, count.rest("turn_o"))
                pe.sem_inc(s_wo, count.rest("wo"))
                pe.drain().then_inc(s_section, 1)
                pe.wait_ge(s_section, (count.section + 1) * 5)
                pe.sem_inc(s_hold, 1)

            pe.wait_ge(s_weights, N_WEIGHTS)
            pe.wait_ge(s_setup, 2)
            turn(pM[:, 0:P], wx_rows[:, :], ident).then_inc(s_wx, 1)
            pe.wait_ge(s_wx, 2)
            section(Count(0, FIRST))
            with pe.Fori(0, PASSES) as i:
                section(Count(i + 1, PASS, ORDER))
            section(Count(PASSES + 1, LAST))

        @block.scalar
        def _(act):
            activation = nc.scalar.activation

            def copy(out, in_):
                return activation(out, in_, ACT.Copy)

            def section(count):
                def link(ins):
                    ins.then_inc(s_act_chain, 1)
                    act.wait_ge(s_act_chain, count.next_link())

                for name, z, layer, arg, n in count.steps():
                    if name == "shift_lo":
                        act.wait_ge(s_turn_x, count.so_far("turn_x"))
                        act.wait_ge(s_qkv, count.so_far("qkv"))
                        act.wait_ge(s_turn_h, count.so_far("turn_h"))
                        copy(hT[0:D // 2, :], pM[0:D // 2, :]).then_inc(s_shift_lo, 1)
                    elif name == "ln_affine":
                        act.wait_ge(s_turn_hn, count.so_far("turn_hn"))
                        act.wait_ge(s_up, count.so_far("up"))
                        activation(hnT[:, :], pM[:, :], ACT.Identity, bias=lnb_s[:, layer:layer + 1],
                                          scale=lng_s[:, layer:layer + 1]).then_inc(s_ln_affine, 1)
                    elif name == "gelu":
                        j = arg
                        act.wait_ge(s_up, count.nth("up", n))
                        act.wait_ge(s_gate, count.nth("gate", n - 2))
                        src = pM[:, :] if j == 1 else pQK[:, 1, :]
                        size = SIZES[j]
                        activation(gates[0:size, n % 2, :], src[0:size], ACT.Gelu, bias=b1_s[0:size, layer, 1, j:j + 1]).then_inc(s_gelu, 1)
                    elif name == "qk_copy":
                        m = arg
                        act.wait_ge(s_qkv, count.nth("qkv", n))
                        act.wait_ge(s_rope_s, count.nth("rope_s", n - 2))
                        act.wait_ge(s_rope_c, count.nth("rope_c", n - 2))
                        act.wait_ge(s_qk_square, count.nth("qk_square", n - 2))
                        copy(qk[:, n % 2, :], pQK[:, :, :]).then_inc(s_qk_copy, 1)
                    elif name == "qk_square":
                        m = arg
                        act.wait_ge(s_qk_copy, count.nth("qk_copy", n))
                        act.wait_ge(s_qk_sum, count.nth("qk_sum", n - 1))
                        activation(sq[:, :], qk[:, n % 2, :], ACT.Square).then_inc(s_qk_square, 1)
                    elif name == "q_evac":
                        m = arg
                        act.wait_ge(s_turn_q, count.nth("turn_q", n))
                        copy(qT[z][:, :, m * P:(m + 1) * P], pM[:, :].rearrange("p (c t) -> p c t", c=4)).then_inc(s_q_evac, 1)
                    elif name == "k_evac":
                        m = arg
                        act.wait_ge(s_turn_k, count.nth("turn_k", n))
                        copy(kT[z][:, :, WIN + m * P:WIN + (m + 1) * P],
                             pM[:, :].rearrange("p (c t) -> p c t", c=4)).then_inc(s_k_evac, 1)
                    elif name == "v_evac":
                        m = arg
                        act.wait_ge(s_qkv, count.nth("qkv", n))
                        copy(v_odd[z][:, m, :, 0:DH],
                             pV[:, :].rearrange("p (h d) -> p h d", h=HEADS)).then_inc(s_v_evac, 1)
                    elif name == "xn_evac":
                        act.wait_ge(s_turn_xn, count.so_far("turn_xn"))
                        act.wait_ge(s_ssd_proj, count.so_far("ssd_proj"))
                        copy(xnT[:, :], pM[:, :]).then_inc(s_xn_evac, 1)
                    elif name == "bt_evac":
                        act.wait_ge(s_ssd_proj, count.so_far("ssd_proj"))
                        act.wait_ge(s_ssd_g, count.so_far("ssd_g"))
                        copy(BT[:, :], pQK[0:STATE, 0, :]).then_inc(s_bt_evac, 1)
                    elif name == "tok_evac":
                        act.wait_ge(s_ssd_proj, count.so_far("ssd_proj"))
                        act.wait_ge(s_mt, count.so_far("mt"))
                        copy(tok[:, :, :], pQK[:, 1, 0:BLK * (1 + STATE)].rearrange("p (m f) -> p m f", m=BLK)).then_inc(s_tok_evac, 1)
                    elif name == "dt_log":
                        act.wait_ge(s_dt_abs, count.so_far("dt_abs"))
                        act.wait_ge(s_decay, count.so_far("decay"))
                        link(activation(ez[:, :], nz[:, :], ACT.Exp))
                        activation(lz[:, :], ez[:, :], ACT.Ln, bias=1.0).then_inc(s_dt_log, 1)
                    elif name == "seg_exp":
                        act.wait_ge(s_ssd_seg, count.so_far("ssd_seg"))
                        act.wait_ge(s_mt, count.so_far("mt"))
                        act.wait_ge(s_y_off, count.so_far("y_off"))
                        activation(E[:, :, :], pV[:, :].rearrange("p (m l) -> p m l", m=BLK), ACT.Exp)
                        activation(et[:, :], pM[:, 0:2 * BLK], ACT.Exp).then_inc(s_seg_exp, 1)
                    elif name == "exp":
                        mg = arg
                        m, g = mg
                        act.wait_ge(s_smax, count.nth("smax", n))
                        act.wait_ge(s_turn_p, count.nth("turn_p", n - 2))
                        for h in range(4):
                            last = activation(probs[:, n % 2, h, :], pS[n % 2][:, h, :], ACT.Exp,
                                              bias=nb[:, n % 2, h:h + 1], scale=rnorm[z][:, m, 2 * h + g:2 * h + g + 1])
                        last.then_inc(s_exp, 1)
                    elif name == "p_evac":
                        mg = arg
                        act.wait_ge(s_turn_p, count.nth("turn_p", n))
                        act.wait_ge(s_pv, count.nth("pv", n - 2))
                        copy(probsT[:, n % 2, :, :], pT[:, :, :]).then_inc(s_p_evac, 1)
                    elif name == "o_evac":
                        mg = arg
                        act.wait_ge(s_turn_o, count.nth("turn_o", n))
                        act.wait_ge(s_wo, count.nth("wo", n - 1))
                        copy(oT[:, :, :], pT[:, :, :]).then_inc(s_o_evac, 1)
                act.drain()
                act.sem_inc(s_shift_lo, count.rest("shift_lo"))
                act.sem_inc(s_ln_affine, count.rest("ln_affine"))
                act.sem_inc(s_gelu, count.rest("gelu"))
                act.sem_inc(s_qk_copy, count.rest("qk_copy"))
                act.sem_inc(s_qk_square, count.rest("qk_square"))
                act.sem_inc(s_q_evac, count.rest("q_evac"))
                act.sem_inc(s_k_evac, count.rest("k_evac"))
                act.sem_inc(s_v_evac, count.rest("v_evac"))
                act.sem_inc(s_xn_evac, count.rest("xn_evac"))
                act.sem_inc(s_bt_evac, count.rest("bt_evac"))
                act.sem_inc(s_tok_evac, count.rest("tok_evac"))
                act.sem_inc(s_dt_log, count.rest("dt_log"))
                act.sem_inc(s_seg_exp, count.rest("seg_exp"))
                act.sem_inc(s_exp, count.rest("exp"))
                act.sem_inc(s_p_evac, count.rest("p_evac"))
                act.sem_inc(s_o_evac, count.rest("o_evac"))
                act.sem_inc(s_act_chain, CHAIN - count.links)
                act.drain().then_inc(s_section, 1)
                act.wait_ge(s_section, (count.section + 1) * 5)
                act.sem_inc(s_hold, 1)

            act.wait_ge(s_weights, N_WEIGHTS)
            activation(ssd_par[:, 3:4], ssd_par[:, 1:2], ACT.Exp).then_inc(s_rows, 1)
            section(Count(0, FIRST))
            with act.Fori(0, PASSES) as i:
                section(Count(i + 1, PASS, ORDER))
            section(Count(PASSES + 1, LAST))

        @block.vector
        def _(dve):
            v = nc.vector

            def section(count):
                def link(ins):
                    ins.then_inc(s_dve_chain, 1)
                    dve.wait_ge(s_dve_chain, count.next_link())

                def halves(a):
                    return a.rearrange("p (a h f) -> p a h f", a=2, h=HEADS)
                for name, z, layer, arg, n in count.steps():
                    if name == "shift_hi":
                        dve.wait_ge(s_turn_x, count.so_far("turn_x"))
                        dve.wait_ge(s_qkv, count.so_far("qkv"))
                        dve.wait_ge(s_turn_h, count.so_far("turn_h"))
                        v.tensor_copy(hT[D // 2:D, 1:T], pM[D // 2:D, 0:T - 1]).then_inc(s_shift_hi, 1)
                    elif name == "ln_stats":
                        kind = arg
                        if kind == "x":
                            dve.wait_ge(s_loaded[z], (count.section + (1 if z == 0 else 0)) * 16)
                        dve.wait_ge(s_turn_h, count.so_far("turn_h"))
                        dve.wait_ge(s_y_off, count.so_far("y_off"))
                        dve.wait_ge(s_ln_apply, count.so_far("ln_apply"))
                        dve.wait_ge(s_ln_rstd, count.so_far("ln_rstd"))
                        dve.wait_ge(s_resid, count.so_far("resid"))
                        src = {"h": pV[:, :].rearrange("p (m d) -> p m d", m=BLK), "x": xin[z], "y": y, "1": x1[z],
                               "o": xres[z]}[kind]
                        for m in range(BLK):
                            ins = v.bn_stats(stats[:, m, :], src[:, m, :])
                        link(ins)
                        dve.sem_inc(s_hold, 1)
                        for m in range(BLK):
                            last = v.bn_aggr(mv[:, m, :], stats[:, m, :])
                        last.then_inc(s_ln_stats, 1)
                    elif name == "ln_apply":
                        kind = arg
                        dve.wait_ge(s_ln_rstd, count.so_far("ln_rstd"))
                        dve.wait_ge(s_ln_stats, count.so_far("ln_stats"))
                        src = {"h": pV[:, :].rearrange("p (m d) -> p m d", m=BLK), "x": xin[z], "y": y, "1": x1[z],
                               "o": xres[z]}[kind]
                        dst = {"h": hn, "x": xn, "y": yn, "1": xres[z], "o": yn}[kind]
                        if kind == "h":
                            dve.wait_ge(s_turn_hn, count.so_far("turn_hn"))
                        if kind == "o":
                            dve.wait_ge(s_stored[z], count.section * 16)
                        for m in range(BLK):
                            last = v.tensor_scalar(dst[:, m, :], src[:, m, :], mv[:, m, 0:1], rstd[:, m:m + 1],
                                                   ALU.subtract, ALU.mult)
                        if kind == "y":
                            link(last)
                            last = v.tensor_tensor(x1[z][:, :, :], xin[z][:, :, :], yn[:, :, :], ALU.add)
                        if kind == "o":
                            link(last)
                            last = v.tensor_tensor(outb[z][:, :, :], x1[z][:, :, :], yn[:, :, :], ALU.add)
                        last.then_inc(s_ln_apply, 1)
                    elif name == "gate":
                        j = arg
                        dve.wait_ge(s_gelu, count.nth("gelu", n))
                        dve.wait_ge(s_down, count.so_far("down"))
                        src = pV[:, :] if j == 1 else pQK[:, 0, :]
                        size = SIZES[j]
                        v.scalar_tensor_tensor(uT[0:size, j, :], src[0:size], b1_s[0:size, layer, 0, j:j + 1],
                                                      gates[0:size, n % 2, :], ALU.add, ALU.mult).then_inc(s_gate, 1)
                    elif name == "resid":
                        dve.wait_ge(s_down, count.so_far("down"))
                        dve.wait_ge(s_resid_bias, count.so_far("resid_bias"))
                        dve.wait_ge(s_turn_x, count.so_far("turn_x"))
                        v.tensor_tensor(xres[z][:, :, :], pV[:, :].rearrange("p (m d) -> p m d", m=BLK),
                                               xb[:, :, :], ALU.add).then_inc(s_resid, 1)
                    elif name == "rope_s":
                        m = arg
                        dve.wait_ge(s_qk_copy, count.nth("qk_copy", n))
                        dve.wait_ge(s_rope_add, count.nth("rope_add", n - 1))
                        q, o, hf = halves(qk[:, n % 2, :]), halves(rs[:, :]), DH // 2
                        for a, b in ((0, hf), (hf, 0)):
                            table = tab_s[:, layer, m, :, a:a + hf].unsqueeze(2).to_broadcast([P, 2, HEADS, hf])
                            last = v.tensor_tensor(o[:, :, :, a:a + hf], q[:, :, :, b:b + hf], table, ALU.mult)
                        last.then_inc(s_rope_s, 1)
                    elif name == "qk_sum":
                        m = arg
                        dve.wait_ge(s_qk_square, count.nth("qk_square", n))
                        dve.wait_ge(s_rinv, count.nth("rinv", n - 1))
                        v.tensor_reduce(ss[:, :], sq[:, :].rearrange("p (h d) -> p h d", d=DH), AX.X, ALU.add).then_inc(s_qk_sum, 1)
                    elif name == "rinv":
                        m = arg
                        dve.wait_ge(s_qk_sum, count.nth("qk_sum", n))
                        link(v.tensor_scalar(ssc[:, :], ss[:, :], 1e-24, None, ALU.max))
                        link(v.tensor_scalar(guess[:, :].bitcast(I32), ssc[:, :].bitcast(I32), -0.5, float(0x5f3759df),
                                             ALU.mult, ALU.add))
                        for step in range(3):
                            link(v.tensor_tensor(square[:, :], guess[:, :], guess[:, :], ALU.mult))
                            link(v.scalar_tensor_tensor(square[:, :], square[:, :], -0.5, ssc[:, :], ALU.mult, ALU.mult))
                            to = guess[:, :] if step < 2 else rnorm[z][:, m, :]
                            last = v.scalar_tensor_tensor(to, square[:, :], 1.5, guess[:, :], ALU.add, ALU.mult)
                            if step < 2:
                                link(last)
                        last.then_inc(s_rinv, 1)
                    elif name == "rope_add":
                        m = arg
                        dve.wait_ge(s_rope_c, count.nth("rope_c", n))
                        dve.wait_ge(s_rope_s, count.nth("rope_s", n))
                        dve.wait_ge(s_turn_k, count.nth("turn_k", n - 2))
                        v.tensor_tensor(rot[:, n % 2, :], rc[:, :], rs[:, :], ALU.add).then_inc(s_rope_add, 1)
                    elif name == "ct_evac":
                        dve.wait_ge(s_ssd_proj, count.so_far("ssd_proj"))
                        dve.wait_ge(s_ssd_off, count.so_far("ssd_off"))
                        v.tensor_copy(CT[:, :], pQK[STATE:P, 0, :]).then_inc(s_ct_evac, 1)
                    elif name == "dt_abs":
                        dve.wait_ge(s_tok_evac, count.so_far("tok_evac"))
                        link(v.tensor_scalar(zb[:, :], tok[:, :, 0], ssd_par[:, 0:1], None, ALU.add))
                        v.scalar_tensor_tensor(nz[:, :], zb[:, :], -1.0, zb[:, :], ALU.mult, ALU.min).then_inc(s_dt_abs, 1)
                    elif name == "decay":
                        dve.wait_ge(s_dt_log, count.so_far("dt_log"))
                        dve.wait_ge(s_ssd_seg, count.so_far("ssd_seg"))
                        link(v.scalar_tensor_tensor(dts[:, :], zb[:, :], 0.0, lz[:, :], ALU.max, ALU.add))
                        link(v.tensor_scalar(adt[:, :], dts[:, :], ssd_par[:, 3:4], None, ALU.mult))
                        v.tensor_tensor(R[:, :, :], upto.unsqueeze(1).to_broadcast([P, BLK, P]),
                                               adt[:, :].unsqueeze(2).to_broadcast([P, BLK, P]), ALU.mult).then_inc(s_decay, 1)
                    elif name == "mt":
                        dve.wait_ge(s_ssd_g, count.so_far("ssd_g"))
                        dve.wait_ge(s_seg_exp, count.so_far("seg_exp"))
                        dve.wait_ge(s_ssd_y, count.so_far("ssd_y"))
                        link(v.tensor_tensor(wdt[:, :], dts[:, :], E[:, :, P - 1], ALU.mult))
                        v.tensor_tensor(Bd[:, :, :], tok[:, :, 1:1 + STATE],
                                        wdt[:, :].unsqueeze(2).to_broadcast([P, BLK, STATE]), ALU.mult)
                        for m in range(BLK):
                            last = v.scalar_tensor_tensor(MT[:, m, :], pQK[:, 0, m * P:(m + 1) * P], dts[:, m:m + 1],
                                                          E[:, m, :], ALU.mult, ALU.mult)
                        last.then_inc(s_mt, 1)
                    elif name == "y_skip":
                        dve.wait_ge(s_ssd_y, count.so_far("ssd_y"))
                        dve.wait_ge(s_ssd_off, count.so_far("ssd_off"))
                        v.scalar_tensor_tensor(y[:, :, :], xn[:, :, :], ssd_par[:, 2:3],
                                               pM[:, :].rearrange("p (m d) -> p m d", m=BLK), ALU.mult, ALU.add)
                        last = v.tensor_copy(St[:, 0, :], pQK[0:STATE, 1, 0:D])
                        for m in range(1, BLK - 1):
                            link(last)
                            last = v.scalar_tensor_tensor(St[:, m, :], St[:, m - 1, :], et[0:STATE, BLK + m:BLK + m + 1],
                                                          pQK[0:STATE, 1, m * D:(m + 1) * D], ALU.mult, ALU.add)
                        last.then_inc(s_y_skip, 1)
                    elif name == "y_off":
                        dve.wait_ge(s_ssd_off, count.so_far("ssd_off"))
                        dve.wait_ge(s_y_skip, count.so_far("y_skip"))
                        for m in range(1, BLK):
                            last = v.scalar_tensor_tensor(y[:, m, :], pV[:, m * D:(m + 1) * D], et[:, m:m + 1], y[:, m, :],
                                                          ALU.mult, ALU.add)
                        last.then_inc(s_y_off, 1)
                    elif name == "smax":
                        mg = arg
                        m, g = mg
                        dve.wait_ge(s_rinv, count.nth("rinv", 4 * (PHASE[z, layer] - 1) + m + 1))
                        dve.wait_ge(s_scores, count.nth("scores", n))
                        dve.wait_ge(s_exp, count.nth("exp", n - 2))
                        link(v.tensor_reduce(nmx[:, n % 2, :], pS[n % 2][:, :, :], AX.X, ALU.max, negate=True))
                        v.tensor_tensor(nb[:, n % 2, :], nmx[:, n % 2, :], rnorm[z][:, m, g:HEADS:2], ALU.mult).then_inc(s_smax, 1)
                    elif name == "o_norm":
                        mg = arg
                        m, g = mg
                        dve.wait_ge(s_pv, count.nth("pv", n))
                        dve.wait_ge(s_turn_o, count.nth("turn_o", (n - 1) // 2 - 1))
                        o = pO[:, 0:4 * (DH + 1)].rearrange("p (h d) -> p h d", h=4)
                        link(v.reciprocal(rl[:, :], o[:, :, DH]))
                        dst = otok[:, m % 2, :].rearrange("p (h a d) -> p a h d", h=4, a=2)[:, g, :, :]
                        v.tensor_tensor(dst, o[:, :, 0:DH], rl[:, :].unsqueeze(2).to_broadcast([P, 4, DH]), ALU.mult).then_inc(s_o_norm, 1)
                    elif name == "wo_add":
                        mg = arg
                        m = mg[0]
                        dve.wait_ge(s_wo, count.so_far("wo"))
                        v.tensor_tensor(xres[z][:, m, :], xres[z][:, m, :], pO[:, 0:D], ALU.add).then_inc(s_wo_add, 1)
                dve.drain()
                dve.sem_inc(s_shift_hi, count.rest("shift_hi"))
                dve.sem_inc(s_ln_stats, count.rest("ln_stats"))
                dve.sem_inc(s_ln_apply, count.rest("ln_apply"))
                dve.sem_inc(s_gate, count.rest("gate"))
                dve.sem_inc(s_resid, count.rest("resid"))
                dve.sem_inc(s_rope_s, count.rest("rope_s"))
                dve.sem_inc(s_qk_sum, count.rest("qk_sum"))
                dve.sem_inc(s_rinv, count.rest("rinv"))
                dve.sem_inc(s_rope_add, count.rest("rope_add"))
                dve.sem_inc(s_ct_evac, count.rest("ct_evac"))
                dve.sem_inc(s_dt_abs, count.rest("dt_abs"))
                dve.sem_inc(s_decay, count.rest("decay"))
                dve.sem_inc(s_mt, count.rest("mt"))
                dve.sem_inc(s_y_skip, count.rest("y_skip"))
                dve.sem_inc(s_y_off, count.rest("y_off"))
                dve.sem_inc(s_smax, count.rest("smax"))
                dve.sem_inc(s_o_norm, count.rest("o_norm"))
                dve.sem_inc(s_wo_add, count.rest("wo_add"))
                dve.sem_inc(s_dve_chain, CHAIN - count.links)
                dve.drain().then_inc(s_section, 1)
                dve.wait_ge(s_section, (count.section + 1) * 5)
                dve.sem_inc(s_hold, 1)

            for z in range(2):
                v.memset(kT[z][:, :, 0:WIN], 0.0)
                v.memset(v_odd[z][:, :, :, DH:DH + 1], 1.0)
                v.memset(v_even[z][:, :, :, DH:DH + 1], 1.0)
                v.memset(v_even[z][WIN:P, 0, :, 0:DH], 0.0)
                v.memset(xres[z][:, :, :], 0.0)
                v.memset(x1[z][:, :, :], 0.0)
            v.memset(hT[D // 2:D, 0:1], 0.0)
            v.memset(ones[:, :], 1.0)
            v.memset(minus_half[:, :], -0.5).then_inc(s_setup, 1)
            dve.wait_ge(s_weights, N_WEIGHTS)
            v.tensor_copy(ident_h[:, :], ident)
            v.tensor_copy(masks_h[:, :, :], cst[:, 3 * P:6 * P].rearrange("p (k j) -> p k j", k=3))
            hf = DH // 2
            v.tensor_scalar(scales[:, :, 0, :], scales[:, :, 0, :], QK_SCALE, None, ALU.mult).then_inc(s_scaled, 1)
            dve.wait_ge(s_scaled, 1)
            for l in range(DEPTH):
                wide = [P, BLK, 2, DH]
                v.tensor_tensor(tab_c[:, l, :, :, :], rope_cos, scales[:, l, :, :].unsqueeze(1).to_broadcast(wide), ALU.mult)
                for a, b in ((0, hf), (hf, 0)):
                    last = v.tensor_tensor(tab_s[:, l, :, :, a:a + hf], rope_sin[:, :, :, a:a + hf],
                                           scales[:, l, :, b:b + hf].unsqueeze(1).to_broadcast([P, BLK, 2, hf]), ALU.mult)
            dve.wait_ge(s_rows, 1)
            v.tensor_scalar(ssd_par[:, 3:4], ssd_par[:, 3:4], -1.0, None, ALU.mult).then_inc(s_setup, 1)
            dve.wait_ge(s_wx, 1)
            v.tensor_copy(wx_bc[:, :], pM[:, 0:P])
            v.tensor_copy(wx_tok[:, 1:1 + STATE], pM[:, 0:STATE]).then_inc(s_wx, 1)
            dve.wait_ge(s_wx, 2)
            section(Count(0, FIRST))
            with dve.Fori(0, PASSES) as i:
                section(Count(i + 1, PASS, ORDER))
            section(Count(PASSES + 1, LAST))

        @block.gpsimd
        def _(pool):
            g = nc.gpsimd

            def section(count):
                def link(ins):
                    ins.then_inc(s_pool_chain, 1)
                    pool.wait_ge(s_pool_chain, count.next_link())

                for name, z, layer, arg, n in count.steps():
                    if name == "ln_rstd":
                        kind = arg
                        pool.wait_ge(s_ln_stats, count.so_far("ln_stats"))
                        pool.wait_ge(s_ln_apply, count.so_far("ln_apply"))
                        pool.sem_inc(s_hold, 1)
                        link(g.tensor_scalar(veps[:, :], mv[:, :, 1], LN_EPS, None, ALU.add))
                        g.tensor_tensor(rstd[:, :], veps[:, :], minus_half[:, :], ALU.pow).then_inc(s_ln_rstd, 1)
                    elif name == "resid_bias":
                        pool.wait_ge(s_wo_add, count.nth("wo_add", 4 * REST_PHASE[z, layer]))
                        pool.wait_ge(s_resid, count.so_far("resid"))
                        g.tensor_tensor(xb[:, :, :], xres[z][:, :, :],
                                               b2_s[:, layer, :].unsqueeze(1).to_broadcast([P, BLK, D]), ALU.add).then_inc(s_resid_bias, 1)
                    elif name == "rope_c":
                        m = arg
                        pool.wait_ge(s_qk_copy, count.nth("qk_copy", n))
                        pool.wait_ge(s_rope_add, count.nth("rope_add", n - 1))
                        for a in range(2):
                            q = qk[:, n % 2, a * INNER:(a + 1) * INNER].rearrange("p (h f) -> p h f", h=HEADS)
                            o = rc[:, a * INNER:(a + 1) * INNER].rearrange("p (h f) -> p h f", h=HEADS)
                            table = tab_c[:, layer, m, a, :].unsqueeze(1).to_broadcast([P, HEADS, DH])
                            last = g.tensor_tensor(o, q, table, ALU.mult)
                        last.then_inc(s_rope_c, 1)
                    elif name == "k_scale":
                        m = arg
                        pool.wait_ge(s_rope_add, count.nth("rope_add", n))
                        pool.wait_ge(s_rinv, count.nth("rinv", n))
                        k = rot[:, n % 2, INNER:2 * INNER].rearrange("p (h f) -> p h f", h=HEADS)
                        g.tensor_tensor(k, k, rnorm[z][:, arg, HEADS:2 * HEADS].unsqueeze(2).to_broadcast([P, HEADS, DH]),
                                               ALU.mult).then_inc(s_k_scale, 1)
                pool.drain()
                pool.sem_inc(s_ln_rstd, count.rest("ln_rstd"))
                pool.sem_inc(s_resid_bias, count.rest("resid_bias"))
                pool.sem_inc(s_rope_c, count.rest("rope_c"))
                pool.sem_inc(s_k_scale, count.rest("k_scale"))
                pool.sem_inc(s_pool_chain, CHAIN - count.links)
                pool.drain().then_inc(s_section, 1)
                pool.wait_ge(s_section, (count.section + 1) * 5)
                pool.sem_inc(s_hold, 1)

            pool.wait_ge(s_setup, 2)
            section(Count(0, FIRST))
            with pool.Fori(0, PASSES) as i:
                section(Count(i + 1, PASS, ORDER))
            section(Count(PASSES + 1, LAST))


_INS = ['L0_attn_x', 'L0_attn_W_xproj', 'L0_attn_dt_bias', 'L0_attn_A_log', 'L0_attn_D', 'L0_ffn_wqkv',
        'L0_ffn_q_scale', 'L0_ffn_k_scale', 'L0_ffn_wo', 'L0_ffn_ln_g', 'L0_ffn_ln_b', 'L0_ffn_w1', 'L0_ffn_b1',
        'L0_ffn_w2', 'L0_ffn_b2']


def kernel(**inputs):
    import concourse.bacc as _bacc
    from concourse.bass_utils import run_bass_kernel_spmd as _run

    nc = _bacc.Bacc("TRN2", target_bir_lowering=False, num_devices=1)
    arrays, args = {}, []
    for name in _INS:
        a = np.ascontiguousarray(inputs[name])
        arrays[f"in_{name}_dram"] = a
        args.append(nc.dram_tensor(f"in_{name}_dram", a.shape, F32, kind="ExternalInput").ap())
    shape = inputs['L0_attn_x'].shape
    const = shape_constants(shape[1])
    arrays["const_dram"] = const
    args.append(nc.dram_tensor("const_dram", const.shape, F32, kind="ExternalInput").ap())
    args.append(nc.dram_tensor("out_0_dram", shape, F32, kind="ExternalOutput").ap())
    build(nc, *args)
    r = _run(nc, [arrays], core_ids=[0])
    return r.results[0]["out_0_dram"]
```

```python
from contextlib import ExitStack

import numpy as np
import concourse.bass as bass
from concourse import mybir

F32 = mybir.dt.float32
BF16 = mybir.dt.bfloat16
ALU = mybir.AluOpType
ACT = mybir.ActivationFunctionType
AX = mybir.AxisListType

P = 128
D = 128
STATE = 64
HEADS, DH, WIN = 8, 64, 64
INNER = HEADS * DH
QK_SCALE = 8.0
NEG = -1.0e30
LN_EPS = 1e-5
CHUNKS = 3
STRIDE = 64
CHAIN = 1024


def shape_constants(tokens):
    k = np.arange(P)
    ident = (k[:, None] == k[None, :]).astype(np.float32)
    upto = (k[:, None] <= k[None, :]).astype(np.float32)
    later = (k[:, None] > k[None, :]).astype(np.float32)
    causal = np.where(k[:, None] <= k[None, :], 0.0, NEG).astype(np.float32)
    i = (k % WIN)[:, None]
    j = np.arange(WIN)[None, :]
    own = np.where(j <= i, 0.0, NEG)
    prev = np.where(j >= i, 0.0, NEG)
    even = k[:, None] < WIN
    rest = np.concatenate([np.where(even, own, prev), np.where(even, prev, own)], axis=1).astype(np.float32)
    first = rest.copy()
    first[:WIN, WIN:] = NEG
    half = np.arange(0, DH, 2, dtype=np.float32)
    inv_freq = (1.0 / np.float32(10000.0) ** (half / np.float32(DH))).astype(np.float32)
    t = np.arange(tokens, dtype=np.float32)
    freqs = (t[:, None] * inv_freq[None, :]).astype(np.float32)
    base = ((half + np.float32(0.4 * DH)) / np.float32(1.4 * DH)).astype(np.float32)
    power = ((t - tokens // 2) / np.float32(WIN // 2)).astype(np.float32)
    scale = (base[None, :] ** power[:, None]).astype(np.float32)
    cos, sin = np.cos(freqs), np.sin(freqs)
    cosines = np.stack([np.tile(cos * scale, 2), np.tile(cos / scale, 2)], axis=1)
    sines = np.stack([np.concatenate([-sin * scale, sin * scale], 1), np.concatenate([-sin / scale, sin / scale], 1)],
                     axis=1)

    def rows(a):
        return a.reshape(tokens // P, P, 2 * DH).transpose(1, 0, 2).reshape(P, -1)

    return np.ascontiguousarray(
        np.concatenate([ident, upto, later, causal, first, rest, rows(cosines), rows(sines)], axis=1).astype(np.float32))


def attention_steps(z, layer):
    units = [(m, g) for m in range(4) for g in range(2)]
    slots = []
    for k in range(len(units) + 2):
        now, late, last = [], [], []
        if k < len(units):
            for name in ("scores", "smax", "exp"):
                now.append((name, z, layer, units[k]))
        if 0 < k <= len(units):
            m, g = units[k - 1]
            now += [(name, z, layer, (m, g)) for name in ("turn_p", "p_evac")]
            late += [(name, z, layer, (m, g)) for name in ("pv", "o_norm")]
            if g == 1:
                last += [(name, z, layer, (m, g)) for name in ("turn_o", "o_evac")]
        if k > 1 and units[k - 2][1] == 1:
            m, g = units[k - 2]
            now += [(name, z, layer, (m, g)) for name in ("wo", "wo_add")]
        slots += now + late + last
    return slots


def ln_steps(z, layer, kind):
    return [(n, z, layer, kind) for n in ("ln_stats", "ln_rstd", "ln_apply")]


def mlp_steps(z, layer, beside=()):
    s = [(n, z, layer, "mlp") for n in ("turn_x", "shift_lo", "shift_hi", "resid_bias", "turn_h")]
    s += ln_steps(z, layer, "h")
    s += [(n, z, layer, 0) for n in ("turn_hn", "ln_affine")]
    s += [("up", z, layer, 0), ("up", z, layer, 1), ("gelu", z, layer, 0), ("gate", z, layer, 0), ("up", z, layer, 2)]
    s += [(n, z, layer, j) for j in (1, 2) for n in ("gelu", "gate")]
    s += beside
    s += [("down", z, layer, 0), ("resid", z, layer, 0)]
    return s


def qkv_steps(z, layer):
    s = [(n, z, layer, "qkv") for n in ("turn_x", "shift_lo", "shift_hi")]
    for m in range(5):
        if m < 4:
            s += [(n, z, layer, m) for n in ("proj_q", "q_copy", "proj_k", "k_copy", "proj_v", "v_evac", "rope_c",
                                             "qk_square", "v_shift", "rope_s", "qk_sum", "rinv", "rope_add", "k_scale")]
            s += [("v_next", z, layer, m)] if m < 3 else []
        if m > 0:
            s += [(n, z, layer, m - 1) for n in ("turn_q", "q_evac", "turn_k", "k_evac")]
    return s


def output_steps(z):
    return ln_steps(z, 1, "o") + [("store", z, 1, 0)]


def ssd_norm_steps(z):
    return ln_steps(z, 0, "x") + [(n, z, 0, 0) for n in ("turn_xn", "xn_evac")]


def ssd_steps(z):
    s = [(n, z, 0, 0) for n in (
        "ssd_proj", "bt_evac", "ct_evac", "tok_evac", "dt_abs", "dt_log", "decay", "ssd_g",
        "ssd_seg", "seg_exp", "mt", "ssd_y", "y_skip", "ssd_off", "y_off")]
    return s + ln_steps(z, 0, "y") + [("load", z, 0, 0)] + ln_steps(z, 0, "1")


PHASE = {(0, 0): 0, (1, 0): 1, (0, 1): 2, (1, 1): 3}
REST_PHASE = {(1, 1): 0, (0, 0): 1, (1, 0): 2, (0, 1): 3}

FIRST = ssd_norm_steps(0) + ssd_steps(0) + qkv_steps(0, 0)
ATTENTION = [attention_steps(0, 0), attention_steps(1, 0), attention_steps(0, 1), attention_steps(1, 1)]
REST = [mlp_steps(1, 1, ssd_norm_steps(1)) + output_steps(1) + ssd_steps(1) + qkv_steps(1, 0),
        mlp_steps(0, 0) + qkv_steps(0, 1),
        mlp_steps(1, 0) + qkv_steps(1, 1),
        mlp_steps(0, 1, ssd_norm_steps(0)) + output_steps(0) + ssd_steps(0) + qkv_steps(0, 0)]
PASS = sum(ATTENTION, []) + sum(REST, [])
ORDER = [
    288, 289, 290, 292, 293, 291, 294, 0, 1, 2, 3, 295, 6, 296, 4, 10, 297, 298, 5, 299, 307, 300, 301, 308,
    309, 302, 303, 305, 304, 11, 7, 310, 311, 306, 8, 9, 318, 321, 320, 319, 322, 312, 13, 313, 323, 14, 325,
    15, 324, 16, 326, 12, 17, 327, 314, 328, 19, 18, 24, 20, 329, 22, 25, 23, 315, 316, 28, 21, 330, 29, 26,
    331, 31, 27, 332, 333, 32, 37, 38, 33, 30, 34, 334, 335, 337, 35, 46, 47, 36, 40, 39, 42, 41, 43, 49, 55,
    50, 44, 338, 339, 45, 340, 48, 342, 341, 51, 345, 346, 343, 56, 52, 344, 53, 347, 349, 54, 350, 360, 348,
    361, 358, 352, 359, 362, 58, 353, 365, 351, 59, 60, 354, 355, 373, 61, 379, 57, 380, 356, 363, 62, 364, 377,
    374, 398, 375, 381, 63, 357, 368, 367, 378, 370, 369, 376, 382, 64, 72, 73, 400, 384, 392, 65, 66, 67, 371,
    75, 383, 68, 399, 74, 401, 387, 393, 394, 396, 69, 395, 76, 78, 386, 397, 389, 70, 82, 366, 403, 71, 388,
    405, 410, 79, 80, 385, 77, 83, 411, 390, 406, 85, 418, 86, 81, 91, 402, 87, 412, 419, 407, 84, 420, 422, 88,
    92, 372, 423, 424, 336, 89, 408, 413, 409, 404, 100, 90, 93, 96, 94, 97, 95, 414, 425, 109, 426, 98, 101,
    415, 416, 427, 103, 102, 428, 104, 99, 110, 105, 106, 417, 429, 421, 430, 433, 431, 432, 434, 435, 118, 391,
    107, 436, 437, 438, 108, 119, 111, 112, 114, 113, 439, 115, 121, 116, 440, 441, 442, 122, 443, 444, 117,
    123, 445, 449, 457, 124, 448, 452, 458, 120, 127, 125, 459, 451, 460, 126, 476, 446, 454, 447, 478, 472,
    464, 473, 461, 477, 466, 453, 467, 317, 463, 479, 462, 455, 130, 132, 133, 128, 131, 495, 474, 497, 483,
    469, 496, 485, 450, 456, 475, 480, 134, 129, 498, 481, 491, 468, 492, 470, 486, 482, 136, 135, 137, 144,
    145, 146, 138, 147, 139, 140, 471, 487, 493, 141, 502, 499, 148, 142, 488, 501, 505, 489, 494, 506, 150,
    500, 143, 504, 154, 151, 509, 155, 152, 149, 510, 153, 507, 157, 517, 158, 518, 465, 511, 163, 519, 159,
    521, 164, 156, 508, 520, 160, 522, 512, 165, 484, 523, 513, 514, 524, 172, 161, 173, 162, 181, 166, 168,
    169, 167, 515, 516, 525, 175, 526, 174, 176, 170, 503, 527, 171, 177, 529, 528, 530, 531, 532, 178, 182,
    190, 534, 533, 535, 179, 183, 180, 536, 184, 185, 537, 538, 540, 186, 539, 543, 541, 187, 188, 191, 189,
    544, 542, 548, 551, 193, 194, 545, 558, 192, 556, 550, 546, 195, 199, 557, 547, 196, 197, 553, 559, 563,
    490, 198, 549, 575, 200, 552, 577, 565, 201, 562, 202, 560, 203, 204, 566, 554, 567, 561, 578, 205, 208,
    206, 555, 571, 579, 576, 209, 568, 207, 581, 210, 572, 596, 580, 584, 211, 212, 582, 597, 573, 598, 569,
    585, 213, 214, 215, 594, 587, 599, 616, 574, 595, 586, 618, 617, 590, 601, 620, 603, 600, 216, 621, 622,
    591, 592, 604, 623, 593, 570, 588, 606, 589, 219, 608, 609, 610, 611, 624, 625, 612, 605, 607, 626, 619,
    564, 635, 636, 613, 628, 217, 220, 614, 629, 615, 627, 631, 637, 630, 632, 633, 638, 634, 639, 218, 646,
    648, 649, 650, 640, 641, 647, 651, 653, 222, 221, 652, 654, 226, 642, 655, 656, 223, 224, 229, 230, 643,
    657, 583, 235, 227, 225, 228, 658, 236, 231, 659, 232, 660, 661, 233, 602, 644, 662, 234, 238, 237, 239,
    240, 241, 247, 248, 663, 244, 242, 253, 665, 243, 245, 666, 249, 667, 668, 250, 251, 246, 670, 669, 673,
    674, 254, 671, 675, 672, 688, 678, 676, 686, 685, 690, 689, 252, 687, 258, 256, 255, 257, 681, 677, 705,
    707, 680, 682, 693, 683, 691, 695, 692, 708, 696, 697, 265, 262, 259, 260, 709, 271, 261, 679, 706, 712,
    694, 684, 700, 701, 710, 698, 266, 263, 702, 728, 714, 267, 703, 268, 719, 729, 724, 264, 704, 713, 269,
    270, 726, 720, 272, 711, 725, 715, 276, 277, 717, 721, 699, 727, 274, 722, 733, 731, 716, 734, 275, 273,
    278, 280, 723, 738, 281, 279, 282, 283, 730, 739, 718, 740, 645, 732, 741, 735, 736, 284, 285, 742, 737,
    743, 286, 664, 744, 287, 745,
]
LAST = mlp_steps(1, 1) + output_steps(1)


def build(nc, x, w_xproj, dt_bias, a_log, d_skip, wqkv, q_scale, k_scale, wo, ln_g, ln_b, w1, b1, w2, b2, const, out):
    SEQS, T, _ = x.shape
    BLK = T // P
    DEPTH = wqkv.shape[0]
    HID = w2.shape[1]
    SIZES = [min(P, HID - P * j) for j in range(CHUNKS)]
    PASSES = SEQS // 2
    assert T == 512 and D == P and SEQS % 2 == 0

    ctx = ExitStack()
    with ctx:
        def sb(name, shape, dt=F32):
            return ctx.enter_context(nc.sbuf_tensor(name, shape, dt))

        def ps(name, shape):
            return ctx.enter_context(nc.psum_tensor(name, shape, F32))

        cst = sb("cst", [P, const.shape[1]])
        ident, upto, later = cst[:, 0:P], cst[:, P:2 * P], cst[:, 2 * P:3 * P]
        rope_cos = cst[:, 6 * P:6 * P + BLK * P].rearrange("p (m a f) -> p m a f", m=BLK, a=2)
        rope_sin = cst[:, 6 * P + BLK * P:6 * P + 2 * BLK * P].rearrange("p (m a f) -> p m a f", m=BLK, a=2)
        ident_h = sb("ident_h", [P, P], BF16)
        masks_h = sb("masks_h", [P, 3, P], BF16)
        wx_rows = sb("wx_rows", [P, D])
        wx_bc = sb("wx_bc", [D, P])
        wx_tok = sb("wx_tok", [D, 1 + STATE])
        wqkv_s = sb("wqkv_s", [D, DEPTH, 3 * INNER])
        wo_s = sb("wo_s", [P, DEPTH, INNER // P, D])
        w1_s = sb("w1_s", [D, DEPTH, 2 * HID])
        w2_s = sb("w2_s", [P, DEPTH, CHUNKS, D])
        b1_s = sb("b1_s", [P, DEPTH, 2, CHUNKS])
        b2_s = sb("b2_s", [P, DEPTH, D])
        lng_s = sb("lng_s", [P, DEPTH])
        lnb_s = sb("lnb_s", [P, DEPTH])
        scales = sb("scales", [P, DEPTH, 2, DH])
        ssd_par = sb("ssd_par", [P, 4])
        tab_c = sb("tab_c", [P, DEPTH, BLK, 2, DH])
        tab_s = sb("tab_s", [P, DEPTH, BLK, 2, DH])
        ones = sb("ones", [P, P])
        minus_half = sb("minus_half", [P, 2 * HEADS])

        xin = [sb(f"xin{z}", [P, BLK, D]) for z in range(2)]
        x1 = [sb(f"x1{z}", [P, BLK, D]) for z in range(2)]
        xres = [sb(f"xres{z}", [P, BLK, D]) for z in range(2)]
        outb = [sb(f"outb{z}", [P, BLK, D]) for z in range(2)]
        qT = [sb(f"qT{z}", [P, HEADS // 2, T]) for z in range(2)]
        kT = [sb(f"kT{z}", [P, HEADS // 2, WIN + T]) for z in range(2)]
        v_odd = [sb(f"v_odd{z}", [P, BLK, HEADS, DH + 1]) for z in range(2)]
        v_even = [sb(f"v_even{z}", [P, BLK, HEADS, DH + 1]) for z in range(2)]
        rnorm = [sb(f"rnorm{z}", [P, BLK, 2 * HEADS]) for z in range(2)]

        hT = sb("hT", [P, T])
        hn = sb("hn", [P, BLK, D])
        hnT = sb("hnT", [P, T])
        xb = sb("xb", [P, BLK, D])
        gates = sb("gates", [P, 2, T])
        uT = sb("uT", [P, CHUNKS, T])
        stats = sb("stats", [P, 2, BLK, 6])
        mv = sb("mv", [P, 2, BLK, 2])
        veps = sb("veps", [P, 2, BLK])
        rstd = sb("rstd", [P, 2, BLK])
        qk = sb("qk", [P, 2, 2 * INNER])
        sq = sb("sq", [P, 2 * INNER])
        ss = sb("ss", [P, 2 * HEADS])
        ssc = sb("ssc", [P, 2 * HEADS])
        rc = sb("rc", [P, 2 * INNER])
        rs = sb("rs", [P, 2 * INNER])
        rot = sb("rot", [P, 2, 2 * INNER])

        xn = sb("xn", [P, BLK, D])
        xnT = sb("xnT", [P, T])
        BT = sb("BT", [STATE, T])
        CT = sb("CT", [STATE, T])
        tok = sb("tok", [P, BLK, 1 + STATE])
        zb = sb("zb", [P, BLK])
        nz = sb("nz", [P, BLK])
        ez = sb("ez", [P, BLK])
        lz = sb("lz", [P, BLK])
        dts = sb("dts", [P, BLK])
        adt = sb("adt", [P, BLK])
        wdt = sb("wdt", [P, BLK])
        R = rc[:, 0:T].rearrange("p (m l) -> p m l", m=BLK)
        MT = rc[:, T:2 * T].rearrange("p (m l) -> p m l", m=BLK)
        E = rs[:, 0:T].rearrange("p (m l) -> p m l", m=BLK)
        et = sb("et", [P, 2 * BLK])
        Bd = sb("Bd", [P, BLK, STATE])
        St = sb("St", [STATE, BLK - 1, D])
        y = sb("y", [P, BLK, D])
        yn = hn

        nmx = sb("nmx", [P, 2, 4])
        nb = sb("nb", [P, 2, 4])
        probs = sb("probs", [P, 2, 4, P])
        probsT = sb("probsT", [P, 2, 4, P])
        rl = sb("rl", [P, 4])
        otok = sb("otok", [P, 2, INNER])
        oT = sb("oT", [P, INNER // P, P])

        pS = [ps(f"pS{i}", [P, 4, P]) for i in range(2)]
        pT = ps("pT", [P, 4, P])
        pO = ps("pO", [P, 512])
        pQK = ps("pQK", [P, 2, 512])
        pV = ps("pV", [P, 512])
        pM = ps("pM", [P, 512])

        def semaphore(name):
            return ctx.enter_context(nc.semaphore(name))

        s_bt_evac = semaphore("s_bt_evac")
        s_ct_evac = semaphore("s_ct_evac")
        s_decay = semaphore("s_decay")
        s_down = semaphore("s_down")
        s_dt_abs = semaphore("s_dt_abs")
        s_dt_log = semaphore("s_dt_log")
        s_exp = semaphore("s_exp")
        s_gate = semaphore("s_gate")
        s_gelu = semaphore("s_gelu")
        s_k_evac = semaphore("s_k_evac")
        s_k_scale = semaphore("s_k_scale")
        s_ln_affine = semaphore("s_ln_affine")
        s_ln_apply = semaphore("s_ln_apply")
        s_ln_rstd = semaphore("s_ln_rstd")
        s_ln_stats = semaphore("s_ln_stats")
        s_mt = semaphore("s_mt")
        s_o_evac = semaphore("s_o_evac")
        s_o_norm = semaphore("s_o_norm")
        s_p_evac = semaphore("s_p_evac")
        s_pv = semaphore("s_pv")
        s_q_evac = semaphore("s_q_evac")
        s_q_copy = semaphore("s_q_copy")
        s_k_copy = semaphore("s_k_copy")
        s_qk_square = semaphore("s_qk_square")
        s_qk_sum = semaphore("s_qk_sum")
        s_proj_q = semaphore("s_proj_q")
        s_proj_k = semaphore("s_proj_k")
        s_proj_v = semaphore("s_proj_v")
        s_resid = semaphore("s_resid")
        s_resid_bias = semaphore("s_resid_bias")
        s_rinv = semaphore("s_rinv")
        s_rope_add = semaphore("s_rope_add")
        s_rope_c = semaphore("s_rope_c")
        s_rope_s = semaphore("s_rope_s")
        s_scores = semaphore("s_scores")
        s_seg_exp = semaphore("s_seg_exp")
        s_shift_hi = semaphore("s_shift_hi")
        s_shift_lo = semaphore("s_shift_lo")
        s_smax = semaphore("s_smax")
        s_ssd_g = semaphore("s_ssd_g")
        s_ssd_off = semaphore("s_ssd_off")
        s_ssd_proj = semaphore("s_ssd_proj")
        s_ssd_seg = semaphore("s_ssd_seg")
        s_ssd_y = semaphore("s_ssd_y")
        s_tok_evac = semaphore("s_tok_evac")
        s_turn_h = semaphore("s_turn_h")
        s_turn_hn = semaphore("s_turn_hn")
        s_turn_k = semaphore("s_turn_k")
        s_turn_o = semaphore("s_turn_o")
        s_turn_p = semaphore("s_turn_p")
        s_turn_q = semaphore("s_turn_q")
        s_turn_x = semaphore("s_turn_x")
        s_turn_xn = semaphore("s_turn_xn")
        s_up = semaphore("s_up")
        s_v_evac = semaphore("s_v_evac")
        s_v_next = semaphore("s_v_next")
        s_v_shift = semaphore("s_v_shift")
        s_wo = semaphore("s_wo")
        s_wo_add = semaphore("s_wo_add")
        s_xn_evac = semaphore("s_xn_evac")
        s_y_off = semaphore("s_y_off")
        s_y_skip = semaphore("s_y_skip")
        s_section = semaphore("s_section")
        s_hold = semaphore("s_hold")
        s_weights = semaphore("s_weights")
        s_rows = semaphore("s_rows")
        s_setup = semaphore("s_setup")
        s_wx = semaphore("s_wx")
        s_scaled = semaphore("s_scaled")
        s_loaded = [semaphore(f"s_loaded{z}") for z in range(2)]
        s_stored = [semaphore(f"s_stored{z}") for z in range(2)]
        s_act_chain = semaphore("s_act_chain")
        s_dve_chain = semaphore("s_dve_chain")
        s_pool_chain = semaphore("s_pool_chain")

        class Count:

            def __init__(self, section, listed, order=None):
                self.section, self.listed, self.links = section, listed, 0
                self.order = range(len(listed)) if order is None else order
                self.first = isinstance(section, int) and section == 0

            def steps(self):
                for self.at in self.order:
                    name, z, layer, arg = self.listed[self.at]
                    yield name, z, layer, arg, sum(s[0] == name for s in self.listed[:self.at + 1])

            def nth(self, name, k):
                if self.first:
                    return max(k, 0)
                per_pass = sum(s[0] == name for s in PASS)
                return self.section * per_pass + (STRIDE - per_pass + k)

            def so_far(self, name):
                return self.nth(name, sum(s[0] == name for s in self.listed[:self.at]))

            def rest(self, name):
                return STRIDE - sum(s[0] == name for s in self.listed)

            def next_link(self):
                self.links += 1
                return self.section * CHAIN + self.links

        block = ctx.enter_context(nc.Block())

        @block.sync
        def _(sp):
            def load(z, seq):
                sp.dma_start(xin[z][:, :, :], x[seq].rearrange("(m p) d -> p m d", p=P)).then_inc(s_loaded[z], 16)

            load(0, 0)
            load(1, 1)
            for z in range(2):
                sp.sem_inc(s_stored[z], 16)
            sp.dma_start(cst[:, :], const[:, :]).then_inc(s_weights, 16)
            sp.dma_start(wx_rows[:, :], w_xproj[1:1 + P, :]).then_inc(s_weights, 16)
            sp.dma_start(wx_tok[:, 0:1], w_xproj[0:1, :].rearrange("a d -> d a")).then_inc(s_weights, 16)
            for n, src in enumerate((dt_bias, a_log, d_skip)):
                sp.dma_start(ssd_par[:, n:n + 1], src.partition_broadcast(P)).then_inc(s_weights, 16)
            for l in range(DEPTH):
                sp.dma_start(wqkv_s[:, l, :], wqkv[l]).then_inc(s_weights, 16)
                sp.dma_start(scales[:, l, 0, :], q_scale[l].partition_broadcast(P)).then_inc(s_weights, 16)
                sp.dma_start(scales[:, l, 1, :], k_scale[l].partition_broadcast(P)).then_inc(s_weights, 16)
                sp.dma_start(wo_s[:, l, :, :], wo[l].rearrange("(c p) n -> p c n", p=P)).then_inc(s_weights, 16)
                sp.dma_start(w1_s[:, l, :], w1[l]).then_inc(s_weights, 16)
                sp.dma_start(b2_s[:, l, :], b2[l].partition_broadcast(P)).then_inc(s_weights, 16)
                sp.dma_start(lng_s[:, l:l + 1], ln_g[l:l + 1, :].rearrange("a d -> d a")).then_inc(s_weights, 16)
                sp.dma_start(lnb_s[:, l:l + 1], ln_b[l:l + 1, :].rearrange("a d -> d a")).then_inc(s_weights, 16)
                for j, n in enumerate(SIZES):
                    sp.dma_start(w2_s[0:n, l, j, :], w2[l, P * j:P * j + n, :]).then_inc(s_weights, 16)
                    for half in range(2):
                        lo = half * HID + P * j
                        sp.dma_start(b1_s[0:n, l, half, j:j + 1],
                                     b1[l:l + 1, lo:lo + n].rearrange("a d -> d a")).then_inc(s_weights, 16)

            def section(count):
                for name, z, layer, arg, n in count.steps():
                    if name == "v_shift":
                        m = arg
                        sp.wait_ge(s_v_shift, 16 * count.nth("v_shift", n - 1))
                        sp.sem_inc(s_hold, 1)
                        sp.wait_ge(s_v_evac, count.nth("v_evac", n))
                        sp.dma_start(v_even[z][0:WIN, m, :, :], v_odd[z][0:WIN, m, :, :]).then_inc(s_v_shift, 16)
                    elif name == "v_next":
                        m = arg
                        sp.wait_ge(s_v_next, 16 * count.nth("v_next", n - 1))
                        sp.sem_inc(s_hold, 1)
                        sp.wait_ge(s_v_evac, count.so_far("v_evac"))
                        sp.dma_start(v_even[z][WIN:P, m + 1, :, :], v_odd[z][WIN:P, m, :, :]).then_inc(s_v_next, 16)
                    elif name == "load":
                        sp.wait_ge(s_ln_apply, count.so_far("ln_apply"))
                        sp.sem_inc(s_hold, 1)
                        if count.first:
                            load(0, 2)
                        else:
                            load(z, (2 * count.section + (2 if z == 0 else 1)) % SEQS)
                    elif name == "store":
                        sp.wait_ge(s_ln_apply, count.so_far("ln_apply"))
                        sp.sem_inc(s_hold, 1)
                        if isinstance(count.section, int):
                            seq = SEQS - 1
                        elif z == 0:
                            seq = 2 * (count.section - 1)
                        else:
                            seq = (2 * (count.section - 1) + (SEQS - 1)) % SEQS
                        sp.dma_start(out[seq].rearrange("(m p) d -> p m d", p=P),
                                            outb[z][:, :, :]).then_inc(s_stored[z], 16)
                if count.first:
                    sp.wait_ge(s_v_shift, 16 * count.so_far("v_shift"))
                    sp.sem_inc(s_hold, 1)
                    sp.wait_ge(s_v_next, 16 * count.so_far("v_next"))
                    sp.sem_inc(s_hold, 1)
                    sp.sem_inc(s_v_shift, 16 * count.rest("v_shift"))
                    sp.sem_inc(s_v_next, 16 * count.rest("v_next"))
                    sp.drain()
                    sp.drain().then_inc(s_section, 1)
                    sp.wait_ge(s_section, 5)
                    sp.sem_inc(s_hold, 1)

            section(Count(0, FIRST))
            with sp.Fori(0, PASSES) as i:
                section(Count(i + 1, PASS, ORDER))
            section(Count(PASSES + 1, LAST))
            sp.wait_ge(s_stored[0], 16 * (PASSES + 1))
            sp.wait_ge(s_stored[1], 16 * (PASSES + 2))
            sp.wait_ge(s_loaded[0], 16 * (PASSES + 2))
            sp.wait_ge(s_loaded[1], 16 * (PASSES + 1))

        N_WEIGHTS = 16 * (6 + DEPTH * (8 + 3 * CHUNKS))

        @block.tensor
        def _(pe):
            mm, turn = nc.tensor.matmul, nc.tensor.transpose

            def section(count):
                for name, z, layer, arg, n in count.steps():
                    if name == "turn_x":
                        pe.wait_ge(s_v_evac, count.so_far("v_evac"))
                        if arg == "mlp":
                            pe.wait_ge(s_wo_add, count.nth("wo_add", 4 * REST_PHASE[z, layer]))
                        pe.wait_ge(s_resid, count.so_far("resid"))
                        pe.wait_ge(s_ln_apply, count.so_far("ln_apply"))
                        for m in range(BLK):
                            last = turn(pV[:, m * P:(m + 1) * P], xres[z][:, m, :], ident)
                        last.then_inc(s_turn_x, 1)
                    elif name == "turn_h":
                        pe.wait_ge(s_shift_lo, count.so_far("shift_lo"))
                        pe.wait_ge(s_shift_hi, count.so_far("shift_hi"))
                        pe.wait_ge(s_q_copy, count.so_far("q_copy"))
                        for m in range(BLK):
                            last = turn(pQK[:, 0, m * P:(m + 1) * P], hT[:, m * P:(m + 1) * P], ident)
                        last.then_inc(s_turn_h, 1)
                    elif name == "turn_hn":
                        pe.wait_ge(s_ln_apply, count.so_far("ln_apply"))
                        pe.wait_ge(s_k_copy, count.so_far("k_copy"))
                        for m in range(BLK):
                            last = turn(pQK[:, 1, m * P:(m + 1) * P], hn[:, m, :], ident)
                        last.then_inc(s_turn_hn, 1)
                    elif name == "up":
                        j = arg
                        if j == 0:
                            pe.wait_ge(s_ln_affine, count.so_far("ln_affine"))
                        if j == 1:
                            pe.wait_ge(s_k_evac, count.so_far("k_evac"))
                        if j == 2:
                            pe.wait_ge(s_gate, count.nth("gate", n - 2))
                        a, g = (pV[:, :], pM[:, :]) if j == 1 else (pQK[:, 0, :], pQK[:, 1, :])
                        lo, size = P * j, SIZES[j]
                        mm(a[0:size], w1_s[:, layer, lo:lo + size], hnT[:, :], start=True, stop=True)
                        mm(g[0:size], w1_s[:, layer, HID + lo:HID + lo + size], hnT[:, :], start=True, stop=True).then_inc(s_up, 1)
                    elif name == "down":
                        pe.wait_ge(s_gate, count.so_far("gate"))
                        for m in range(BLK):
                            for j, size in enumerate(SIZES):
                                last = mm(pV[:, m * P:(m + 1) * P], uT[0:size, j, m * P:(m + 1) * P],
                                          w2_s[0:size, layer, j, :], start=j == 0, stop=j == CHUNKS - 1)
                        last.then_inc(s_down, 1)
                    elif name == "proj_q":
                        m = arg
                        pe.wait_ge(s_shift_lo, count.so_far("shift_lo"))
                        pe.wait_ge(s_shift_hi, count.so_far("shift_hi"))
                        pe.wait_ge(s_q_copy, count.so_far("q_copy"))
                        mm(pQK[:, 0, :], hT[:, m * P:(m + 1) * P], wqkv_s[:, layer, 0:INNER],
                           start=True, stop=True).then_inc(s_proj_q, 1)
                    elif name == "proj_k":
                        m = arg
                        pe.wait_ge(s_shift_lo, count.so_far("shift_lo"))
                        pe.wait_ge(s_shift_hi, count.so_far("shift_hi"))
                        pe.wait_ge(s_k_copy, count.so_far("k_copy"))
                        mm(pQK[:, 1, :], hT[:, m * P:(m + 1) * P], wqkv_s[:, layer, INNER:2 * INNER],
                           start=True, stop=True).then_inc(s_proj_k, 1)
                    elif name == "proj_v":
                        m = arg
                        pe.wait_ge(s_shift_lo, count.so_far("shift_lo"))
                        pe.wait_ge(s_shift_hi, count.so_far("shift_hi"))
                        pe.wait_ge(s_v_evac, count.so_far("v_evac"))
                        mm(pV[:, :], hT[:, m * P:(m + 1) * P], wqkv_s[:, layer, 2 * INNER:3 * INNER],
                           start=True, stop=True).then_inc(s_proj_v, 1)
                    elif name == "turn_q":
                        m = arg
                        pe.wait_ge(s_k_evac, count.so_far("k_evac"))
                        pe.wait_ge(s_rope_add, count.nth("rope_add", n))
                        for c in range(4):
                            last = turn(pM[:, c * P:(c + 1) * P], rot[:, n % 2, c * P:(c + 1) * P], ident)
                        last.then_inc(s_turn_q, 1)
                    elif name == "turn_k":
                        m = arg
                        pe.wait_ge(s_q_evac, count.nth("q_evac", n))
                        pe.wait_ge(s_k_scale, count.nth("k_scale", n))
                        for c in range(4):
                            last = turn(pM[:, c * P:(c + 1) * P], rot[:, n % 2, INNER + c * P:INNER + (c + 1) * P], ident)
                        last.then_inc(s_turn_k, 1)
                    elif name == "turn_xn":
                        pe.wait_ge(s_ln_apply, count.so_far("ln_apply"))
                        pe.wait_ge(s_gelu, count.so_far("gelu"))
                        for m in range(BLK):
                            last = turn(pM[:, m * P:(m + 1) * P], xn[:, m, :], ident)
                        last.then_inc(s_turn_xn, 1)
                    elif name == "ssd_proj":
                        pe.wait_ge(s_xn_evac, count.so_far("xn_evac"))
                        pe.wait_ge(s_gate, count.so_far("gate"))
                        mm(pQK[:, 0, :], wx_bc[:, :], xnT[:, :], start=True, stop=True)
                        for m in range(BLK):
                            last = mm(pQK[:, 1, m * (1 + STATE):(m + 1) * (1 + STATE)], xnT[:, m * P:(m + 1) * P],
                                      wx_tok[:, :], start=True, stop=True)
                        last.then_inc(s_ssd_proj, 1)
                    elif name == "ssd_g":
                        pe.wait_ge(s_bt_evac, count.so_far("bt_evac"))
                        pe.wait_ge(s_ct_evac, count.so_far("ct_evac"))
                        for m in range(BLK):
                            last = mm(pQK[:, 0, m * P:(m + 1) * P], BT[:, m * P:(m + 1) * P], CT[:, m * P:(m + 1) * P],
                                      start=True, stop=True)
                        last.then_inc(s_ssd_g, 1)
                    elif name == "ssd_seg":
                        pe.wait_ge(s_decay, count.so_far("decay"))
                        pe.wait_ge(s_resid, count.so_far("resid"))
                        mm(pV[:, :], ident_h[:, :], masks_h[:, 0:1, :].to_broadcast([P, BLK, P]), start=True, stop=False)
                        mm(pV[:, :], later, R[:, :, :], start=False, stop=True)
                        mm(pM[:, 0:BLK], upto, adt[:, :], start=True, stop=True)
                        mm(pM[:, BLK:2 * BLK], ones[:, :], adt[:, :], start=True, stop=True).then_inc(s_ssd_seg, 1)
                    elif name == "ssd_y":
                        pe.wait_ge(s_mt, count.so_far("mt"))
                        for m in range(BLK):
                            mm(pM[:, m * P:(m + 1) * P], MT[:, m, :], xn[:, m, :], start=True, stop=True)
                        for m in range(BLK - 1):
                            last = mm(pQK[0:STATE, 1, m * P:(m + 1) * P], Bd[:, m, :], xn[:, m, :], start=True, stop=True)
                        last.then_inc(s_ssd_y, 1)
                    elif name == "ssd_off":
                        pe.wait_ge(s_y_skip, count.so_far("y_skip"))
                        for m in range(1, BLK):
                            last = mm(pV[:, m * P:(m + 1) * P], CT[:, m * P:(m + 1) * P], St[:, m - 1, :],
                                      start=True, stop=True)
                        last.then_inc(s_ssd_off, 1)
                    elif name == "scores":
                        mg = arg
                        m, g = mg
                        before = 4 * (PHASE[z, layer] - 1)
                        pe.wait_ge(s_k_evac, count.nth("k_evac", before + m + 1))
                        pe.wait_ge(s_exp, count.nth("exp", n - 2))
                        bank = pS[n % 2]
                        mask = masks_h[:, 1:2, :] if m == 0 else masks_h[:, 2:3, :]
                        mm(bank[:, :, :], ident_h[:, :], mask.to_broadcast([P, 4, P]), start=True, stop=False,
                           skip_group_check=True)
                        for h in range(4):
                            c, r = h, DH * g
                            lo = m * P
                            q = qT[z][r:r + DH, c, lo:lo + P]
                            keys = kT[z][r:r + DH, c, lo:lo + WIN + P]
                            own_prev = keys[:, 0:2 * WIN].rearrange("p (a b) -> p a b", a=2)[:, ::-1, :]
                            mm(bank[0:WIN, h, :], q[:, 0:WIN], own_prev, start=False, stop=h == 3, skip_group_check=True)
                            last = mm(bank[WIN:P, h, :], q[:, WIN:P], keys[:, WIN:WIN + P], start=False, stop=h == 3,
                                      skip_group_check=True)
                        last.then_inc(s_scores, 1)
                    elif name == "turn_p":
                        mg = arg
                        pe.wait_ge(s_exp, count.nth("exp", n))
                        pe.wait_ge(s_p_evac, count.so_far("p_evac"))
                        pe.wait_ge(s_o_evac, count.so_far("o_evac"))
                        for h in range(4):
                            last = turn(pT[:, h, :], probs[:, n % 2, h, :], ident)
                        last.then_inc(s_turn_p, 1)
                    elif name == "pv":
                        mg = arg
                        m, g = mg
                        before = PHASE[z, layer] - 1
                        pe.wait_ge(s_v_shift, 16 * count.nth("v_shift", 4 * before + m + 1))
                        pe.wait_ge(s_v_next, 16 * count.nth("v_next", 3 * before + m))
                        pe.wait_ge(s_p_evac, count.nth("p_evac", n))
                        pe.wait_ge(s_o_norm, count.so_far("o_norm"))
                        pe.wait_ge(s_wo_add, count.so_far("wo_add"))
                        for h in range(4):
                            for row, values in ((0, v_even[z]), (WIN, v_odd[z])):
                                last = mm(pO[row:row + WIN, h * (DH + 1):(h + 1) * (DH + 1)],
                                          probsT[:, n % 2, h, row:row + WIN], values[:, m, 2 * h + g, :],
                                          start=True, stop=True)
                        last.then_inc(s_pv, 1)
                    elif name == "turn_o":
                        mg = arg
                        pe.wait_ge(s_o_norm, count.so_far("o_norm"))
                        for c in range(4):
                            last = turn(pT[:, c, :], otok[:, mg[0] % 2, c * P:(c + 1) * P], ident)
                        last.then_inc(s_turn_o, 1)
                    elif name == "wo":
                        mg = arg
                        pe.wait_ge(s_o_evac, count.so_far("o_evac"))
                        for c in range(4):
                            last = mm(pO[:, 0:D], oT[:, c, :], wo_s[:, layer, c, :], start=c == 0, stop=c == 3)
                        last.then_inc(s_wo, 1)
                if count.first:
                    pe.drain()
                    pe.sem_inc(s_turn_x, count.rest("turn_x"))
                    pe.sem_inc(s_turn_h, count.rest("turn_h"))
                    pe.sem_inc(s_turn_hn, count.rest("turn_hn"))
                    pe.sem_inc(s_up, count.rest("up"))
                    pe.sem_inc(s_down, count.rest("down"))
                    pe.sem_inc(s_proj_q, count.rest("proj_q"))
                    pe.sem_inc(s_proj_k, count.rest("proj_k"))
                    pe.sem_inc(s_proj_v, count.rest("proj_v"))
                    pe.sem_inc(s_turn_q, count.rest("turn_q"))
                    pe.sem_inc(s_turn_k, count.rest("turn_k"))
                    pe.sem_inc(s_turn_xn, count.rest("turn_xn"))
                    pe.sem_inc(s_ssd_proj, count.rest("ssd_proj"))
                    pe.sem_inc(s_ssd_g, count.rest("ssd_g"))
                    pe.sem_inc(s_ssd_seg, count.rest("ssd_seg"))
                    pe.sem_inc(s_ssd_y, count.rest("ssd_y"))
                    pe.sem_inc(s_ssd_off, count.rest("ssd_off"))
                    pe.sem_inc(s_scores, count.rest("scores"))
                    pe.sem_inc(s_turn_p, count.rest("turn_p"))
                    pe.sem_inc(s_pv, count.rest("pv"))
                    pe.sem_inc(s_turn_o, count.rest("turn_o"))
                    pe.sem_inc(s_wo, count.rest("wo"))
                    pe.drain().then_inc(s_section, 1)
                    pe.wait_ge(s_section, 5)
                    pe.sem_inc(s_hold, 1)

            pe.wait_ge(s_weights, N_WEIGHTS)
            pe.wait_ge(s_setup, 2)
            turn(pM[:, 0:P], wx_rows[:, :], ident).then_inc(s_wx, 1)
            pe.wait_ge(s_wx, 2)
            section(Count(0, FIRST))
            with pe.Fori(0, PASSES) as i:
                section(Count(i + 1, PASS, ORDER))
            section(Count(PASSES + 1, LAST))

        @block.scalar
        def _(act):
            activation = nc.scalar.activation

            def copy(out, in_):
                return activation(out, in_, ACT.Copy)

            def section(count):
                def link(ins):
                    ins.then_inc(s_act_chain, 1)
                    act.wait_ge(s_act_chain, count.next_link())

                for name, z, layer, arg, n in count.steps():
                    if name == "shift_lo":
                        act.wait_ge(s_turn_x, count.so_far("turn_x"))
                        act.wait_ge(s_proj_q, count.so_far("proj_q"))
                        act.wait_ge(s_proj_k, count.so_far("proj_k"))
                        copy(hT[0:D // 2, :], pV[0:D // 2, :]).then_inc(s_shift_lo, 1)
                    elif name == "ln_affine":
                        act.wait_ge(s_turn_hn, count.so_far("turn_hn"))
                        activation(hnT[:, :], pQK[:, 1, :], ACT.Identity, bias=lnb_s[:, layer:layer + 1],
                                          scale=lng_s[:, layer:layer + 1]).then_inc(s_ln_affine, 1)
                    elif name == "gelu":
                        j = arg
                        act.wait_ge(s_up, count.nth("up", n))
                        src = pM[:, :] if j == 1 else pQK[:, 1, :]
                        size = SIZES[j]
                        activation(gates[0:size, n % 2, :], src[0:size], ACT.Gelu, bias=b1_s[0:size, layer, 1, j:j + 1]).then_inc(s_gelu, 1)
                    elif name == "q_copy":
                        act.wait_ge(s_proj_q, count.nth("proj_q", n))
                        act.wait_ge(s_rope_s, count.nth("rope_s", n - 2))
                        act.wait_ge(s_rope_c, count.nth("rope_c", n - 2))
                        act.wait_ge(s_qk_square, count.nth("qk_square", n - 2))
                        copy(qk[:, n % 2, 0:INNER], pQK[:, 0, :]).then_inc(s_q_copy, 1)
                    elif name == "k_copy":
                        act.wait_ge(s_proj_k, count.nth("proj_k", n))
                        act.wait_ge(s_rope_s, count.nth("rope_s", n - 2))
                        act.wait_ge(s_rope_c, count.nth("rope_c", n - 2))
                        act.wait_ge(s_qk_square, count.nth("qk_square", n - 2))
                        copy(qk[:, n % 2, INNER:2 * INNER], pQK[:, 1, :]).then_inc(s_k_copy, 1)
                    elif name == "qk_square":
                        act.wait_ge(s_q_copy, count.nth("q_copy", n))
                        act.wait_ge(s_k_copy, count.nth("k_copy", n))
                        act.wait_ge(s_qk_sum, count.nth("qk_sum", n - 1))
                        activation(sq[:, :], qk[:, n % 2, :], ACT.Square).then_inc(s_qk_square, 1)
                    elif name == "q_evac":
                        m = arg
                        act.wait_ge(s_turn_q, count.nth("turn_q", n))
                        copy(qT[z][:, :, m * P:(m + 1) * P], pM[:, :].rearrange("p (c t) -> p c t", c=4)).then_inc(s_q_evac, 1)
                    elif name == "k_evac":
                        m = arg
                        act.wait_ge(s_turn_k, count.nth("turn_k", n))
                        copy(kT[z][:, :, WIN + m * P:WIN + (m + 1) * P],
                             pM[:, :].rearrange("p (c t) -> p c t", c=4)).then_inc(s_k_evac, 1)
                    elif name == "v_evac":
                        m = arg
                        act.wait_ge(s_proj_v, count.nth("proj_v", n))
                        copy(v_odd[z][:, m, :, 0:DH],
                             pV[:, :].rearrange("p (h d) -> p h d", h=HEADS)).then_inc(s_v_evac, 1)
                    elif name == "xn_evac":
                        act.wait_ge(s_turn_xn, count.so_far("turn_xn"))
                        copy(xnT[:, :], pM[:, :]).then_inc(s_xn_evac, 1)
                    elif name == "bt_evac":
                        act.wait_ge(s_ssd_proj, count.so_far("ssd_proj"))
                        copy(BT[:, :], pQK[0:STATE, 0, :]).then_inc(s_bt_evac, 1)
                    elif name == "tok_evac":
                        act.wait_ge(s_ssd_proj, count.so_far("ssd_proj"))
                        copy(tok[:, :, :], pQK[:, 1, 0:BLK * (1 + STATE)].rearrange("p (m f) -> p m f", m=BLK)).then_inc(s_tok_evac, 1)
                    elif name == "dt_log":
                        act.wait_ge(s_dt_abs, count.so_far("dt_abs"))
                        link(activation(ez[:, :], nz[:, :], ACT.Exp))
                        activation(lz[:, :], ez[:, :], ACT.Ln, bias=1.0).then_inc(s_dt_log, 1)
                    elif name == "seg_exp":
                        act.wait_ge(s_ssd_seg, count.so_far("ssd_seg"))
                        activation(E[:, :, :], pV[:, :].rearrange("p (m l) -> p m l", m=BLK), ACT.Exp)
                        activation(et[:, :], pM[:, 0:2 * BLK], ACT.Exp).then_inc(s_seg_exp, 1)
                    elif name == "exp":
                        mg = arg
                        m, g = mg
                        act.wait_ge(s_smax, count.nth("smax", n))
                        act.wait_ge(s_turn_p, count.nth("turn_p", n - 2))
                        for h in range(4):
                            last = activation(probs[:, n % 2, h, :], pS[n % 2][:, h, :], ACT.Exp,
                                              bias=nb[:, n % 2, h:h + 1], scale=rnorm[z][:, m, 2 * h + g:2 * h + g + 1])
                        last.then_inc(s_exp, 1)
                    elif name == "p_evac":
                        mg = arg
                        act.wait_ge(s_turn_p, count.nth("turn_p", n))
                        copy(probsT[:, n % 2, :, :], pT[:, :, :]).then_inc(s_p_evac, 1)
                    elif name == "o_evac":
                        mg = arg
                        act.wait_ge(s_turn_o, count.nth("turn_o", n))
                        copy(oT[:, :, :], pT[:, :, :]).then_inc(s_o_evac, 1)
                act.sem_inc(s_act_chain, CHAIN - count.links)
                if count.first:
                    act.drain()
                    act.sem_inc(s_shift_lo, count.rest("shift_lo"))
                    act.sem_inc(s_ln_affine, count.rest("ln_affine"))
                    act.sem_inc(s_gelu, count.rest("gelu"))
                    act.sem_inc(s_q_copy, count.rest("q_copy"))
                    act.sem_inc(s_k_copy, count.rest("k_copy"))
                    act.sem_inc(s_qk_square, count.rest("qk_square"))
                    act.sem_inc(s_q_evac, count.rest("q_evac"))
                    act.sem_inc(s_k_evac, count.rest("k_evac"))
                    act.sem_inc(s_v_evac, count.rest("v_evac"))
                    act.sem_inc(s_xn_evac, count.rest("xn_evac"))
                    act.sem_inc(s_bt_evac, count.rest("bt_evac"))
                    act.sem_inc(s_tok_evac, count.rest("tok_evac"))
                    act.sem_inc(s_dt_log, count.rest("dt_log"))
                    act.sem_inc(s_seg_exp, count.rest("seg_exp"))
                    act.sem_inc(s_exp, count.rest("exp"))
                    act.sem_inc(s_p_evac, count.rest("p_evac"))
                    act.sem_inc(s_o_evac, count.rest("o_evac"))
                    act.drain().then_inc(s_section, 1)
                    act.wait_ge(s_section, 5)
                    act.sem_inc(s_hold, 1)

            act.wait_ge(s_weights, N_WEIGHTS)
            activation(ssd_par[:, 3:4], ssd_par[:, 1:2], ACT.Exp).then_inc(s_rows, 1)
            section(Count(0, FIRST))
            with act.Fori(0, PASSES) as i:
                section(Count(i + 1, PASS, ORDER))
            section(Count(PASSES + 1, LAST))

        @block.vector
        def _(dve):
            v = nc.vector

            def section(count):
                def link(ins):
                    ins.then_inc(s_dve_chain, 1)
                    dve.wait_ge(s_dve_chain, count.next_link())

                def halves(a):
                    return a.rearrange("p (a h f) -> p a h f", a=2, h=HEADS)
                for name, z, layer, arg, n in count.steps():
                    if name == "shift_hi":
                        dve.wait_ge(s_turn_x, count.so_far("turn_x"))
                        dve.wait_ge(s_proj_q, count.so_far("proj_q"))
                        dve.wait_ge(s_proj_k, count.so_far("proj_k"))
                        v.tensor_copy(hT[D // 2:D, 1:T], pV[D // 2:D, 0:T - 1]).then_inc(s_shift_hi, 1)
                    elif name == "ln_stats":
                        kind = arg
                        if kind == "x":
                            dve.wait_ge(s_loaded[z], (count.section + (1 if z == 0 else 0)) * 16)
                        if kind == "h":
                            dve.wait_ge(s_turn_h, count.so_far("turn_h"))
                        if kind == "y":
                            dve.wait_ge(s_y_off, count.so_far("y_off"))
                        if kind == "1":
                            dve.wait_ge(s_ln_apply, count.so_far("ln_apply"))
                        if kind == "o":
                            dve.wait_ge(s_resid, count.so_far("resid"))
                        src = {"h": pQK[:, 0, :].rearrange("p (m d) -> p m d", m=BLK), "x": xin[z], "y": y, "1": x1[z],
                               "o": xres[z]}[kind]
                        for m in range(BLK):
                            ins = v.bn_stats(stats[:, n % 2, m, :], src[:, m, :])
                        link(ins)
                        dve.sem_inc(s_hold, 1)
                        for m in range(BLK):
                            last = v.bn_aggr(mv[:, n % 2, m, :], stats[:, n % 2, m, :])
                        last.then_inc(s_ln_stats, 1)
                    elif name == "ln_apply":
                        kind = arg
                        dve.wait_ge(s_ln_rstd, count.nth("ln_rstd", n))
                        if kind in ("h", "y", "o"):
                            dve.wait_ge(s_ln_apply, count.nth("ln_apply", n - 1))
                        src = {"h": pQK[:, 0, :].rearrange("p (m d) -> p m d", m=BLK), "x": xin[z], "y": y, "1": x1[z],
                               "o": xres[z]}[kind]
                        dst = {"h": hn, "x": xn, "y": yn, "1": xres[z], "o": yn}[kind]
                        if kind == "o":
                            dve.wait_ge(s_stored[z], count.section * 16)
                        for m in range(BLK):
                            last = v.tensor_scalar(dst[:, m, :], src[:, m, :], mv[:, n % 2, m, 0:1], rstd[:, n % 2, m:m + 1],
                                                   ALU.subtract, ALU.mult)
                        if kind == "y":
                            link(last)
                            last = v.tensor_tensor(x1[z][:, :, :], xin[z][:, :, :], yn[:, :, :], ALU.add)
                        if kind == "o":
                            link(last)
                            last = v.tensor_tensor(outb[z][:, :, :], x1[z][:, :, :], yn[:, :, :], ALU.add)
                        last.then_inc(s_ln_apply, 1)
                    elif name == "gate":
                        j = arg
                        dve.wait_ge(s_gelu, count.nth("gelu", n))
                        src = pV[:, :] if j == 1 else pQK[:, 0, :]
                        size = SIZES[j]
                        v.scalar_tensor_tensor(uT[0:size, j, :], src[0:size], b1_s[0:size, layer, 0, j:j + 1],
                                                      gates[0:size, n % 2, :], ALU.add, ALU.mult).then_inc(s_gate, 1)
                    elif name == "resid":
                        dve.wait_ge(s_down, count.so_far("down"))
                        dve.wait_ge(s_resid_bias, count.so_far("resid_bias"))
                        v.tensor_tensor(xres[z][:, :, :], pV[:, :].rearrange("p (m d) -> p m d", m=BLK),
                                               xb[:, :, :], ALU.add).then_inc(s_resid, 1)
                    elif name == "rope_s":
                        m = arg
                        dve.wait_ge(s_q_copy, count.nth("q_copy", n))
                        dve.wait_ge(s_k_copy, count.nth("k_copy", n))
                        dve.wait_ge(s_rope_add, count.nth("rope_add", n - 1))
                        q, o, hf = halves(qk[:, n % 2, :]), halves(rs[:, :]), DH // 2
                        for a, b in ((0, hf), (hf, 0)):
                            table = tab_s[:, layer, m, :, a:a + hf].unsqueeze(2).to_broadcast([P, 2, HEADS, hf])
                            last = v.tensor_tensor(o[:, :, :, a:a + hf], q[:, :, :, b:b + hf], table, ALU.mult)
                        last.then_inc(s_rope_s, 1)
                    elif name == "qk_sum":
                        m = arg
                        dve.wait_ge(s_qk_square, count.nth("qk_square", n))
                        dve.wait_ge(s_rinv, count.nth("rinv", n - 1))
                        v.tensor_reduce(ss[:, :], sq[:, :].rearrange("p (h d) -> p h d", d=DH), AX.X, ALU.add).then_inc(s_qk_sum, 1)
                    elif name == "rope_add":
                        m = arg
                        dve.wait_ge(s_rope_c, count.nth("rope_c", n))
                        dve.wait_ge(s_rope_s, count.nth("rope_s", n))
                        dve.wait_ge(s_turn_k, count.nth("turn_k", n - 2))
                        v.tensor_tensor(rot[:, n % 2, :], rc[:, :], rs[:, :], ALU.add).then_inc(s_rope_add, 1)
                    elif name == "ct_evac":
                        dve.wait_ge(s_ssd_proj, count.so_far("ssd_proj"))
                        v.tensor_copy(CT[:, :], pQK[STATE:P, 0, :]).then_inc(s_ct_evac, 1)
                    elif name == "dt_abs":
                        dve.wait_ge(s_tok_evac, count.so_far("tok_evac"))
                        link(v.tensor_scalar(zb[:, :], tok[:, :, 0], ssd_par[:, 0:1], None, ALU.add))
                        v.scalar_tensor_tensor(nz[:, :], zb[:, :], -1.0, zb[:, :], ALU.mult, ALU.min).then_inc(s_dt_abs, 1)
                    elif name == "decay":
                        dve.wait_ge(s_dt_log, count.so_far("dt_log"))
                        link(v.scalar_tensor_tensor(dts[:, :], zb[:, :], 0.0, lz[:, :], ALU.max, ALU.add))
                        link(v.tensor_scalar(adt[:, :], dts[:, :], ssd_par[:, 3:4], None, ALU.mult))
                        v.tensor_tensor(R[:, :, :], upto.unsqueeze(1).to_broadcast([P, BLK, P]),
                                               adt[:, :].unsqueeze(2).to_broadcast([P, BLK, P]), ALU.mult).then_inc(s_decay, 1)
                    elif name == "mt":
                        dve.wait_ge(s_ssd_g, count.so_far("ssd_g"))
                        dve.wait_ge(s_seg_exp, count.so_far("seg_exp"))
                        link(v.tensor_tensor(wdt[:, :], dts[:, :], E[:, :, P - 1], ALU.mult))
                        v.tensor_tensor(Bd[:, :, :], tok[:, :, 1:1 + STATE],
                                        wdt[:, :].unsqueeze(2).to_broadcast([P, BLK, STATE]), ALU.mult)
                        for m in range(BLK):
                            last = v.scalar_tensor_tensor(MT[:, m, :], pQK[:, 0, m * P:(m + 1) * P], dts[:, m:m + 1],
                                                          E[:, m, :], ALU.mult, ALU.mult)
                        last.then_inc(s_mt, 1)
                    elif name == "y_skip":
                        dve.wait_ge(s_ssd_y, count.so_far("ssd_y"))
                        v.scalar_tensor_tensor(y[:, :, :], xn[:, :, :], ssd_par[:, 2:3],
                                               pM[:, :].rearrange("p (m d) -> p m d", m=BLK), ALU.mult, ALU.add)
                        last = v.tensor_copy(St[:, 0, :], pQK[0:STATE, 1, 0:D])
                        for m in range(1, BLK - 1):
                            link(last)
                            last = v.scalar_tensor_tensor(St[:, m, :], St[:, m - 1, :], et[0:STATE, BLK + m:BLK + m + 1],
                                                          pQK[0:STATE, 1, m * D:(m + 1) * D], ALU.mult, ALU.add)
                        last.then_inc(s_y_skip, 1)
                    elif name == "y_off":
                        dve.wait_ge(s_ssd_off, count.so_far("ssd_off"))
                        for m in range(1, BLK):
                            last = v.scalar_tensor_tensor(y[:, m, :], pV[:, m * D:(m + 1) * D], et[:, m:m + 1], y[:, m, :],
                                                          ALU.mult, ALU.add)
                        last.then_inc(s_y_off, 1)
                    elif name == "smax":
                        mg = arg
                        m, g = mg
                        dve.wait_ge(s_scores, count.nth("scores", n))
                        link(v.tensor_reduce(nmx[:, n % 2, :], pS[n % 2][:, :, :], AX.X, ALU.max, negate=True))
                        v.tensor_tensor(nb[:, n % 2, :], nmx[:, n % 2, :], rnorm[z][:, m, g:HEADS:2], ALU.mult).then_inc(s_smax, 1)
                    elif name == "o_norm":
                        mg = arg
                        m, g = mg
                        dve.wait_ge(s_pv, count.nth("pv", n))
                        o = pO[:, 0:4 * (DH + 1)].rearrange("p (h d) -> p h d", h=4)
                        link(v.reciprocal(rl[:, :], o[:, :, DH]))
                        dst = otok[:, m % 2, :].rearrange("p (h a d) -> p a h d", h=4, a=2)[:, g, :, :]
                        v.tensor_tensor(dst, o[:, :, 0:DH], rl[:, :].unsqueeze(2).to_broadcast([P, 4, DH]), ALU.mult).then_inc(s_o_norm, 1)
                    elif name == "wo_add":
                        mg = arg
                        m = mg[0]
                        dve.wait_ge(s_wo, count.so_far("wo"))
                        v.tensor_tensor(xres[z][:, m, :], xres[z][:, m, :], pO[:, 0:D], ALU.add).then_inc(s_wo_add, 1)
                dve.sem_inc(s_dve_chain, CHAIN - count.links)
                if count.first:
                    dve.drain()
                    dve.sem_inc(s_shift_hi, count.rest("shift_hi"))
                    dve.sem_inc(s_ln_stats, count.rest("ln_stats"))
                    dve.sem_inc(s_ln_apply, count.rest("ln_apply"))
                    dve.sem_inc(s_gate, count.rest("gate"))
                    dve.sem_inc(s_resid, count.rest("resid"))
                    dve.sem_inc(s_rope_s, count.rest("rope_s"))
                    dve.sem_inc(s_qk_sum, count.rest("qk_sum"))
                    dve.sem_inc(s_rope_add, count.rest("rope_add"))
                    dve.sem_inc(s_ct_evac, count.rest("ct_evac"))
                    dve.sem_inc(s_dt_abs, count.rest("dt_abs"))
                    dve.sem_inc(s_decay, count.rest("decay"))
                    dve.sem_inc(s_mt, count.rest("mt"))
                    dve.sem_inc(s_y_skip, count.rest("y_skip"))
                    dve.sem_inc(s_y_off, count.rest("y_off"))
                    dve.sem_inc(s_smax, count.rest("smax"))
                    dve.sem_inc(s_o_norm, count.rest("o_norm"))
                    dve.sem_inc(s_wo_add, count.rest("wo_add"))
                    dve.drain().then_inc(s_section, 1)
                    dve.wait_ge(s_section, 5)
                    dve.sem_inc(s_hold, 1)

            for z in range(2):
                v.memset(kT[z][:, :, 0:WIN], 0.0)
                v.memset(v_odd[z][:, :, :, DH:DH + 1], 1.0)
                v.memset(v_even[z][:, :, :, DH:DH + 1], 1.0)
                v.memset(v_even[z][WIN:P, 0, :, 0:DH], 0.0)
                v.memset(xres[z][:, :, :], 0.0)
                v.memset(x1[z][:, :, :], 0.0)
            v.memset(hT[D // 2:D, 0:1], 0.0)
            v.memset(ones[:, :], 1.0)
            v.memset(minus_half[:, :], -0.5).then_inc(s_setup, 1)
            dve.wait_ge(s_weights, N_WEIGHTS)
            v.tensor_copy(ident_h[:, :], ident)
            v.tensor_copy(masks_h[:, :, :], cst[:, 3 * P:6 * P].rearrange("p (k j) -> p k j", k=3))
            hf = DH // 2
            v.tensor_scalar(scales[:, :, 0, :], scales[:, :, 0, :], QK_SCALE, None, ALU.mult).then_inc(s_scaled, 1)
            dve.wait_ge(s_scaled, 1)
            for l in range(DEPTH):
                wide = [P, BLK, 2, DH]
                v.tensor_tensor(tab_c[:, l, :, :, :], rope_cos, scales[:, l, :, :].unsqueeze(1).to_broadcast(wide), ALU.mult)
                for a, b in ((0, hf), (hf, 0)):
                    last = v.tensor_tensor(tab_s[:, l, :, :, a:a + hf], rope_sin[:, :, :, a:a + hf],
                                           scales[:, l, :, b:b + hf].unsqueeze(1).to_broadcast([P, BLK, 2, hf]), ALU.mult)
            dve.wait_ge(s_rows, 1)
            v.tensor_scalar(ssd_par[:, 3:4], ssd_par[:, 3:4], -1.0, None, ALU.mult).then_inc(s_setup, 1)
            dve.wait_ge(s_wx, 1)
            v.tensor_copy(wx_bc[:, :], pM[:, 0:P])
            v.tensor_copy(wx_tok[:, 1:1 + STATE], pM[:, 0:STATE]).then_inc(s_wx, 1)
            dve.wait_ge(s_wx, 2)
            section(Count(0, FIRST))
            with dve.Fori(0, PASSES) as i:
                section(Count(i + 1, PASS, ORDER))
            section(Count(PASSES + 1, LAST))

        @block.gpsimd
        def _(pool):
            g = nc.gpsimd

            def section(count):
                def link(ins):
                    ins.then_inc(s_pool_chain, 1)
                    pool.wait_ge(s_pool_chain, count.next_link())

                for name, z, layer, arg, n in count.steps():
                    if name == "ln_rstd":
                        kind = arg
                        pool.wait_ge(s_ln_stats, count.nth("ln_stats", n))
                        pool.sem_inc(s_hold, 1)
                        link(g.tensor_scalar(veps[:, n % 2, :], mv[:, n % 2, :, 1], LN_EPS, None, ALU.add))
                        g.tensor_tensor(rstd[:, n % 2, :], veps[:, n % 2, :], minus_half[:, 0:BLK], ALU.pow).then_inc(s_ln_rstd, 1)
                    elif name == "resid_bias":
                        pool.wait_ge(s_wo_add, count.nth("wo_add", 4 * REST_PHASE[z, layer]))
                        pool.wait_ge(s_resid, count.so_far("resid"))
                        g.tensor_tensor(xb[:, :, :], xres[z][:, :, :],
                                               b2_s[:, layer, :].unsqueeze(1).to_broadcast([P, BLK, D]), ALU.add).then_inc(s_resid_bias, 1)
                    elif name == "rope_c":
                        m = arg
                        pool.wait_ge(s_q_copy, count.nth("q_copy", n))
                        pool.wait_ge(s_k_copy, count.nth("k_copy", n))
                        pool.wait_ge(s_rope_add, count.nth("rope_add", n - 1))
                        for a in range(2):
                            q = qk[:, n % 2, a * INNER:(a + 1) * INNER].rearrange("p (h f) -> p h f", h=HEADS)
                            o = rc[:, a * INNER:(a + 1) * INNER].rearrange("p (h f) -> p h f", h=HEADS)
                            table = tab_c[:, layer, m, a, :].unsqueeze(1).to_broadcast([P, HEADS, DH])
                            last = g.tensor_tensor(o, q, table, ALU.mult)
                        last.then_inc(s_rope_c, 1)
                    elif name == "rinv":
                        m = arg
                        pool.wait_ge(s_qk_sum, count.nth("qk_sum", n))
                        pool.sem_inc(s_hold, 1)
                        link(g.tensor_scalar(ssc[:, :], ss[:, :], 1e-24, None, ALU.max))
                        g.tensor_tensor(rnorm[z][:, m, :], ssc[:, :], minus_half[:, :], ALU.pow).then_inc(s_rinv, 1)
                    elif name == "k_scale":
                        m = arg
                        pool.wait_ge(s_rope_add, count.nth("rope_add", n))
                        pool.wait_ge(s_rinv, count.nth("rinv", n))
                        k = rot[:, n % 2, INNER:2 * INNER].rearrange("p (h f) -> p h f", h=HEADS)
                        g.tensor_tensor(k, k, rnorm[z][:, arg, HEADS:2 * HEADS].unsqueeze(2).to_broadcast([P, HEADS, DH]),
                                               ALU.mult).then_inc(s_k_scale, 1)
                pool.sem_inc(s_pool_chain, CHAIN - count.links)
                if count.first:
                    pool.drain()
                    pool.sem_inc(s_ln_rstd, count.rest("ln_rstd"))
                    pool.sem_inc(s_resid_bias, count.rest("resid_bias"))
                    pool.sem_inc(s_rope_c, count.rest("rope_c"))
                    pool.sem_inc(s_rinv, count.rest("rinv"))
                    pool.sem_inc(s_k_scale, count.rest("k_scale"))
                    pool.drain().then_inc(s_section, 1)
                    pool.wait_ge(s_section, 5)
                    pool.sem_inc(s_hold, 1)

            pool.wait_ge(s_setup, 2)
            section(Count(0, FIRST))
            with pool.Fori(0, PASSES) as i:
                section(Count(i + 1, PASS, ORDER))
            section(Count(PASSES + 1, LAST))


_INS = ['L0_attn_x', 'L0_attn_W_xproj', 'L0_attn_dt_bias', 'L0_attn_A_log', 'L0_attn_D', 'L0_ffn_wqkv',
        'L0_ffn_q_scale', 'L0_ffn_k_scale', 'L0_ffn_wo', 'L0_ffn_ln_g', 'L0_ffn_ln_b', 'L0_ffn_w1', 'L0_ffn_b1',
        'L0_ffn_w2', 'L0_ffn_b2']


def kernel(**inputs):
    import concourse.bacc as _bacc
    from concourse.bass_utils import run_bass_kernel_spmd as _run

    nc = _bacc.Bacc("TRN2", target_bir_lowering=False, num_devices=1)
    arrays, args = {}, []
    for name in _INS:
        a = np.ascontiguousarray(inputs[name])
        arrays[f"in_{name}_dram"] = a
        args.append(nc.dram_tensor(f"in_{name}_dram", a.shape, F32, kind="ExternalInput").ap())
    shape = inputs['L0_attn_x'].shape
    const = shape_constants(shape[1])
    arrays["const_dram"] = const
    args.append(nc.dram_tensor("const_dram", const.shape, F32, kind="ExternalInput").ap())
    args.append(nc.dram_tensor("out_0_dram", shape, F32, kind="ExternalOutput").ap())
    build(nc, *args)
    r = _run(nc, [arrays], core_ids=[0])
    return r.results[0]["out_0_dram"]
```

```python
from contextlib import ExitStack

import numpy as np
import concourse.bass as bass
from concourse import mybir

F32 = mybir.dt.float32
BF16 = mybir.dt.bfloat16
ALU = mybir.AluOpType
ACT = mybir.ActivationFunctionType
AX = mybir.AxisListType

P = 128
D = 128
STATE = 64
HEADS, DH, WIN = 8, 64, 64
INNER = HEADS * DH
QK_SCALE = 8.0
NEG = -1.0e30
LN_EPS = 1e-5
CHUNKS = 3
STRIDE = 64
CHAIN = 1024


def shape_constants(tokens):
    k = np.arange(P)
    ident = (k[:, None] == k[None, :]).astype(np.float32)
    upto = (k[:, None] <= k[None, :]).astype(np.float32)
    later = (k[:, None] > k[None, :]).astype(np.float32)
    causal = np.where(k[:, None] <= k[None, :], 0.0, NEG).astype(np.float32)
    i = (k % WIN)[:, None]
    j = np.arange(WIN)[None, :]
    own = np.where(j <= i, 0.0, NEG)
    prev = np.where(j >= i, 0.0, NEG)
    even = k[:, None] < WIN
    rest = np.concatenate([np.where(even, own, prev), np.where(even, prev, own)], axis=1).astype(np.float32)
    first = rest.copy()
    first[:WIN, WIN:] = NEG
    half = np.arange(0, DH, 2, dtype=np.float32)
    inv_freq = (1.0 / np.float32(10000.0) ** (half / np.float32(DH))).astype(np.float32)
    t = np.arange(tokens, dtype=np.float32)
    freqs = (t[:, None] * inv_freq[None, :]).astype(np.float32)
    base = ((half + np.float32(0.4 * DH)) / np.float32(1.4 * DH)).astype(np.float32)
    power = ((t - tokens // 2) / np.float32(WIN // 2)).astype(np.float32)
    scale = (base[None, :] ** power[:, None]).astype(np.float32)
    cos, sin = np.cos(freqs), np.sin(freqs)
    cosines = np.stack([np.tile(cos * scale, 2), np.tile(cos / scale, 2)], axis=1)
    sines = np.stack([np.concatenate([-sin * scale, sin * scale], 1), np.concatenate([-sin / scale, sin / scale], 1)],
                     axis=1)

    def rows(a):
        return a.reshape(tokens // P, P, 2 * DH).transpose(1, 0, 2).reshape(P, -1)

    return np.ascontiguousarray(
        np.concatenate([ident, upto, later, causal, first, rest, rows(cosines), rows(sines)], axis=1).astype(np.float32))


def attention_steps(z, layer):
    units = [(m, g) for m in range(4) for g in range(2)]
    steps = []
    for k in range(len(units) + 2):
        if k < len(units):
            steps += [(name, z, layer, units[k]) for name in ("scores", "smax", "exp", "p_norm")]
        if 0 < k <= len(units):
            steps += [(name, z, layer, units[k - 1]) for name in ("turn_p", "p_evac")]
        if k > 1 and units[k - 2][1] == 1:
            steps += [(name, z, layer, units[k - 2][0]) for name in ("pv", "o_evac", "wo", "wo_add")]
    return steps


def ln_steps(z, layer, kind):
    return [(n, z, layer, kind) for n in ("ln_stats", "ln_rstd", "ln_apply")]


def mlp_steps(z, layer, beside=()):
    s = [(n, z, layer, "mlp") for n in ("turn_x", "shift_lo", "shift_hi", "resid_bias", "turn_h")]
    s += ln_steps(z, layer, "h")
    s += [(n, z, layer, 0) for n in ("turn_hn", "ln_affine")]
    s += [("up", z, layer, 0), ("up", z, layer, 1), ("gelu", z, layer, 0), ("gate", z, layer, 0), ("up", z, layer, 2)]
    s += [(n, z, layer, j) for j in (1, 2) for n in ("gelu", "gate")]
    s += beside
    s += [("down", z, layer, 0), ("resid", z, layer, 0)]
    return s


def qkv_steps(z, layer):
    s = [(n, z, layer, "qkv") for n in ("turn_x", "shift_lo", "shift_hi")]
    for m in range(5):
        if m < 4:
            s += [(n, z, layer, m) for n in ("proj_q", "q_copy", "proj_k", "k_copy", "proj_v", "v_evac", "rope_c",
                                             "qk_square", "rope_k", "v_shift", "rope_s", "qk_sum", "rinv",
                                             "rope_add", "k_scale", "rinv_q")]
            s += [("v_next", z, layer, m)] if m < 3 else []
        if m > 0:
            s += [(n, z, layer, m - 1) for n in ("turn_q", "q_evac", "turn_k", "k_evac")]
    return s


def output_steps(z):
    return ln_steps(z, 1, "o") + [("store", z, 1, 0)]


def ssd_norm_steps(z):
    return ln_steps(z, 0, "x") + [(n, z, 0, 0) for n in ("turn_xn", "xn_evac")]


def ssd_steps(z):
    s = [(n, z, 0, 0) for n in (
        "ssd_proj", "bt_evac", "ct_evac", "tok_evac", "dt_abs", "dt_log", "decay", "ssd_g",
        "ssd_seg", "seg_exp", "mt", "ssd_y", "y_skip", "ssd_off", "y_off")]
    return s + ln_steps(z, 0, "y") + [("load", z, 0, 0)] + ln_steps(z, 0, "1")


PHASE = {(0, 0): 0, (1, 0): 1, (0, 1): 2, (1, 1): 3}
REST_PHASE = {(1, 1): 0, (0, 0): 1, (1, 0): 2, (0, 1): 3}

FIRST = ssd_norm_steps(0) + ssd_steps(0) + qkv_steps(0, 0)
ATTENTION = [attention_steps(0, 0), attention_steps(1, 0), attention_steps(0, 1), attention_steps(1, 1)]
REST = [mlp_steps(1, 1, ssd_norm_steps(1)) + output_steps(1) + ssd_steps(1) + qkv_steps(1, 0),
        mlp_steps(0, 0) + qkv_steps(0, 1),
        mlp_steps(1, 0) + qkv_steps(1, 1),
        mlp_steps(0, 1, ssd_norm_steps(0)) + output_steps(0) + ssd_steps(0) + qkv_steps(0, 0)]
PASS = sum(ATTENTION, []) + sum(REST, [])
ORDER = [
    256, 257, 258, 0, 260, 4, 1, 2, 261, 10, 262, 5, 3, 263, 8, 6, 259, 264, 9, 16, 275, 265, 266, 268, 276,
    277, 269, 267, 271, 270, 273, 7, 278, 272, 274, 11, 279, 14, 17, 286, 12, 289, 280, 288, 287, 293, 290, 291,
    15, 13, 18, 281, 26, 292, 294, 282, 295, 283, 22, 27, 19, 296, 32, 20, 297, 23, 21, 33, 284, 298, 28, 29,
    24, 25, 30, 299, 34, 31, 300, 301, 42, 35, 36, 37, 38, 43, 302, 303, 48, 305, 39, 46, 306, 40, 41, 44, 47,
    45, 54, 52, 53, 55, 307, 308, 49, 310, 56, 309, 50, 51, 57, 311, 312, 313, 315, 314, 328, 317, 318, 316,
    330, 321, 322, 319, 58, 329, 332, 349, 331, 333, 59, 324, 335, 350, 351, 60, 323, 334, 326, 338, 352, 353,
    61, 325, 345, 336, 339, 356, 62, 346, 372, 341, 357, 347, 373, 354, 348, 320, 370, 340, 355, 371, 374, 359,
    360, 362, 63, 342, 376, 343, 366, 375, 361, 367, 380, 377, 64, 368, 394, 369, 395, 65, 68, 66, 378, 386,
    396, 387, 398, 383, 363, 74, 69, 388, 364, 67, 70, 72, 75, 337, 399, 71, 389, 80, 400, 381, 382, 401, 73,
    76, 390, 78, 391, 81, 90, 384, 402, 79, 77, 86, 392, 327, 403, 404, 82, 83, 393, 405, 406, 358, 407, 84, 91,
    85, 397, 409, 408, 96, 410, 87, 411, 412, 97, 92, 94, 95, 413, 93, 414, 98, 88, 100, 415, 106, 379, 417,
    416, 99, 385, 420, 418, 421, 89, 107, 422, 419, 437, 425, 424, 426, 428, 429, 435, 438, 436, 431, 430, 443,
    445, 102, 112, 423, 103, 432, 101, 442, 108, 441, 458, 439, 456, 446, 344, 440, 448, 457, 452, 433, 110,
    104, 459, 109, 105, 111, 113, 479, 453, 463, 116, 454, 447, 464, 114, 365, 466, 455, 467, 477, 462, 460,
    478, 449, 117, 115, 461, 118, 469, 119, 480, 473, 484, 450, 468, 434, 474, 485, 128, 122, 123, 120, 132,
    129, 121, 124, 427, 488, 130, 451, 475, 487, 481, 125, 476, 126, 483, 482, 133, 131, 127, 136, 493, 134,
    490, 444, 471, 501, 470, 138, 503, 502, 505, 135, 137, 139, 142, 494, 143, 506, 489, 507, 495, 496, 144,
    150, 140, 151, 145, 508, 497, 154, 492, 509, 141, 152, 146, 148, 491, 498, 510, 499, 500, 504, 511, 513,
    514, 512, 516, 147, 517, 149, 153, 515, 160, 155, 158, 518, 519, 161, 520, 156, 162, 170, 521, 522, 465,
    176, 171, 159, 523, 524, 527, 157, 525, 528, 526, 486, 532, 163, 164, 172, 177, 166, 165, 167, 529, 536,
    533, 535, 544, 530, 545, 542, 472, 174, 168, 546, 543, 565, 531, 538, 175, 552, 169, 549, 563, 173, 178,
    559, 566, 182, 180, 547, 537, 564, 550, 181, 548, 553, 567, 555, 539, 540, 179, 183, 584, 184, 570, 560,
    186, 554, 187, 568, 573, 569, 557, 185, 585, 561, 586, 562, 574, 587, 571, 188, 575, 588, 189, 576, 556,
    534, 594, 591, 595, 580, 190, 192, 541, 191, 592, 589, 577, 193, 581, 608, 590, 578, 610, 582, 609, 612,
    597, 583, 613, 596, 600, 194, 601, 196, 197, 614, 602, 615, 598, 551, 603, 198, 202, 604, 611, 605, 616,
    606, 195, 617, 200, 627, 618, 572, 599, 607, 628, 619, 620, 621, 623, 622, 629, 624, 199, 203, 201, 625,
    630, 626, 631, 638, 641, 304, 558, 640, 642, 632, 643, 639, 645, 633, 644, 646, 634, 204, 206, 208, 205,
    593, 635, 647, 648, 636, 649, 207, 218, 209, 210, 212, 650, 285, 219, 651, 652, 653, 654, 224, 225, 213,
    220, 211, 222, 226, 655, 657, 234, 214, 240, 221, 223, 658, 228, 215, 659, 579, 660, 235, 216, 229, 662,
    661, 663, 665, 236, 664, 666, 680, 227, 669, 670, 637, 682, 683, 238, 217, 230, 241, 237, 239, 667, 671,
    674, 681, 687, 673, 675, 703, 676, 678, 668, 688, 686, 244, 691, 656, 704, 692, 231, 701, 684, 702, 690,
    708, 697, 685, 232, 698, 724, 693, 233, 245, 677, 246, 242, 712, 709, 722, 679, 243, 247, 695, 707, 711,
    713, 699, 705, 725, 700, 696, 694, 723, 718, 729, 719, 250, 248, 714, 720, 730, 706, 721, 726, 716, 251,
    672, 249, 738, 252, 689, 715, 727, 739, 740, 253, 717, 254, 733, 728, 741, 732, 735, 734, 736, 737, 742,
    710, 743, 744, 731, 745, 255,
]
LAST = mlp_steps(1, 1) + output_steps(1)


def build(nc, x, w_xproj, dt_bias, a_log, d_skip, wqkv, q_scale, k_scale, wo, ln_g, ln_b, w1, b1, w2, b2, const, out):
    SEQS, T, _ = x.shape
    BLK = T // P
    DEPTH = wqkv.shape[0]
    HID = w2.shape[1]
    SIZES = [min(P, HID - P * j) for j in range(CHUNKS)]
    PASSES = SEQS // 2
    assert T == 512 and D == P and SEQS % 2 == 0

    ctx = ExitStack()
    with ctx:
        def sb(name, shape, dt=F32):
            return ctx.enter_context(nc.sbuf_tensor(name, shape, dt))

        def ps(name, shape):
            return ctx.enter_context(nc.psum_tensor(name, shape, F32))

        cst = sb("cst", [P, const.shape[1]])
        ident, upto, later = cst[:, 0:P], cst[:, P:2 * P], cst[:, 2 * P:3 * P]
        rope_cos = cst[:, 6 * P:6 * P + BLK * P].rearrange("p (m a f) -> p m a f", m=BLK, a=2)
        rope_sin = cst[:, 6 * P + BLK * P:6 * P + 2 * BLK * P].rearrange("p (m a f) -> p m a f", m=BLK, a=2)
        ident_h = sb("ident_h", [P, P], BF16)
        masks_h = sb("masks_h", [P, 3, P], BF16)
        wx_rows = sb("wx_rows", [P, D])
        wx_bc = sb("wx_bc", [D, P])
        wx_tok = sb("wx_tok", [D, 1 + STATE])
        wqkv_s = sb("wqkv_s", [D, DEPTH, 3 * INNER])
        wo_s = sb("wo_s", [P, DEPTH, INNER // P, D])
        w1_s = sb("w1_s", [D, DEPTH, 2 * HID])
        w2_s = sb("w2_s", [P, DEPTH, CHUNKS, D])
        b1_s = sb("b1_s", [P, DEPTH, 2, CHUNKS])
        b2_s = sb("b2_s", [P, DEPTH, D])
        lng_s = sb("lng_s", [P, DEPTH])
        lnb_s = sb("lnb_s", [P, DEPTH])
        scales = sb("scales", [P, DEPTH, 2, DH])
        ssd_par = sb("ssd_par", [P, 4])
        tab_c = sb("tab_c", [P, DEPTH, BLK, 2, DH])
        tab_s = sb("tab_s", [P, DEPTH, BLK, 2, DH])
        ones = sb("ones", [P, P])
        minus_half = sb("minus_half", [P, HEADS])

        xin = [sb(f"xin{z}", [P, BLK, D]) for z in range(2)]
        x1 = [sb(f"x1{z}", [P, BLK, D]) for z in range(2)]
        xres = [sb(f"xres{z}", [P, BLK, D]) for z in range(2)]
        outb = [sb(f"outb{z}", [P, BLK, D]) for z in range(2)]
        qT = [sb(f"qT{z}", [P, HEADS // 2, T]) for z in range(2)]
        kT = [sb(f"kT{z}", [P, HEADS // 2, WIN + T]) for z in range(2)]
        v_odd = [sb(f"v_odd{z}", [P, BLK, HEADS, DH]) for z in range(2)]
        v_even = [sb(f"v_even{z}", [P, BLK, HEADS, DH]) for z in range(2)]
        rnorm = [sb(f"rnorm{z}", [P, BLK, 2 * HEADS]) for z in range(2)]

        hT = sb("hT", [P, T])
        hn = sb("hn", [P, BLK, D])
        hnT = sb("hnT", [P, T])
        xb = sb("xb", [P, BLK, D])
        gates = sb("gates", [P, 2, T])
        uT = sb("uT", [P, CHUNKS, T])
        stats = sb("stats", [P, 2, BLK, 6])
        mv = sb("mv", [P, 2, BLK, 2])
        veps = sb("veps", [P, 2, BLK])
        rstd = sb("rstd", [P, 2, BLK])
        qk = sb("qk", [P, 2, 2 * INNER])
        sq = sb("sq", [P, 2 * INNER])
        ss = sb("ss", [P, 2 * HEADS])
        ssc = sb("ssc", [P, 2 * HEADS])
        rc = sb("rc", [P, 2 * INNER])
        rs = sb("rs", [P, 2 * INNER])
        rot = sb("rot", [P, 2, 2 * INNER])

        xn = sb("xn", [P, BLK, D])
        xnT = sb("xnT", [P, T])
        BT = sb("BT", [STATE, T])
        CT = sb("CT", [STATE, T])
        tok = sb("tok", [P, BLK, 1 + STATE])
        zb = sb("zb", [P, BLK])
        nz = sb("nz", [P, BLK])
        ez = sb("ez", [P, BLK])
        lz = sb("lz", [P, BLK])
        dts = sb("dts", [P, BLK])
        adt = sb("adt", [P, BLK])
        wdt = sb("wdt", [P, BLK])
        R = rc[:, 0:T].rearrange("p (m l) -> p m l", m=BLK)
        MT = rc[:, T:2 * T].rearrange("p (m l) -> p m l", m=BLK)
        E = rs[:, 0:T].rearrange("p (m l) -> p m l", m=BLK)
        et = sb("et", [P, 2 * BLK])
        Bd = sb("Bd", [P, BLK, STATE])
        St = sb("St", [STATE, BLK - 1, D])
        y = sb("y", [P, BLK, D])
        yn = hn

        nmx = sb("nmx", [P, 2, 4])
        nb = sb("nb", [P, 2, 4])
        probs = sb("probs", [P, 2, 4, P])
        probsT = sb("probsT", [P, 4, 4, P])
        sums = sb("sums", [P, 2, 4])
        rl = sb("rl", [P, 2, 4])
        oT = sb("oT", [P, INNER // P, P])

        pS = [ps(f"pS{i}", [P, 4, P]) for i in range(2)]
        pT = ps("pT", [P, 4, P])
        pO = ps("pO", [P, 512])
        pQK = ps("pQK", [P, 2, 512])
        pV = ps("pV", [P, 512])
        pM = ps("pM", [P, 512])

        def semaphore(name):
            return ctx.enter_context(nc.semaphore(name))

        s_bt_evac = semaphore("s_bt_evac")
        s_ct_evac = semaphore("s_ct_evac")
        s_decay = semaphore("s_decay")
        s_down = semaphore("s_down")
        s_dt_abs = semaphore("s_dt_abs")
        s_dt_log = semaphore("s_dt_log")
        s_exp = semaphore("s_exp")
        s_gate = semaphore("s_gate")
        s_gelu = semaphore("s_gelu")
        s_k_evac = semaphore("s_k_evac")
        s_k_scale = semaphore("s_k_scale")
        s_ln_affine = semaphore("s_ln_affine")
        s_ln_apply = semaphore("s_ln_apply")
        s_ln_rstd = semaphore("s_ln_rstd")
        s_ln_stats = semaphore("s_ln_stats")
        s_mt = semaphore("s_mt")
        s_o_evac = semaphore("s_o_evac")
        s_p_norm = semaphore("s_p_norm")
        s_p_evac = semaphore("s_p_evac")
        s_pv = semaphore("s_pv")
        s_q_evac = semaphore("s_q_evac")
        s_q_copy = semaphore("s_q_copy")
        s_k_copy = semaphore("s_k_copy")
        s_qk_square = semaphore("s_qk_square")
        s_qk_sum = semaphore("s_qk_sum")
        s_proj_q = semaphore("s_proj_q")
        s_proj_k = semaphore("s_proj_k")
        s_proj_v = semaphore("s_proj_v")
        s_resid = semaphore("s_resid")
        s_resid_bias = semaphore("s_resid_bias")
        s_rinv = semaphore("s_rinv")
        s_rinv_q = semaphore("s_rinv_q")
        s_rope_k = semaphore("s_rope_k")
        s_rope_add = semaphore("s_rope_add")
        s_rope_c = semaphore("s_rope_c")
        s_rope_s = semaphore("s_rope_s")
        s_scores = semaphore("s_scores")
        s_seg_exp = semaphore("s_seg_exp")
        s_shift_hi = semaphore("s_shift_hi")
        s_shift_lo = semaphore("s_shift_lo")
        s_smax = semaphore("s_smax")
        s_ssd_g = semaphore("s_ssd_g")
        s_ssd_off = semaphore("s_ssd_off")
        s_ssd_proj = semaphore("s_ssd_proj")
        s_ssd_seg = semaphore("s_ssd_seg")
        s_ssd_y = semaphore("s_ssd_y")
        s_tok_evac = semaphore("s_tok_evac")
        s_turn_h = semaphore("s_turn_h")
        s_turn_hn = semaphore("s_turn_hn")
        s_turn_k = semaphore("s_turn_k")
        s_turn_p = semaphore("s_turn_p")
        s_turn_q = semaphore("s_turn_q")
        s_turn_x = semaphore("s_turn_x")
        s_turn_xn = semaphore("s_turn_xn")
        s_up = semaphore("s_up")
        s_v_evac = semaphore("s_v_evac")
        s_v_next = semaphore("s_v_next")
        s_v_shift = semaphore("s_v_shift")
        s_wo = semaphore("s_wo")
        s_wo_add = semaphore("s_wo_add")
        s_xn_evac = semaphore("s_xn_evac")
        s_y_off = semaphore("s_y_off")
        s_y_skip = semaphore("s_y_skip")
        s_section = semaphore("s_section")
        s_hold = semaphore("s_hold")
        s_tables = semaphore("s_tables")
        s_weights = semaphore("s_weights")
        s_rows = semaphore("s_rows")
        s_setup = semaphore("s_setup")
        s_wx = semaphore("s_wx")
        s_scaled = semaphore("s_scaled")
        s_loaded = [semaphore(f"s_loaded{z}") for z in range(2)]
        s_stored = [semaphore(f"s_stored{z}") for z in range(2)]
        s_act_chain = semaphore("s_act_chain")
        s_dve_chain = semaphore("s_dve_chain")
        s_pool_chain = semaphore("s_pool_chain")

        class Count:

            def __init__(self, section, listed, order=None):
                self.section, self.listed, self.links = section, listed, 0
                self.order = range(len(listed)) if order is None else order
                self.first = isinstance(section, int) and section == 0

            def steps(self):
                for self.at in self.order:
                    name, z, layer, arg = self.listed[self.at]
                    yield name, z, layer, arg, sum(s[0] == name for s in self.listed[:self.at + 1])

            def nth(self, name, k):
                if self.first:
                    return max(k, 0)
                per_pass = sum(s[0] == name for s in PASS)
                return self.section * per_pass + (STRIDE - per_pass + k)

            def so_far(self, name):
                return self.nth(name, sum(s[0] == name for s in self.listed[:self.at]))

            def rest(self, name):
                return STRIDE - sum(s[0] == name for s in self.listed)

            def next_link(self):
                self.links += 1
                return self.section * CHAIN + self.links

        block = ctx.enter_context(nc.Block())

        @block.sync
        def _(sp):
            def load(z, seq):
                sp.dma_start(xin[z][:, :, :], x[seq].rearrange("(m p) d -> p m d", p=P)).then_inc(s_loaded[z], 16)

            sp.dma_start(cst[:, :], const[:, :]).then_inc(s_tables, 16)
            for l in range(DEPTH):
                sp.dma_start(scales[:, l, 0, :], q_scale[l].partition_broadcast(P)).then_inc(s_tables, 16)
                sp.dma_start(scales[:, l, 1, :], k_scale[l].partition_broadcast(P)).then_inc(s_tables, 16)
            sp.dma_start(wx_rows[:, :], w_xproj[1:1 + P, :]).then_inc(s_tables, 16)
            sp.dma_start(wx_tok[:, 0:1], w_xproj[0:1, :].rearrange("a d -> d a")).then_inc(s_tables, 16)
            for n, src in enumerate((dt_bias, a_log, d_skip)):
                sp.dma_start(ssd_par[:, n:n + 1], src.partition_broadcast(P)).then_inc(s_tables, 16)
            load(0, 0)
            for z in range(2):
                sp.sem_inc(s_stored[z], 16)
            for l in range(DEPTH):
                sp.dma_start(wqkv_s[:, l, :], wqkv[l]).then_inc(s_weights, 16)
                sp.dma_start(wo_s[:, l, :, :], wo[l].rearrange("(c p) n -> p c n", p=P)).then_inc(s_weights, 16)
                sp.dma_start(w1_s[:, l, :], w1[l]).then_inc(s_weights, 16)
                sp.dma_start(b2_s[:, l, :], b2[l].partition_broadcast(P)).then_inc(s_weights, 16)
                sp.dma_start(lng_s[:, l:l + 1], ln_g[l:l + 1, :].rearrange("a d -> d a")).then_inc(s_weights, 16)
                sp.dma_start(lnb_s[:, l:l + 1], ln_b[l:l + 1, :].rearrange("a d -> d a")).then_inc(s_weights, 16)
                for j, n in enumerate(SIZES):
                    sp.dma_start(w2_s[0:n, l, j, :], w2[l, P * j:P * j + n, :]).then_inc(s_weights, 16)
                    for half in range(2):
                        lo = half * HID + P * j
                        sp.dma_start(b1_s[0:n, l, half, j:j + 1],
                                     b1[l:l + 1, lo:lo + n].rearrange("a d -> d a")).then_inc(s_weights, 16)
            load(1, 1)

            def section(count):
                for name, z, layer, arg, n in count.steps():
                    if name == "v_shift":
                        m = arg
                        sp.wait_ge(s_v_shift, 16 * count.nth("v_shift", n - 1))
                        sp.sem_inc(s_hold, 1)
                        sp.wait_ge(s_v_evac, count.nth("v_evac", n))
                        sp.dma_start(v_even[z][0:WIN, m, :, :], v_odd[z][0:WIN, m, :, :]).then_inc(s_v_shift, 16)
                    elif name == "v_next":
                        m = arg
                        sp.wait_ge(s_v_next, 16 * count.nth("v_next", n - 1))
                        sp.sem_inc(s_hold, 1)
                        sp.wait_ge(s_v_evac, count.so_far("v_evac"))
                        sp.dma_start(v_even[z][WIN:P, m + 1, :, :], v_odd[z][WIN:P, m, :, :]).then_inc(s_v_next, 16)
                    elif name == "load":
                        sp.wait_ge(s_ln_apply, count.so_far("ln_apply"))
                        sp.sem_inc(s_hold, 1)
                        if count.first:
                            load(0, 2)
                        else:
                            load(z, (2 * count.section + (2 if z == 0 else 1)) % SEQS)
                    elif name == "store":
                        sp.wait_ge(s_ln_apply, count.so_far("ln_apply"))
                        sp.sem_inc(s_hold, 1)
                        if isinstance(count.section, int):
                            seq = SEQS - 1
                        elif z == 0:
                            seq = 2 * (count.section - 1)
                        else:
                            seq = (2 * (count.section - 1) + (SEQS - 1)) % SEQS
                        sp.dma_start(out[seq].rearrange("(m p) d -> p m d", p=P),
                                            outb[z][:, :, :]).then_inc(s_stored[z], 16)
                if count.first:
                    sp.wait_ge(s_v_shift, 16 * count.so_far("v_shift"))
                    sp.sem_inc(s_hold, 1)
                    sp.wait_ge(s_v_next, 16 * count.so_far("v_next"))
                    sp.sem_inc(s_hold, 1)
                    sp.sem_inc(s_v_shift, 16 * count.rest("v_shift"))
                    sp.sem_inc(s_v_next, 16 * count.rest("v_next"))
                    sp.drain()
                    sp.drain().then_inc(s_section, 1)
                    sp.wait_ge(s_section, 5)
                    sp.sem_inc(s_hold, 1)

            section(Count(0, FIRST))
            with sp.Fori(0, PASSES) as i:
                section(Count(i + 1, PASS, ORDER))
            section(Count(PASSES + 1, LAST))
            sp.wait_ge(s_stored[0], 16 * (PASSES + 1))
            sp.wait_ge(s_stored[1], 16 * (PASSES + 2))
            sp.wait_ge(s_loaded[0], 16 * (PASSES + 2))
            sp.wait_ge(s_loaded[1], 16 * (PASSES + 1))

        N_TABLES = 16 * (6 + DEPTH * 2)
        N_WEIGHTS = 16 * DEPTH * (6 + 3 * CHUNKS)

        @block.tensor
        def _(pe):
            mm, turn = nc.tensor.matmul, nc.tensor.transpose

            def section(count):
                for name, z, layer, arg, n in count.steps():
                    if name == "turn_x":
                        pe.wait_ge(s_v_evac, count.so_far("v_evac"))
                        if count.first:
                            pe.wait_ge(s_weights, N_WEIGHTS)
                        if arg == "mlp":
                            pe.wait_ge(s_wo_add, count.nth("wo_add", 4 * REST_PHASE[z, layer]))
                        pe.wait_ge(s_resid, count.so_far("resid"))
                        pe.wait_ge(s_ln_apply, count.so_far("ln_apply"))
                        for m in range(BLK):
                            last = turn(pV[:, m * P:(m + 1) * P], xres[z][:, m, :], ident)
                        last.then_inc(s_turn_x, 1)
                    elif name == "turn_h":
                        pe.wait_ge(s_shift_lo, count.so_far("shift_lo"))
                        pe.wait_ge(s_shift_hi, count.so_far("shift_hi"))
                        pe.wait_ge(s_q_copy, count.so_far("q_copy"))
                        for m in range(BLK):
                            last = turn(pQK[:, 0, m * P:(m + 1) * P], hT[:, m * P:(m + 1) * P], ident)
                        last.then_inc(s_turn_h, 1)
                    elif name == "turn_hn":
                        pe.wait_ge(s_ln_apply, count.so_far("ln_apply"))
                        pe.wait_ge(s_k_copy, count.so_far("k_copy"))
                        for m in range(BLK):
                            last = turn(pQK[:, 1, m * P:(m + 1) * P], hn[:, m, :], ident)
                        last.then_inc(s_turn_hn, 1)
                    elif name == "up":
                        j = arg
                        if j == 0:
                            pe.wait_ge(s_ln_affine, count.so_far("ln_affine"))
                        if j == 1:
                            pe.wait_ge(s_k_evac, count.so_far("k_evac"))
                        if j == 2:
                            pe.wait_ge(s_gate, count.nth("gate", n - 2))
                        a, g = (pV[:, :], pM[:, :]) if j == 1 else (pQK[:, 0, :], pQK[:, 1, :])
                        lo, size = P * j, SIZES[j]
                        mm(a[0:size], w1_s[:, layer, lo:lo + size], hnT[:, :], start=True, stop=True)
                        mm(g[0:size], w1_s[:, layer, HID + lo:HID + lo + size], hnT[:, :], start=True,
                           stop=True).then_inc(s_up, 1)
                    elif name == "down":
                        pe.wait_ge(s_gate, count.so_far("gate"))
                        for m in range(BLK):
                            for j, size in enumerate(SIZES):
                                last = mm(pV[:, m * P:(m + 1) * P], uT[0:size, j, m * P:(m + 1) * P],
                                          w2_s[0:size, layer, j, :], start=j == 0, stop=j == CHUNKS - 1)
                        last.then_inc(s_down, 1)
                    elif name == "proj_q":
                        m = arg
                        pe.wait_ge(s_shift_lo, count.so_far("shift_lo"))
                        pe.wait_ge(s_shift_hi, count.so_far("shift_hi"))
                        pe.wait_ge(s_q_copy, count.so_far("q_copy"))
                        mm(pQK[:, 0, :], hT[:, m * P:(m + 1) * P], wqkv_s[:, layer, 0:INNER],
                           start=True, stop=True).then_inc(s_proj_q, 1)
                    elif name == "proj_k":
                        m = arg
                        pe.wait_ge(s_shift_lo, count.so_far("shift_lo"))
                        pe.wait_ge(s_shift_hi, count.so_far("shift_hi"))
                        pe.wait_ge(s_k_copy, count.so_far("k_copy"))
                        mm(pQK[:, 1, :], hT[:, m * P:(m + 1) * P], wqkv_s[:, layer, INNER:2 * INNER],
                           start=True, stop=True).then_inc(s_proj_k, 1)
                    elif name == "proj_v":
                        m = arg
                        pe.wait_ge(s_shift_lo, count.so_far("shift_lo"))
                        pe.wait_ge(s_shift_hi, count.so_far("shift_hi"))
                        pe.wait_ge(s_v_evac, count.so_far("v_evac"))
                        mm(pV[:, :], hT[:, m * P:(m + 1) * P], wqkv_s[:, layer, 2 * INNER:3 * INNER],
                           start=True, stop=True).then_inc(s_proj_v, 1)
                    elif name == "turn_q":
                        m = arg
                        pe.wait_ge(s_k_evac, count.so_far("k_evac"))
                        pe.wait_ge(s_rope_add, count.nth("rope_add", n))
                        for c in range(4):
                            last = turn(pM[:, c * P:(c + 1) * P], rot[:, n % 2, c * P:(c + 1) * P], ident)
                        last.then_inc(s_turn_q, 1)
                    elif name == "turn_k":
                        m = arg
                        pe.wait_ge(s_q_evac, count.nth("q_evac", n))
                        pe.wait_ge(s_k_scale, count.nth("k_scale", n))
                        for c in range(4):
                            last = turn(pM[:, c * P:(c + 1) * P], rot[:, n % 2, INNER + c * P:INNER + (c + 1) * P], ident)
                        last.then_inc(s_turn_k, 1)
                    elif name == "turn_xn":
                        pe.wait_ge(s_ln_apply, count.so_far("ln_apply"))
                        pe.wait_ge(s_gelu, count.so_far("gelu"))
                        for m in range(BLK):
                            last = turn(pM[:, m * P:(m + 1) * P], xn[:, m, :], ident)
                        last.then_inc(s_turn_xn, 1)
                    elif name == "ssd_proj":
                        pe.wait_ge(s_xn_evac, count.so_far("xn_evac"))
                        pe.wait_ge(s_gate, count.so_far("gate"))
                        mm(pQK[:, 0, :], wx_bc[:, :], xnT[:, :], start=True, stop=True)
                        for m in range(BLK):
                            last = mm(pQK[:, 1, m * (1 + STATE):(m + 1) * (1 + STATE)], xnT[:, m * P:(m + 1) * P],
                                      wx_tok[:, :], start=True, stop=True)
                        last.then_inc(s_ssd_proj, 1)
                    elif name == "ssd_g":
                        pe.wait_ge(s_bt_evac, count.so_far("bt_evac"))
                        pe.wait_ge(s_ct_evac, count.so_far("ct_evac"))
                        for m in range(BLK):
                            last = mm(pQK[:, 0, m * P:(m + 1) * P], BT[:, m * P:(m + 1) * P], CT[:, m * P:(m + 1) * P],
                                      start=True, stop=True)
                        last.then_inc(s_ssd_g, 1)
                    elif name == "ssd_seg":
                        pe.wait_ge(s_decay, count.so_far("decay"))
                        pe.wait_ge(s_resid, count.so_far("resid"))
                        mm(pV[:, :], ident_h[:, :], masks_h[:, 0:1, :].to_broadcast([P, BLK, P]), start=True, stop=False)
                        mm(pV[:, :], later, R[:, :, :], start=False, stop=True)
                        mm(pM[:, 0:BLK], upto, adt[:, :], start=True, stop=True)
                        mm(pM[:, BLK:2 * BLK], ones[:, :], adt[:, :], start=True, stop=True).then_inc(s_ssd_seg, 1)
                    elif name == "ssd_y":
                        pe.wait_ge(s_mt, count.so_far("mt"))
                        for m in range(BLK):
                            mm(pM[:, m * P:(m + 1) * P], MT[:, m, :], xn[:, m, :], start=True, stop=True)
                        for m in range(BLK - 1):
                            last = mm(pQK[0:STATE, 1, m * P:(m + 1) * P], Bd[:, m, :], xn[:, m, :], start=True, stop=True)
                        last.then_inc(s_ssd_y, 1)
                    elif name == "ssd_off":
                        pe.wait_ge(s_y_skip, count.so_far("y_skip"))
                        for m in range(1, BLK):
                            last = mm(pV[:, m * P:(m + 1) * P], CT[:, m * P:(m + 1) * P], St[:, m - 1, :],
                                      start=True, stop=True)
                        last.then_inc(s_ssd_off, 1)
                    elif name == "scores":
                        m, g = arg
                        before = 4 * (PHASE[z, layer] - 1)
                        pe.wait_ge(s_k_evac, count.nth("k_evac", before + m + 1))
                        pe.wait_ge(s_exp, count.nth("exp", n - 2))
                        bank = pS[n % 2]
                        mask = masks_h[:, 1:2, :] if m == 0 else masks_h[:, 2:3, :]
                        mm(bank[:, :, :], ident_h[:, :], mask.to_broadcast([P, 4, P]), start=True, stop=False,
                           skip_group_check=True)
                        for h in range(4):
                            c, r = h, DH * g
                            lo = m * P
                            q = qT[z][r:r + DH, c, lo:lo + P]
                            keys = kT[z][r:r + DH, c, lo:lo + WIN + P]
                            own_prev = keys[:, 0:2 * WIN].rearrange("p (a b) -> p a b", a=2)[:, ::-1, :]
                            mm(bank[0:WIN, h, :], q[:, 0:WIN], own_prev, start=False, stop=h == 3, skip_group_check=True)
                            last = mm(bank[WIN:P, h, :], q[:, WIN:P], keys[:, WIN:WIN + P], start=False, stop=h == 3,
                                      skip_group_check=True)
                        last.then_inc(s_scores, 1)
                    elif name == "turn_p":
                        pe.wait_ge(s_p_norm, count.nth("p_norm", n))
                        pe.wait_ge(s_p_evac, count.so_far("p_evac"))
                        for h in range(4):
                            last = turn(pT[:, h, :], probs[:, n % 2, h, :], ident)
                        last.then_inc(s_turn_p, 1)
                    elif name == "pv":
                        m = arg
                        before = PHASE[z, layer] - 1
                        pe.wait_ge(s_v_shift, 16 * count.nth("v_shift", 4 * before + m + 1))
                        pe.wait_ge(s_v_next, 16 * count.nth("v_next", 3 * before + m))
                        pe.wait_ge(s_p_evac, count.nth("p_evac", 2 * n))
                        pe.wait_ge(s_wo_add, count.so_far("wo_add"))
                        for c in range(4):
                            for row, values in ((0, v_even[z]), (WIN, v_odd[z])):
                                for g in range(2):
                                    last = mm(pO[DH * g:DH * g + DH, c * P + row:c * P + row + WIN],
                                              values[:, m, 2 * c + g, :],
                                              probsT[:, (2 * n - 1 + g) % 4, c, row:row + WIN], start=True, stop=True)
                        last.then_inc(s_pv, 1)
                    elif name == "wo":
                        pe.wait_ge(s_o_evac, count.nth("o_evac", n))
                        for c in range(4):
                            last = mm(pO[:, 0:D], oT[:, c, :], wo_s[:, layer, c, :], start=c == 0, stop=c == 3)
                        last.then_inc(s_wo, 1)
                if count.first:
                    pe.drain()
                    pe.sem_inc(s_turn_x, count.rest("turn_x"))
                    pe.sem_inc(s_turn_h, count.rest("turn_h"))
                    pe.sem_inc(s_turn_hn, count.rest("turn_hn"))
                    pe.sem_inc(s_up, count.rest("up"))
                    pe.sem_inc(s_down, count.rest("down"))
                    pe.sem_inc(s_proj_q, count.rest("proj_q"))
                    pe.sem_inc(s_proj_k, count.rest("proj_k"))
                    pe.sem_inc(s_proj_v, count.rest("proj_v"))
                    pe.sem_inc(s_turn_q, count.rest("turn_q"))
                    pe.sem_inc(s_turn_k, count.rest("turn_k"))
                    pe.sem_inc(s_turn_xn, count.rest("turn_xn"))
                    pe.sem_inc(s_ssd_proj, count.rest("ssd_proj"))
                    pe.sem_inc(s_ssd_g, count.rest("ssd_g"))
                    pe.sem_inc(s_ssd_seg, count.rest("ssd_seg"))
                    pe.sem_inc(s_ssd_y, count.rest("ssd_y"))
                    pe.sem_inc(s_ssd_off, count.rest("ssd_off"))
                    pe.sem_inc(s_scores, count.rest("scores"))
                    pe.sem_inc(s_turn_p, count.rest("turn_p"))
                    pe.sem_inc(s_pv, count.rest("pv"))
                    pe.sem_inc(s_wo, count.rest("wo"))
                    pe.drain().then_inc(s_section, 1)
                    pe.wait_ge(s_section, 5)
                    pe.sem_inc(s_hold, 1)

            pe.wait_ge(s_tables, N_TABLES)
            pe.wait_ge(s_setup, 2)
            turn(pM[:, 0:P], wx_rows[:, :], ident).then_inc(s_wx, 1)
            pe.wait_ge(s_wx, 2)
            section(Count(0, FIRST))
            with pe.Fori(0, PASSES) as i:
                section(Count(i + 1, PASS, ORDER))
            section(Count(PASSES + 1, LAST))

        @block.scalar
        def _(act):
            activation = nc.scalar.activation

            def copy(out, in_):
                return activation(out, in_, ACT.Copy)

            def section(count):
                def link(ins):
                    ins.then_inc(s_act_chain, 1)
                    act.wait_ge(s_act_chain, count.next_link())

                for name, z, layer, arg, n in count.steps():
                    if name == "shift_lo":
                        act.wait_ge(s_turn_x, count.so_far("turn_x"))
                        act.wait_ge(s_proj_q, count.so_far("proj_q"))
                        act.wait_ge(s_proj_k, count.so_far("proj_k"))
                        copy(hT[0:D // 2, :], pV[0:D // 2, :]).then_inc(s_shift_lo, 1)
                    elif name == "ln_affine":
                        act.wait_ge(s_turn_hn, count.so_far("turn_hn"))
                        activation(hnT[:, :], pQK[:, 1, :], ACT.Identity, bias=lnb_s[:, layer:layer + 1],
                                          scale=lng_s[:, layer:layer + 1]).then_inc(s_ln_affine, 1)
                    elif name == "gelu":
                        j = arg
                        act.wait_ge(s_up, count.nth("up", n))
                        src = pM[:, :] if j == 1 else pQK[:, 1, :]
                        size = SIZES[j]
                        activation(gates[0:size, n % 2, :], src[0:size], ACT.Gelu,
                                   bias=b1_s[0:size, layer, 1, j:j + 1]).then_inc(s_gelu, 1)
                    elif name == "q_copy":
                        act.wait_ge(s_proj_q, count.nth("proj_q", n))
                        act.wait_ge(s_rope_s, count.nth("rope_s", n - 2))
                        act.wait_ge(s_rope_c, count.nth("rope_c", n - 2))
                        act.wait_ge(s_rope_k, count.nth("rope_k", n - 2))
                        act.wait_ge(s_qk_square, count.nth("qk_square", n - 2))
                        copy(qk[:, n % 2, 0:INNER], pQK[:, 0, :]).then_inc(s_q_copy, 1)
                    elif name == "k_copy":
                        act.wait_ge(s_proj_k, count.nth("proj_k", n))
                        act.wait_ge(s_rope_s, count.nth("rope_s", n - 2))
                        act.wait_ge(s_rope_c, count.nth("rope_c", n - 2))
                        act.wait_ge(s_rope_k, count.nth("rope_k", n - 2))
                        act.wait_ge(s_qk_square, count.nth("qk_square", n - 2))
                        copy(qk[:, n % 2, INNER:2 * INNER], pQK[:, 1, :]).then_inc(s_k_copy, 1)
                    elif name == "qk_square":
                        act.wait_ge(s_q_copy, count.nth("q_copy", n))
                        act.wait_ge(s_k_copy, count.nth("k_copy", n))
                        act.wait_ge(s_qk_sum, count.nth("qk_sum", n - 1))
                        activation(sq[:, :], qk[:, n % 2, :], ACT.Square).then_inc(s_qk_square, 1)
                    elif name == "q_evac":
                        m = arg
                        act.wait_ge(s_turn_q, count.nth("turn_q", n))
                        copy(qT[z][:, :, m * P:(m + 1) * P],
                             pM[:, :].rearrange("p (c t) -> p c t", c=4)).then_inc(s_q_evac, 1)
                    elif name == "k_evac":
                        m = arg
                        act.wait_ge(s_turn_k, count.nth("turn_k", n))
                        copy(kT[z][:, :, WIN + m * P:WIN + (m + 1) * P],
                             pM[:, :].rearrange("p (c t) -> p c t", c=4)).then_inc(s_k_evac, 1)
                    elif name == "v_evac":
                        m = arg
                        act.wait_ge(s_proj_v, count.nth("proj_v", n))
                        copy(v_odd[z][:, m, :, :],
                             pV[:, :].rearrange("p (h d) -> p h d", h=HEADS)).then_inc(s_v_evac, 1)
                    elif name == "xn_evac":
                        act.wait_ge(s_turn_xn, count.so_far("turn_xn"))
                        copy(xnT[:, :], pM[:, :]).then_inc(s_xn_evac, 1)
                    elif name == "bt_evac":
                        act.wait_ge(s_ssd_proj, count.so_far("ssd_proj"))
                        copy(BT[:, :], pQK[0:STATE, 0, :]).then_inc(s_bt_evac, 1)
                    elif name == "tok_evac":
                        act.wait_ge(s_ssd_proj, count.so_far("ssd_proj"))
                        copy(tok[:, :, :],
                             pQK[:, 1, 0:BLK * (1 + STATE)].rearrange("p (m f) -> p m f", m=BLK)).then_inc(s_tok_evac, 1)
                    elif name == "dt_log":
                        act.wait_ge(s_dt_abs, count.so_far("dt_abs"))
                        link(activation(ez[:, :], nz[:, :], ACT.Exp))
                        activation(lz[:, :], ez[:, :], ACT.Ln, bias=1.0).then_inc(s_dt_log, 1)
                    elif name == "seg_exp":
                        act.wait_ge(s_ssd_seg, count.so_far("ssd_seg"))
                        activation(E[:, :, :], pV[:, :].rearrange("p (m l) -> p m l", m=BLK), ACT.Exp)
                        activation(et[:, :], pM[:, 0:2 * BLK], ACT.Exp).then_inc(s_seg_exp, 1)
                    elif name == "exp":
                        m, g = arg
                        act.wait_ge(s_smax, count.nth("smax", n))
                        act.wait_ge(s_turn_p, count.nth("turn_p", n - 2))
                        for h in range(4):
                            last = activation(probs[:, n % 2, h, :], pS[n % 2][:, h, :], ACT.Exp,
                                              bias=nb[:, n % 2, h:h + 1], scale=rnorm[z][:, m, 2 * h + g:2 * h + g + 1],
                                              accum_out=sums[:, n % 2, h:h + 1])
                        last.then_inc(s_exp, 1)
                    elif name == "p_evac":
                        act.wait_ge(s_turn_p, count.nth("turn_p", n))
                        act.wait_ge(s_pv, count.nth("pv", (n - 3) // 2))
                        copy(probsT[:, n % 4, :, :], pT[:, :, :]).then_inc(s_p_evac, 1)
                    elif name == "o_evac":
                        act.wait_ge(s_pv, count.nth("pv", n))
                        act.wait_ge(s_wo, count.nth("wo", n - 1))
                        copy(oT[:, :, :], pO[:, :].rearrange("p (c t) -> p c t", c=4)).then_inc(s_o_evac, 1)
                act.sem_inc(s_act_chain, CHAIN - count.links)
                if count.first:
                    act.drain()
                    act.sem_inc(s_shift_lo, count.rest("shift_lo"))
                    act.sem_inc(s_ln_affine, count.rest("ln_affine"))
                    act.sem_inc(s_gelu, count.rest("gelu"))
                    act.sem_inc(s_q_copy, count.rest("q_copy"))
                    act.sem_inc(s_k_copy, count.rest("k_copy"))
                    act.sem_inc(s_qk_square, count.rest("qk_square"))
                    act.sem_inc(s_q_evac, count.rest("q_evac"))
                    act.sem_inc(s_k_evac, count.rest("k_evac"))
                    act.sem_inc(s_v_evac, count.rest("v_evac"))
                    act.sem_inc(s_xn_evac, count.rest("xn_evac"))
                    act.sem_inc(s_bt_evac, count.rest("bt_evac"))
                    act.sem_inc(s_tok_evac, count.rest("tok_evac"))
                    act.sem_inc(s_dt_log, count.rest("dt_log"))
                    act.sem_inc(s_seg_exp, count.rest("seg_exp"))
                    act.sem_inc(s_exp, count.rest("exp"))
                    act.sem_inc(s_p_evac, count.rest("p_evac"))
                    act.sem_inc(s_o_evac, count.rest("o_evac"))
                    act.drain().then_inc(s_section, 1)
                    act.wait_ge(s_section, 5)
                    act.sem_inc(s_hold, 1)

            act.wait_ge(s_tables, N_TABLES)
            activation(ssd_par[:, 3:4], ssd_par[:, 1:2], ACT.Exp).then_inc(s_rows, 1)
            section(Count(0, FIRST))
            with act.Fori(0, PASSES) as i:
                section(Count(i + 1, PASS, ORDER))
            section(Count(PASSES + 1, LAST))

        @block.vector
        def _(dve):
            v = nc.vector

            def section(count):
                def link(ins):
                    ins.then_inc(s_dve_chain, 1)
                    dve.wait_ge(s_dve_chain, count.next_link())

                def halves(a):
                    return a.rearrange("p (a h f) -> p a h f", a=2, h=HEADS)
                for name, z, layer, arg, n in count.steps():
                    if name == "shift_hi":
                        dve.wait_ge(s_turn_x, count.so_far("turn_x"))
                        dve.wait_ge(s_proj_q, count.so_far("proj_q"))
                        dve.wait_ge(s_proj_k, count.so_far("proj_k"))
                        v.tensor_copy(hT[D // 2:D, 1:T],
                                      pV[D // 2:D, 0:T - 1]).then_inc(s_shift_hi, 1)
                    elif name == "ln_stats":
                        kind = arg
                        if kind == "x":
                            dve.wait_ge(s_loaded[z], (count.section + (1 if z == 0 else 0)) * 16)
                        if kind == "h":
                            dve.wait_ge(s_turn_h, count.so_far("turn_h"))
                        if kind == "y":
                            dve.wait_ge(s_y_off, count.so_far("y_off"))
                        if kind == "1":
                            dve.wait_ge(s_ln_apply, count.so_far("ln_apply"))
                        if kind == "o":
                            dve.wait_ge(s_resid, count.so_far("resid"))
                        src = {"h": pQK[:, 0, :].rearrange("p (m d) -> p m d", m=BLK), "x": xin[z], "y": y, "1": x1[z],
                               "o": xres[z]}[kind]
                        for m in range(BLK):
                            ins = v.bn_stats(stats[:, n % 2, m, :], src[:, m, :])
                        link(ins)
                        dve.sem_inc(s_hold, 1)
                        for m in range(BLK):
                            last = v.bn_aggr(mv[:, n % 2, m, :], stats[:, n % 2, m, :])
                        last.then_inc(s_ln_stats, 1)
                    elif name == "ln_apply":
                        kind = arg
                        dve.wait_ge(s_ln_rstd, count.nth("ln_rstd", n))
                        if kind in ("h", "y", "o"):
                            dve.wait_ge(s_ln_apply, count.nth("ln_apply", n - 1))
                        src = {"h": pQK[:, 0, :].rearrange("p (m d) -> p m d", m=BLK), "x": xin[z], "y": y, "1": x1[z],
                               "o": xres[z]}[kind]
                        dst = {"h": hn, "x": xn, "y": yn, "1": xres[z], "o": yn}[kind]
                        if kind == "o":
                            dve.wait_ge(s_stored[z], count.section * 16)
                        for m in range(BLK):
                            last = v.tensor_scalar(dst[:, m, :], src[:, m, :], mv[:, n % 2, m, 0:1],
                                                   rstd[:, n % 2, m:m + 1], ALU.subtract, ALU.mult)
                        if kind == "y":
                            link(last)
                            last = v.tensor_tensor(x1[z][:, :, :], xin[z][:, :, :], yn[:, :, :], ALU.add)
                        if kind == "o":
                            link(last)
                            last = v.tensor_tensor(outb[z][:, :, :], x1[z][:, :, :], yn[:, :, :], ALU.add)
                        last.then_inc(s_ln_apply, 1)
                    elif name == "gate":
                        j = arg
                        dve.wait_ge(s_gelu, count.nth("gelu", n))
                        src = pV[:, :] if j == 1 else pQK[:, 0, :]
                        size = SIZES[j]
                        v.scalar_tensor_tensor(uT[0:size, j, :], src[0:size], b1_s[0:size, layer, 0, j:j + 1],
                                                      gates[0:size, n % 2, :], ALU.add, ALU.mult).then_inc(s_gate, 1)
                    elif name == "resid":
                        dve.wait_ge(s_down, count.so_far("down"))
                        dve.wait_ge(s_resid_bias, count.so_far("resid_bias"))
                        v.tensor_tensor(xres[z][:, :, :], pV[:, :].rearrange("p (m d) -> p m d", m=BLK),
                                               xb[:, :, :], ALU.add).then_inc(s_resid, 1)
                    elif name == "rope_k":
                        m = arg
                        dve.wait_ge(s_k_copy, count.nth("k_copy", n))
                        dve.wait_ge(s_rope_add, count.nth("rope_add", n - 1))
                        v.tensor_tensor(rc[:, INNER:2 * INNER].rearrange("p (h f) -> p h f", h=HEADS),
                                        qk[:, n % 2, INNER:2 * INNER].rearrange("p (h f) -> p h f", h=HEADS),
                                        tab_c[:, layer, m, 1, :].unsqueeze(1).to_broadcast([P, HEADS, DH]),
                                        ALU.mult).then_inc(s_rope_k, 1)
                    elif name == "rope_s":
                        m = arg
                        dve.wait_ge(s_q_copy, count.nth("q_copy", n))
                        dve.wait_ge(s_k_copy, count.nth("k_copy", n))
                        dve.wait_ge(s_rope_add, count.nth("rope_add", n - 1))
                        q, o, hf = halves(qk[:, n % 2, :]), halves(rs[:, :]), DH // 2
                        for a, b in ((0, hf), (hf, 0)):
                            table = tab_s[:, layer, m, :, a:a + hf].unsqueeze(2).to_broadcast([P, 2, HEADS, hf])
                            last = v.tensor_tensor(o[:, :, :, a:a + hf], q[:, :, :, b:b + hf], table, ALU.mult)
                        last.then_inc(s_rope_s, 1)
                    elif name == "qk_sum":
                        m = arg
                        dve.wait_ge(s_qk_square, count.nth("qk_square", n))
                        dve.wait_ge(s_rinv, count.nth("rinv", n - 1))
                        v.tensor_reduce(ss[:, :], sq[:, :].rearrange("p (h d) -> p h d", d=DH), AX.X,
                                        ALU.add).then_inc(s_qk_sum, 1)
                    elif name == "rope_add":
                        m = arg
                        dve.wait_ge(s_rope_c, count.nth("rope_c", n))
                        dve.wait_ge(s_rope_k, count.nth("rope_k", n))
                        dve.wait_ge(s_rope_s, count.nth("rope_s", n))
                        dve.wait_ge(s_turn_k, count.nth("turn_k", n - 2))
                        v.tensor_tensor(rot[:, n % 2, :], rc[:, :], rs[:, :], ALU.add).then_inc(s_rope_add, 1)
                    elif name == "ct_evac":
                        dve.wait_ge(s_ssd_proj, count.so_far("ssd_proj"))
                        v.tensor_copy(CT[:, :], pQK[STATE:P, 0, :]).then_inc(s_ct_evac, 1)
                    elif name == "dt_abs":
                        dve.wait_ge(s_tok_evac, count.so_far("tok_evac"))
                        link(v.tensor_scalar(zb[:, :], tok[:, :, 0], ssd_par[:, 0:1], None, ALU.add))
                        v.scalar_tensor_tensor(nz[:, :], zb[:, :], -1.0, zb[:, :], ALU.mult,
                                               ALU.min).then_inc(s_dt_abs, 1)
                    elif name == "decay":
                        dve.wait_ge(s_dt_log, count.so_far("dt_log"))
                        link(v.scalar_tensor_tensor(dts[:, :], zb[:, :], 0.0, lz[:, :], ALU.max, ALU.add))
                        link(v.tensor_scalar(adt[:, :], dts[:, :], ssd_par[:, 3:4], None, ALU.mult))
                        v.tensor_tensor(R[:, :, :], upto.unsqueeze(1).to_broadcast([P, BLK, P]),
                                        adt[:, :].unsqueeze(2).to_broadcast([P, BLK, P]),
                                        ALU.mult).then_inc(s_decay, 1)
                    elif name == "mt":
                        dve.wait_ge(s_ssd_g, count.so_far("ssd_g"))
                        dve.wait_ge(s_seg_exp, count.so_far("seg_exp"))
                        link(v.tensor_tensor(wdt[:, :], dts[:, :], E[:, :, P - 1], ALU.mult))
                        v.tensor_tensor(Bd[:, :, :], tok[:, :, 1:1 + STATE],
                                        wdt[:, :].unsqueeze(2).to_broadcast([P, BLK, STATE]), ALU.mult)
                        for m in range(BLK):
                            last = v.scalar_tensor_tensor(MT[:, m, :], pQK[:, 0, m * P:(m + 1) * P], dts[:, m:m + 1],
                                                          E[:, m, :], ALU.mult, ALU.mult)
                        last.then_inc(s_mt, 1)
                    elif name == "y_skip":
                        dve.wait_ge(s_ssd_y, count.so_far("ssd_y"))
                        v.scalar_tensor_tensor(y[:, :, :], xn[:, :, :], ssd_par[:, 2:3],
                                               pM[:, :].rearrange("p (m d) -> p m d", m=BLK), ALU.mult, ALU.add)
                        last = v.tensor_copy(St[:, 0, :], pQK[0:STATE, 1, 0:D])
                        for m in range(1, BLK - 1):
                            link(last)
                            last = v.scalar_tensor_tensor(St[:, m, :], St[:, m - 1, :], et[0:STATE, BLK + m:BLK + m + 1],
                                                          pQK[0:STATE, 1, m * D:(m + 1) * D], ALU.mult, ALU.add)
                        last.then_inc(s_y_skip, 1)
                    elif name == "y_off":
                        dve.wait_ge(s_ssd_off, count.so_far("ssd_off"))
                        for m in range(1, BLK):
                            last = v.scalar_tensor_tensor(y[:, m, :], pV[:, m * D:(m + 1) * D], et[:, m:m + 1],
                                                          y[:, m, :], ALU.mult, ALU.add)
                        last.then_inc(s_y_off, 1)
                    elif name == "smax":
                        m, g = arg
                        dve.wait_ge(s_rinv_q, count.nth("rinv_q", 4 * (PHASE[z, layer] - 1) + m + 1))
                        dve.wait_ge(s_scores, count.nth("scores", n))
                        link(v.tensor_reduce(nmx[:, n % 2, :], pS[n % 2][:, :, :], AX.X, ALU.max, negate=True))
                        v.tensor_tensor(nb[:, n % 2, :], nmx[:, n % 2, :], rnorm[z][:, m, g:HEADS:2],
                                        ALU.mult).then_inc(s_smax, 1)
                    elif name == "p_norm":
                        dve.wait_ge(s_exp, count.nth("exp", n))
                        link(v.reciprocal(rl[:, n % 2, :], sums[:, n % 2, :]))
                        v.tensor_tensor(probs[:, n % 2, :, :], probs[:, n % 2, :, :],
                                        rl[:, n % 2, :].unsqueeze(2).to_broadcast([P, 4, P]),
                                        ALU.mult).then_inc(s_p_norm, 1)
                    elif name == "wo_add":
                        m = arg
                        dve.wait_ge(s_wo, count.so_far("wo"))
                        v.tensor_tensor(xres[z][:, m, :], xres[z][:, m, :], pO[:, 0:D], ALU.add).then_inc(s_wo_add, 1)
                dve.sem_inc(s_dve_chain, CHAIN - count.links)
                if count.first:
                    dve.drain()
                    dve.sem_inc(s_shift_hi, count.rest("shift_hi"))
                    dve.sem_inc(s_ln_stats, count.rest("ln_stats"))
                    dve.sem_inc(s_ln_apply, count.rest("ln_apply"))
                    dve.sem_inc(s_gate, count.rest("gate"))
                    dve.sem_inc(s_resid, count.rest("resid"))
                    dve.sem_inc(s_rope_k, count.rest("rope_k"))
                    dve.sem_inc(s_rope_s, count.rest("rope_s"))
                    dve.sem_inc(s_qk_sum, count.rest("qk_sum"))
                    dve.sem_inc(s_rope_add, count.rest("rope_add"))
                    dve.sem_inc(s_ct_evac, count.rest("ct_evac"))
                    dve.sem_inc(s_dt_abs, count.rest("dt_abs"))
                    dve.sem_inc(s_decay, count.rest("decay"))
                    dve.sem_inc(s_mt, count.rest("mt"))
                    dve.sem_inc(s_y_skip, count.rest("y_skip"))
                    dve.sem_inc(s_y_off, count.rest("y_off"))
                    dve.sem_inc(s_smax, count.rest("smax"))
                    dve.sem_inc(s_p_norm, count.rest("p_norm"))
                    dve.sem_inc(s_wo_add, count.rest("wo_add"))
                    dve.drain().then_inc(s_section, 1)
                    dve.wait_ge(s_section, 5)
                    dve.sem_inc(s_hold, 1)

            for z in range(2):
                v.memset(kT[z][:, :, 0:WIN], 0.0)
                v.memset(v_even[z][WIN:P, 0, :, :], 0.0)
                v.memset(xres[z][:, :, :], 0.0)
                v.memset(x1[z][:, :, :], 0.0)
            v.memset(hT[D // 2:D, 0:1], 0.0)
            v.memset(ones[:, :], 1.0)
            v.memset(minus_half[:, :], -0.5).then_inc(s_setup, 1)
            dve.wait_ge(s_tables, N_TABLES)
            v.tensor_copy(ident_h[:, :], ident)
            v.tensor_copy(masks_h[:, :, :], cst[:, 3 * P:6 * P].rearrange("p (k j) -> p k j", k=3))
            hf = DH // 2
            v.tensor_scalar(scales[:, :, 0, :], scales[:, :, 0, :], QK_SCALE, None, ALU.mult).then_inc(s_scaled, 1)
            dve.wait_ge(s_scaled, 1)
            for l in range(DEPTH):
                wide = [P, BLK, 2, DH]
                v.tensor_tensor(tab_c[:, l, :, :, :], rope_cos,
                                scales[:, l, :, :].unsqueeze(1).to_broadcast(wide), ALU.mult)
                for a, b in ((0, hf), (hf, 0)):
                    last = v.tensor_tensor(tab_s[:, l, :, :, a:a + hf], rope_sin[:, :, :, a:a + hf],
                                           scales[:, l, :, b:b + hf].unsqueeze(1).to_broadcast([P, BLK, 2, hf]), ALU.mult)
            dve.wait_ge(s_rows, 1)
            v.tensor_scalar(ssd_par[:, 3:4], ssd_par[:, 3:4], -1.0, None, ALU.mult).then_inc(s_setup, 1)
            dve.wait_ge(s_wx, 1)
            v.tensor_copy(wx_bc[:, :], pM[:, 0:P])
            v.tensor_copy(wx_tok[:, 1:1 + STATE], pM[:, 0:STATE]).then_inc(s_wx, 1)
            dve.wait_ge(s_wx, 2)
            section(Count(0, FIRST))
            with dve.Fori(0, PASSES) as i:
                section(Count(i + 1, PASS, ORDER))
            section(Count(PASSES + 1, LAST))

        @block.gpsimd
        def _(pool):
            g = nc.gpsimd

            def section(count):
                def link(ins):
                    ins.then_inc(s_pool_chain, 1)
                    pool.wait_ge(s_pool_chain, count.next_link())

                for name, z, layer, arg, n in count.steps():
                    if name == "ln_rstd":
                        kind = arg
                        pool.wait_ge(s_ln_stats, count.nth("ln_stats", n))
                        pool.sem_inc(s_hold, 1)
                        link(g.tensor_scalar(veps[:, n % 2, :], mv[:, n % 2, :, 1], LN_EPS, None, ALU.add))
                        g.tensor_tensor(rstd[:, n % 2, :], veps[:, n % 2, :], minus_half[:, 0:BLK],
                                        ALU.pow).then_inc(s_ln_rstd, 1)
                    elif name == "resid_bias":
                        pool.wait_ge(s_wo_add, count.nth("wo_add", 4 * REST_PHASE[z, layer]))
                        pool.wait_ge(s_resid, count.so_far("resid"))
                        g.tensor_tensor(xb[:, :, :], xres[z][:, :, :],
                                        b2_s[:, layer, :].unsqueeze(1).to_broadcast([P, BLK, D]),
                                        ALU.add).then_inc(s_resid_bias, 1)
                    elif name == "rope_c":
                        m = arg
                        pool.wait_ge(s_q_copy, count.nth("q_copy", n))
                        pool.wait_ge(s_rope_add, count.nth("rope_add", n - 1))
                        g.tensor_tensor(rc[:, 0:INNER].rearrange("p (h f) -> p h f", h=HEADS),
                                        qk[:, n % 2, 0:INNER].rearrange("p (h f) -> p h f", h=HEADS),
                                        tab_c[:, layer, m, 0, :].unsqueeze(1).to_broadcast([P, HEADS, DH]),
                                        ALU.mult).then_inc(s_rope_c, 1)
                    elif name == "rinv":
                        m = arg
                        pool.wait_ge(s_rinv_q, count.nth("rinv_q", n - 1))
                        pool.wait_ge(s_qk_sum, count.nth("qk_sum", n))
                        pool.sem_inc(s_hold, 1)
                        link(g.tensor_scalar(ssc[:, :], ss[:, :], 1e-24, None, ALU.max))
                        g.tensor_tensor(rnorm[z][:, m, HEADS:2 * HEADS], ssc[:, HEADS:2 * HEADS], minus_half[:, :],
                                        ALU.pow).then_inc(s_rinv, 1)
                    elif name == "rinv_q":
                        m = arg
                        pool.wait_ge(s_rinv, count.nth("rinv", n))
                        g.tensor_tensor(rnorm[z][:, m, 0:HEADS], ssc[:, 0:HEADS], minus_half[:, :],
                                        ALU.pow).then_inc(s_rinv_q, 1)
                    elif name == "k_scale":
                        m = arg
                        pool.wait_ge(s_rope_add, count.nth("rope_add", n))
                        pool.wait_ge(s_rinv, count.nth("rinv", n))
                        k = rot[:, n % 2, INNER:2 * INNER].rearrange("p (h f) -> p h f", h=HEADS)
                        g.tensor_tensor(k, k, rnorm[z][:, arg, HEADS:2 * HEADS].unsqueeze(2).to_broadcast([P, HEADS, DH]),
                                               ALU.mult).then_inc(s_k_scale, 1)
                pool.sem_inc(s_pool_chain, CHAIN - count.links)
                if count.first:
                    pool.drain()
                    pool.sem_inc(s_ln_rstd, count.rest("ln_rstd"))
                    pool.sem_inc(s_resid_bias, count.rest("resid_bias"))
                    pool.sem_inc(s_rope_c, count.rest("rope_c"))
                    pool.sem_inc(s_rinv, count.rest("rinv"))
                    pool.sem_inc(s_rinv_q, count.rest("rinv_q"))
                    pool.sem_inc(s_k_scale, count.rest("k_scale"))
                    pool.drain().then_inc(s_section, 1)
                    pool.wait_ge(s_section, 5)
                    pool.sem_inc(s_hold, 1)

            pool.wait_ge(s_setup, 2)
            section(Count(0, FIRST))
            with pool.Fori(0, PASSES) as i:
                section(Count(i + 1, PASS, ORDER))
            section(Count(PASSES + 1, LAST))


_INS = ['L0_attn_x', 'L0_attn_W_xproj', 'L0_attn_dt_bias', 'L0_attn_A_log', 'L0_attn_D', 'L0_ffn_wqkv',
        'L0_ffn_q_scale', 'L0_ffn_k_scale', 'L0_ffn_wo', 'L0_ffn_ln_g', 'L0_ffn_ln_b', 'L0_ffn_w1', 'L0_ffn_b1',
        'L0_ffn_w2', 'L0_ffn_b2']


def kernel(**inputs):
    import concourse.bacc as _bacc
    from concourse.bass_utils import run_bass_kernel_spmd as _run

    nc = _bacc.Bacc("TRN2", target_bir_lowering=False, num_devices=1)
    arrays, args = {}, []
    for name in _INS:
        a = np.ascontiguousarray(inputs[name])
        arrays[f"in_{name}_dram"] = a
        args.append(nc.dram_tensor(f"in_{name}_dram", a.shape, F32, kind="ExternalInput").ap())
    shape = inputs['L0_attn_x'].shape
    const = shape_constants(shape[1])
    arrays["const_dram"] = const
    args.append(nc.dram_tensor("const_dram", const.shape, F32, kind="ExternalInput").ap())
    args.append(nc.dram_tensor("out_0_dram", shape, F32, kind="ExternalOutput").ap())
    build(nc, *args)
    r = _run(nc, [arrays], core_ids=[0])
    return r.results[0]["out_0_dram"]
```
